# Optimizing a Trainium2 kernel written in Bass

```python
import numpy as np
import jax
import jax.numpy as jnp

def _softmax(x, axis=-1):
    return jax.nn.softmax(x, axis=axis)

def _gelu(x):
    return jax.nn.gelu(x, approximate=True)

def _silu(x):
    return jax.nn.silu(x)

def _sigmoid(x):
    return jax.nn.sigmoid(x)

def _layernorm(x, axis=-1, eps=1e-05):
    m = jnp.mean(x, axis=axis, keepdims=True)
    v = jnp.var(x, axis=axis, keepdims=True)
    return (x - m) / jnp.sqrt(v + eps)

def _scatter_add(tgt, idx, src, axis=0):
    return tgt.at[idx].add(src)

def _segment_sum(src, seg, n):
    return jax.ops.segment_sum(src, seg, n)
kernel_name = 'mk_recurrent_d2_jaxref_r8_b04944'

def setup_inputs(seed: int=0):
    np.random.seed(seed)
    _w = jnp.asarray

    def _L0_attn_setup():
        import jax, jax.numpy as jnp
        import numpy as np
        DIM = 128
        HEADS = 16
        DIM_HEAD = 64
        INNER = HEADS * DIM_HEAD
        EPS = 1e-06

        def elu_feature_map(t):
            return jnp.where(t > 0, t + 1.0, jnp.exp(t))
        key = jax.random.key(seed)
        k1, k2, k3, k4 = jax.random.split(key, 4)
        B, N = (4, 1024)
        x = jax.random.normal(k1, (B, N, DIM), dtype=jnp.float32)
        s_in = 1.0 / np.sqrt(DIM)
        s_out = 1.0 / np.sqrt(INNER)
        Wqkv = jax.random.uniform(k2, (DIM, 3 * INNER), dtype=jnp.float32, minval=-s_in, maxval=s_in)
        Wout = jax.random.uniform(k3, (INNER, DIM), dtype=jnp.float32, minval=-s_out, maxval=s_out)
        bout = jax.random.uniform(k4, (DIM,), dtype=jnp.float32, minval=-s_out, maxval=s_out)
        return {'x': x, 'Wqkv': Wqkv, 'Wout': Wout, 'bout': bout}
    _L0_attn_in = _L0_attn_setup()

    def _L0_ffn_setup():
        import jax, jax.numpy as jnp
        import numpy as np
        HID = 128
        NH = 16
        NKV = 4
        HD = HID // NH
        E = 8
        TOPK = 2
        FFN = 256
        EPS = 1e-05
        THETA = 10000.0

        def _rmsnorm(x, w):
            var = jnp.mean(x * x, axis=-1, keepdims=True)
            return x * jax.lax.rsqrt(var + EPS) * w

        def _rope_tables(S):
            inv_freq = 1.0 / THETA ** (jnp.arange(0, HD, 2, dtype=jnp.float32) / HD)
            freqs = jnp.arange(S, dtype=jnp.float32)[:, None] * inv_freq[None, :]
            emb = jnp.concatenate([freqs, freqs], axis=-1)
            return (jnp.cos(emb), jnp.sin(emb))

        def _apply_rope(t, cos, sin):
            t1, t2 = jnp.split(t, 2, axis=-1)
            rot = jnp.concatenate([-t2, t1], axis=-1)
            return t * cos[None, :, None, :] + rot * sin[None, :, None, :]
        key = jax.random.key(seed)
        ks = jax.random.split(key, 6)
        B, S = (1, 256)
        x = jax.random.normal(ks[0], (B, S, HID), dtype=jnp.float32)
        wqkv = jax.random.normal(ks[1], ((NH + 2 * NKV) * HD, HID), dtype=jnp.float32) * 0.02
        wo = jax.random.normal(ks[2], (HID, NH * HD), dtype=jnp.float32) * 0.02
        gate_w = jax.random.normal(ks[3], (E, HID), dtype=jnp.float32) * 0.02
        w13 = jax.random.normal(ks[4], (E, 2 * FFN, HID), dtype=jnp.float32) * 0.02
        w2 = jax.random.normal(ks[5], (E, HID, FFN), dtype=jnp.float32) * 0.02
        return {'x': x, 'ln1_w': jnp.ones((HID,), jnp.float32), 'ln2_w': jnp.ones((HID,), jnp.float32), 'wqkv': wqkv, 'wo': wo, 'gate_w': gate_w, 'w13': w13, 'w2': w2}
    _L0_ffn_in = _L0_ffn_setup()

    def _L1_attn_setup():
        import jax, jax.numpy as jnp
        import numpy as np
        D_MODEL = 128
        H = 16
        DH = 64
        FFN = 512
        CHUNK = 64
        LN_EPS = 1e-05

        def layer_norm(x, w, b):
            mu = x.mean(-1, keepdims=True)
            var = x.var(-1, keepdims=True)
            return (x - mu) * jax.lax.rsqrt(var + LN_EPS) * w + b

        def l2_normalize(x):
            n = jnp.sqrt(jnp.sum(x * x, axis=-1, keepdims=True))
            return x / jnp.maximum(n, 1e-12)

        def chunk_gla(q, k, v, alpha, C=CHUNK):
            B, Hh, N, D = q.shape
            nc = N // C
            q = q.reshape(B, Hh, nc, C, D)
            k = k.reshape(B, Hh, nc, C, D)
            v = v.reshape(B, Hh, nc, C, D)
            alpha = alpha.reshape(B, Hh, nc, C, D)
            log_a = jnp.log(jnp.maximum(alpha, 1e-06))
            la_cum = jnp.cumsum(log_a, axis=3)
            la_mean = la_cum.mean(-1)
            tril = jnp.tril(jnp.ones((C, C), dtype=q.dtype))
            decay = jnp.exp(la_mean[..., :, None] - la_mean[..., None, :]) * tril
            attn_intra = jnp.einsum('bhncd,bhnmd->bhncm', q, k) * decay
            o_intra = jnp.einsum('bhncm,bhnmd->bhncd', attn_intra, v)
            decay_to_end = jnp.exp(la_cum[:, :, :, -1:, :] - la_cum)
            kv_chunk = jnp.einsum('bhncf,bhnce->bhnfe', k * decay_to_end, v)
            chunk_decay = jnp.exp(log_a.sum(3))
            q_dec = q * jnp.exp(la_cum)

            def step(S, inp):
                qd, kv, cd = inp
                o = jnp.einsum('bhcd,bhde->bhce', qd, S)
                S_new = S * cd[:, :, :, None] + kv
                return (S_new, o)
            S0 = jnp.zeros((B, Hh, D, D), dtype=q.dtype)
            _, o_inter = jax.lax.scan(step, S0, (jnp.moveaxis(q_dec, 2, 0), jnp.moveaxis(kv_chunk, 2, 0), jnp.moveaxis(chunk_decay, 2, 0)))
            o_inter = jnp.moveaxis(o_inter, 0, 2)
            return (o_intra + o_inter).reshape(B, Hh, N, D)
        key = jax.random.key(seed)
        ks = jax.random.split(key, 16)
        s = 0.02
        td = H * DH
        return {'x': jax.random.normal(ks[0], (2, 512, D_MODEL), dtype=jnp.float32), 'Wq': jax.random.normal(ks[1], (D_MODEL, td), dtype=jnp.float32) * s, 'Wk': jax.random.normal(ks[2], (D_MODEL, td), dtype=jnp.float32) * s, 'Wv': jax.random.normal(ks[3], (D_MODEL, td), dtype=jnp.float32) * s, 'Wg': jax.random.normal(ks[4], (D_MODEL, td), dtype=jnp.float32) * s, 'bg': jnp.full((td,), -0.5, dtype=jnp.float32), 'Wo': jax.random.normal(ks[5], (td, D_MODEL), dtype=jnp.float32) * s, 'ln1_w': jnp.ones((D_MODEL,), jnp.float32), 'ln1_b': jnp.zeros((D_MODEL,), jnp.float32), 'ln2_w': jnp.ones((D_MODEL,), jnp.float32), 'ln2_b': jnp.zeros((D_MODEL,), jnp.float32), 'W1': jax.random.normal(ks[6], (D_MODEL, FFN), dtype=jnp.float32) * s, 'b1': jnp.zeros((FFN,), jnp.float32), 'W2': jax.random.normal(ks[7], (FFN, D_MODEL), dtype=jnp.float32) * s, 'b2': jnp.zeros((D_MODEL,), jnp.float32)}
    _L1_attn_in = _L1_attn_setup()

    def _L1_ffn_setup():
        import jax, jax.numpy as jnp
        import numpy as np
        B, T, D, H, E = (4, 256, 128, 512, 8)
        key = jax.random.key(seed)
        ks = jax.random.split(key, 7)
        x = jax.random.normal(ks[0], (B, T, D), dtype=jnp.float32)
        Wg = jax.random.normal(ks[1], (D, E), dtype=jnp.float32) / np.sqrt(D)
        bg = jax.random.normal(ks[2], (E,), dtype=jnp.float32) * 0.01
        W1 = jax.random.normal(ks[3], (E, D, H), dtype=jnp.float32) / np.sqrt(D)
        b1 = jax.random.normal(ks[4], (E, H), dtype=jnp.float32) * 0.01
        W2 = jax.random.normal(ks[5], (E, H, D), dtype=jnp.float32) / np.sqrt(H)
        b2 = jax.random.normal(ks[6], (E, D), dtype=jnp.float32) * 0.01
        return {'x': x, 'Wg': Wg, 'bg': bg, 'W1': W1, 'b1': b1, 'W2': W2, 'b2': b2}
    _L1_ffn_in = _L1_ffn_setup()
    _d = {'L0_attn_x': _L0_attn_in['x'], 'L0_attn_Wqkv': _L0_attn_in['Wqkv'], 'L0_attn_Wout': _L0_attn_in['Wout'], 'L0_attn_bout': _L0_attn_in['bout'], 'L0_ffn_ln1_w': _L0_ffn_in['ln1_w'], 'L0_ffn_ln2_w': _L0_ffn_in['ln2_w'], 'L0_ffn_wqkv': _L0_ffn_in['wqkv'], 'L0_ffn_wo': _L0_ffn_in['wo'], 'L0_ffn_gate_w': _L0_ffn_in['gate_w'], 'L0_ffn_w13': _L0_ffn_in['w13'], 'L0_ffn_w2': _L0_ffn_in['w2'], 'L1_attn_Wq': _L1_attn_in['Wq'], 'L1_attn_Wk': _L1_attn_in['Wk'], 'L1_attn_Wv': _L1_attn_in['Wv'], 'L1_attn_Wg': _L1_attn_in['Wg'], 'L1_attn_bg': _L1_attn_in['bg'], 'L1_attn_Wo': _L1_attn_in['Wo'], 'L1_attn_ln1_w': _L1_attn_in['ln1_w'], 'L1_attn_ln1_b': _L1_attn_in['ln1_b'], 'L1_attn_ln2_w': _L1_attn_in['ln2_w'], 'L1_attn_ln2_b': _L1_attn_in['ln2_b'], 'L1_attn_W1': _L1_attn_in['W1'], 'L1_attn_b1': _L1_attn_in['b1'], 'L1_attn_W2': _L1_attn_in['W2'], 'L1_attn_b2': _L1_attn_in['b2'], 'L1_ffn_Wg': _L1_ffn_in['Wg'], 'L1_ffn_bg': _L1_ffn_in['bg'], 'L1_ffn_W1': _L1_ffn_in['W1'], 'L1_ffn_b1': _L1_ffn_in['b1'], 'L1_ffn_W2': _L1_ffn_in['W2'], 'L1_ffn_b2': _L1_ffn_in['b2']}
    _x0 = _d['L0_attn_x']
    _d['L0_attn_x'] = jax.random.normal(jax.random.fold_in(jax.random.key(seed), 1), (16, 256, 128), dtype=_x0.dtype)
    del _x0
    return _d

def reference(L0_attn_x, L0_attn_Wqkv, L0_attn_Wout, L0_attn_bout, L0_ffn_ln1_w, L0_ffn_ln2_w, L0_ffn_wqkv, L0_ffn_wo, L0_ffn_gate_w, L0_ffn_w13, L0_ffn_w2, L1_attn_Wq, L1_attn_Wk, L1_attn_Wv, L1_attn_Wg, L1_attn_bg, L1_attn_Wo, L1_attn_ln1_w, L1_attn_ln1_b, L1_attn_ln2_w, L1_attn_ln2_b, L1_attn_W1, L1_attn_b1, L1_attn_W2, L1_attn_b2, L1_ffn_Wg, L1_ffn_bg, L1_ffn_W1, L1_ffn_b1, L1_ffn_W2, L1_ffn_b2):

    def _L0_attn_ref(x, Wqkv, Wout, bout):
        import jax, jax.numpy as jnp
        import numpy as np
        DIM = 128
        HEADS = 16
        DIM_HEAD = 64
        INNER = HEADS * DIM_HEAD
        EPS = 1e-06

        def elu_feature_map(t):
            return jnp.where(t > 0, t + 1.0, jnp.exp(t))
        B, N, D = x.shape
        qkv = x @ Wqkv
        q, k, v = jnp.split(qkv, 3, axis=-1)
        resh = lambda t: t.reshape(B, N, HEADS, DIM_HEAD).transpose(0, 2, 1, 3)
        q, k, v = (resh(q), resh(k), resh(v))
        q = elu_feature_map(q)
        k = elu_feature_map(k)
        kv = jnp.einsum('bhnd,bhnf->bhdf', k, v)
        k_sum = k.sum(axis=-2)
        qkv_out = jnp.einsum('bhnd,bhdf->bhnf', q, kv)
        q_k_sum = jnp.einsum('bhnd,bhd->bhn', q, k_sum)
        out = qkv_out / (q_k_sum[..., None] + EPS)
        out = out.transpose(0, 2, 1, 3).reshape(B, N, INNER)
        return out @ Wout + bout

    def _L0_ffn_ref(x, ln1_w, ln2_w, wqkv, wo, gate_w, w13, w2):
        import jax, jax.numpy as jnp
        import numpy as np
        HID = 128
        NH = 16
        NKV = 4
        HD = HID // NH
        E = 8
        TOPK = 2
        FFN = 256
        EPS = 1e-05
        THETA = 10000.0

        def _rmsnorm(x, w):
            var = jnp.mean(x * x, axis=-1, keepdims=True)
            return x * jax.lax.rsqrt(var + EPS) * w

        def _rope_tables(S):
            inv_freq = 1.0 / THETA ** (jnp.arange(0, HD, 2, dtype=jnp.float32) / HD)
            freqs = jnp.arange(S, dtype=jnp.float32)[:, None] * inv_freq[None, :]
            emb = jnp.concatenate([freqs, freqs], axis=-1)
            return (jnp.cos(emb), jnp.sin(emb))

        def _apply_rope(t, cos, sin):
            t1, t2 = jnp.split(t, 2, axis=-1)
            rot = jnp.concatenate([-t2, t1], axis=-1)
            return t * cos[None, :, None, :] + rot * sin[None, :, None, :]
        B, S, _ = x.shape
        h = _rmsnorm(x, ln1_w)
        qkv = jnp.einsum('bsh,oh->bso', h, wqkv)
        q = qkv[..., :NH * HD].reshape(B, S, NH, HD)
        k = qkv[..., NH * HD:(NH + NKV) * HD].reshape(B, S, NKV, HD)
        v = qkv[..., (NH + NKV) * HD:].reshape(B, S, NKV, HD)
        cos, sin = _rope_tables(S)
        q = _apply_rope(q, cos, sin)
        k = _apply_rope(k, cos, sin)
        groups = NH // NKV
        k = jnp.repeat(k, groups, axis=2)
        v = jnp.repeat(v, groups, axis=2)
        scale = HD ** (-0.5)
        scores = jnp.einsum('bqhd,bkhd->bhqk', q, k) * scale
        causal = jnp.tril(jnp.ones((S, S), dtype=bool))
        scores = jnp.where(causal[None, None], scores, jnp.finfo(scores.dtype).min)
        probs = jax.nn.softmax(scores, axis=-1)
        attn = jnp.einsum('bhqk,bkhd->bqhd', probs, v).reshape(B, S, NH * HD)
        x = x + jnp.einsum('bso,ho->bsh', attn, wo)
        h = _rmsnorm(x, ln2_w).reshape(-1, HID)
        T = h.shape[0]
        logits = jnp.einsum('th,eh->te', h, gate_w)
        rprobs = jax.nn.softmax(logits.astype(jnp.float32), axis=-1)
        topw, topi = jax.lax.top_k(rprobs, TOPK)
        topw = topw / jnp.sum(topw, axis=-1, keepdims=True)
        wfull = jnp.zeros((T, E), jnp.float32).at[jnp.arange(T)[:, None], topi].set(topw)
        wfull = wfull.astype(h.dtype)
        out = jnp.zeros((T, HID), h.dtype)
        for e in range(E):
            w1 = w13[e, :FFN]
            w3 = w13[e, FFN:]
            g = jax.nn.silu(h @ w1.T) * (h @ w3.T)
            out = out + jnp.einsum('tf,hf->th', g, w2[e]) * wfull[:, e:e + 1]
        return x + out.reshape(B, S, HID)

    def _L1_attn_ref(x, Wq, Wk, Wv, Wg, bg, Wo, ln1_w, ln1_b, ln2_w, ln2_b, W1, b1, W2, b2):
        import jax, jax.numpy as jnp
        import numpy as np
        D_MODEL = 128
        H = 16
        DH = 64
        FFN = 512
        CHUNK = 64
        LN_EPS = 1e-05

        def layer_norm(x, w, b):
            mu = x.mean(-1, keepdims=True)
            var = x.var(-1, keepdims=True)
            return (x - mu) * jax.lax.rsqrt(var + LN_EPS) * w + b

        def l2_normalize(x):
            n = jnp.sqrt(jnp.sum(x * x, axis=-1, keepdims=True))
            return x / jnp.maximum(n, 1e-12)

        def chunk_gla(q, k, v, alpha, C=CHUNK):
            B, Hh, N, D = q.shape
            nc = N // C
            q = q.reshape(B, Hh, nc, C, D)
            k = k.reshape(B, Hh, nc, C, D)
            v = v.reshape(B, Hh, nc, C, D)
            alpha = alpha.reshape(B, Hh, nc, C, D)
            log_a = jnp.log(jnp.maximum(alpha, 1e-06))
            la_cum = jnp.cumsum(log_a, axis=3)
            la_mean = la_cum.mean(-1)
            tril = jnp.tril(jnp.ones((C, C), dtype=q.dtype))
            decay = jnp.exp(la_mean[..., :, None] - la_mean[..., None, :]) * tril
            attn_intra = jnp.einsum('bhncd,bhnmd->bhncm', q, k) * decay
            o_intra = jnp.einsum('bhncm,bhnmd->bhncd', attn_intra, v)
            decay_to_end = jnp.exp(la_cum[:, :, :, -1:, :] - la_cum)
            kv_chunk = jnp.einsum('bhncf,bhnce->bhnfe', k * decay_to_end, v)
            chunk_decay = jnp.exp(log_a.sum(3))
            q_dec = q * jnp.exp(la_cum)

            def step(S, inp):
                qd, kv, cd = inp
                o = jnp.einsum('bhcd,bhde->bhce', qd, S)
                S_new = S * cd[:, :, :, None] + kv
                return (S_new, o)
            S0 = jnp.zeros((B, Hh, D, D), dtype=q.dtype)
            _, o_inter = jax.lax.scan(step, S0, (jnp.moveaxis(q_dec, 2, 0), jnp.moveaxis(kv_chunk, 2, 0), jnp.moveaxis(chunk_decay, 2, 0)))
            o_inter = jnp.moveaxis(o_inter, 0, 2)
            return (o_intra + o_inter).reshape(B, Hh, N, D)
        B, N, _ = x.shape
        xn = layer_norm(x, ln1_w, ln1_b)
        q = (xn @ Wq).reshape(B, N, H, DH).transpose(0, 2, 1, 3)
        k = (xn @ Wk).reshape(B, N, H, DH).transpose(0, 2, 1, 3)
        v = (xn @ Wv).reshape(B, N, H, DH).transpose(0, 2, 1, 3)
        q = l2_normalize(q)
        k = l2_normalize(k)
        alpha = jax.nn.sigmoid(xn @ Wg + bg).reshape(B, N, H, DH).transpose(0, 2, 1, 3)
        o = chunk_gla(q, k, v, alpha)
        o = o.transpose(0, 2, 1, 3).reshape(B, N, H * DH)
        x = x + o @ Wo
        h = layer_norm(x, ln2_w, ln2_b)
        x = x + jax.nn.gelu(h @ W1 + b1, approximate=False) @ W2 + b2
        return x

    def _L1_ffn_ref(x, Wg, bg, W1, b1, W2, b2):
        import jax, jax.numpy as jnp
        import numpy as np
        B, T, D, H, E = (4, 256, 128, 512, 8)
        gate_scores = x @ Wg + bg
        top1 = jnp.argmax(gate_scores, axis=-1)
        onehot = jax.nn.one_hot(top1, Wg.shape[-1], dtype=x.dtype)
        h = jax.nn.relu(jnp.einsum('btd,edh->beth', x, W1) + b1[None, :, None, :])
        y = jnp.einsum('beth,ehd->betd', h, W2) + b2[None, :, None, :]
        out = jnp.einsum('betd,bte->btd', y, onehot)
        return out
    x = L0_attn_x
    xn = _layernorm(x, axis=-1)
    s = _L0_attn_ref(xn, L0_attn_Wqkv, L0_attn_Wout, L0_attn_bout)
    g = _silu(_L0_ffn_ref(xn, L0_ffn_ln1_w, L0_ffn_ln2_w, L0_ffn_wqkv, L0_ffn_wo, L0_ffn_gate_w, L0_ffn_w13, L0_ffn_w2))
    x = x + s * g
    xn = _layernorm(x, axis=-1)
    s = _L1_attn_ref(xn, L1_attn_Wq, L1_attn_Wk, L1_attn_Wv, L1_attn_Wg, L1_attn_bg, L1_attn_Wo, L1_attn_ln1_w, L1_attn_ln1_b, L1_attn_ln2_w, L1_attn_ln2_b, L1_attn_W1, L1_attn_b1, L1_attn_W2, L1_attn_b2)
    g = _silu(_L1_ffn_ref(xn, L1_ffn_Wg, L1_ffn_bg, L1_ffn_W1, L1_ffn_b1, L1_ffn_W2, L1_ffn_b2))
    x = x + s * g
    return x

_drawn_inputs = setup_inputs


def setup_inputs(seed=0):
    import zlib

    import numpy as np

    out = dict(_drawn_inputs(seed))
    spreads = {'L0_ffn_ln1_w': (1.0, 0.2),
     'L0_ffn_ln2_w': (1.0, 0.2),
     'L1_attn_bg': (-0.5, 0.2),
     'L1_attn_ln1_w': (1.0, 0.2),
     'L1_attn_ln1_b': (0.0, 0.1),
     'L1_attn_ln2_w': (1.0, 0.2),
     'L1_attn_ln2_b': (0.0, 0.1),
     'L1_attn_b1': (0.0, 0.1),
     'L1_attn_b2': (0.0, 0.1)}
    factors = {}
    for name, (base, spread) in spreads.items():
        noise = np.random.default_rng([zlib.crc32(name.encode()), seed]).standard_normal(out[name].shape)
        drawn = base * np.exp(spread * noise) if base else spread * noise
        out[name] = jnp.asarray(drawn.astype(out[name].dtype))
    for name, factor in factors.items():
        out[name] = (out[name] * factor).astype(out[name].dtype)
    return out
```

```python
from contextlib import ExitStack

import concourse.bass as bass
import numpy as np
from concourse import mybir

B, N, D = 16, 256, 128
P = 128
NT = N // P
H, DH = 16, 64
NP = H // 2
INNER = H * DH
NHF, NKV, HD = 16, 4, 8
GR = NHF // NKV
E = 8
F0 = 256
F1 = 512
CH = 64
NC = N // CH
V1 = HD + 1
V0 = DH + 1
NEG = -3.0e38

RING = 7


def psum_plan():
    names = ["xT"]
    names += [f"q{j}" for j in range(4)]
    names += [f"k{t}{c}" for t in range(2) for c in range(2)]
    names += [f"v{t}{c}" for t in range(2) for c in range(2)]
    names += [f"rq{j}" for j in range(2)] + [f"rs{j}" for j in range(2)] + ["rk", "v9"]
    names += [f"kv{j}" for j in range(4)]
    names += [f"num{t}{j}" for t in range(2) for j in range(4)]
    names += [f"oT{t}{c}" for t in range(2) for c in range(2)]
    names += ["s0"]
    names += [f"sc{n}" for n in range(12)]
    names += [f"pT{n}" for n in range(12)]
    names += ["pv", "aT", "wo", "hT", "gate"]
    for e in range(E + 1):
        if e < E:
            names += [f"a{e}", f"b{e}"]
        if e:
            names += [f"y{e - 1}"]
    names += ["zT"]
    names += [f"lq{j}" for j in range(4)] + ["ssq"] + [f"lk{j}" for j in range(4)]
    names += [f"tk{t}{c}" for t in range(2) for c in range(2)]
    names += [f"z{t}{c}" for t in range(2) for c in range(2)]
    names += ["rqT"] + [f"rep{j}" for j in range(4)]
    names += [f"tv{t}{c}" for t in range(2) for c in range(2)]
    names += [f"d{t}{c}" for t in range(2) for c in range(2)]
    names += [f"s{t}{c}" for t in range(2) for c in range(2)]
    names += [f"te{t}{c}" for t in range(2) for c in range(2)]
    names += [f"la{j}" for j in range(4)]
    names += [f"st{n}{hh}" for n in range(NC - 1) for hh in range(2)]
    names += [f"o{j}" for j in range(4)]
    names += ["wo1", "gate1", "z2T", "ohT", "f0", "f1", "w2", "b2y"]
    for e in range(E + 1):
        if e < E:
            names += [f"h{e}0", f"h{e}1"]
        if e:
            names += [f"yy{e - 1}"]
    plan, uses = {}, [0] * RING
    for i, name in enumerate(names):
        bank = i % RING
        uses[bank] += 1
        plan[name] = (bank, uses[bank])
    return plan, uses


PLAN, USES = psum_plan()

PER = {'act_chain': 10, 'eq': 4, 'ek': 4, 'p_ready': 12, 'sq_done': 4, 'ks': 4, 'a_ready': 2, 'dec_half': 4, 'gelu_half': 2,
       'dve_chain': 100, 'q0_part': 3, 'k0_part': 3, 'ez_clamped': 2, 'at3_ready': 2, 'kd_part': 3, 'ew0_free': 4, 'ew1_free': 4}


def build(nc, A, out, debug=None):
    dt = mybir.dt
    f32, b16 = dt.float32, dt.bfloat16
    ALU, ACT, AX = mybir.AluOpType, mybir.ActivationFunctionType, mybir.AxisListType
    ctx = ExitStack()
    with ctx:
        def sb(name, shape, d=f32):
            return ctx.enter_context(nc.sbuf_tensor(name, shape, d))

        wqkv0 = sb("wqkv0", [P, 3 * INNER])
        wout0 = sb("wout0", [P, NP, D])
        boutb = sb("boutb", [P, D])
        wrope = sb("wrope", [P, 10, P])
        wv9 = sb("wv9", [P, NKV * HD])
        woT = sb("woT", [P, D])
        gateT = sb("gateT", [P, E])
        w13T = sb("w13T", [P, E, 2 * F0])
        w2T = sb("w2T", [P, E, 2, D])
        lqkvg = sb("lqkvg", [P, 4 * INNER])
        bg3 = sb("bg3", [3, INNER], b16)
        lwo = sb("lwo", [P, NP, D])
        lw1 = sb("lw1", [P, F1])
        lw2 = sb("lw2", [P, 4, D])
        mg = sb("mg", [P, E])
        mb2 = sb("mb2", [E, D])
        cols = sb("cols", [P, 43])
        bgb = sb("bgb", [P, E])
        b2b = sb("b2b", [P, D])
        ropec = sb("ropec", [P, 2, N])
        tri = sb("tri", [P, P])
        strict = sb("strict", [P, P])
        tri64 = sb("tri64", [P, CH])
        ident = sb("ident", [P, P])
        identb = sb("identb", [P, P], b16)
        cmask = sb("cmask", [P, 2, 2 * N], b16)
        dmask = sb("dmask", [P, 8, CH], b16)
        ones3 = sb("ones3", [3, P], b16)
        pairsel = sb("pairsel", [P, NP, H])
        headsel = sb("headsel", [H, NP, P])
        iota8 = sb("iota8", [P, E])
        ew = sb("ew", [P, 2, 2 * F1 * 1])
        x = sb("x", [P, NT, D])
        xn = sb("xn", [P, NT, D])
        xr = sb("xr", [P, NT, D])
        xT = sb("xT_s", [P, 2, N])
        x2 = sb("x2", [P, NT, D])
        hT = sb("hT_s", [P, N])
        acc = sb("acc", [P, NT, D])
        s0 = sb("s0_s", [P, NT, D])
        sg = sb("sg", [P, NT, D])
        x1 = sb("x1", [P, NT, D])
        ov = sb("ov", [P, NT, D])
        sq = sb("sq", [P, NT, D])
        small = sb("small", [P, 512])
        idx8 = sb("idx8", [P, NT, 8], dt.uint32)
        qt = sb("qt", [P, NP, N])
        big = sb("big", [P, 2 * INNER + NT * H * V0 + 2 * INNER])
        reg = sb("reg", [P, 12 * 512])
        kvb = sb("kvb", [P, NP, 2 * V0])
        pbd = sb("pbd", [P, NT, 2, NP, P])
        st = sb("st", [P, NC - 1, NP, P])
        cd = sb("cd", [P, NP, NC])
        rqT = sb("rqT_s", [H, N])
        ohT = sb("ohT_s", [E, N])
        aT = sb("aT_s", [P, N])
        v9 = sb("v9_s", [P, NT, NKV, V1])
        kr = sb("kr", [P, N])
        ao = sb("ao", [P, NT, D])

        k_tok = big[:, 0:2 * INNER].rearrange("p (t f) -> p t f", t=NT)
        v_tok = big[:, 2 * INNER:2 * INNER + NT * H * V0].rearrange("p (t h v) -> p t h v", t=NT, v=V0)
        o_tok = big[:, 2 * INNER + NT * H * V0:].rearrange("p (t f) -> p t f", t=NT)
        oT = big[:, 0:2 * INNER].rearrange("p (a n) -> p a n", a=NP)
        a_tok = o_tok
        pT = big[:, 0:12 * 512].rearrange("p (n k) -> p n k", n=12)
        e_q = reg[:, 0:2048].rearrange("p (a n) -> p a n", a=NP)
        e_k = reg[:, 2048:4096].rearrange("p (t f) -> p t f", t=NT)
        qr = qt[:, 0:4, :]
        qs = qt[:, 4:8, :]
        krs = sq[:, :, :].rearrange("p t d -> p (t d)")
        rp = reg[:, 4096:6144].rearrange("p (a n) -> p a n", a=8)
        pp = reg[:, :].rearrange("p (n k) -> p n k", n=12)
        g0 = reg[:, 0:1024].rearrange("p (s c n) -> p s c n", s=2, c=2)
        kd = reg[:, 0:2048].rearrange("p (t f) -> p t f", t=NT)
        at3 = reg[:, 0:2048].rearrange("p (t h c) -> p t h c", t=NT, h=H)
        el = reg[:, 2048:4096].rearrange("p (a n) -> p a n", a=NP)
        sqT = el
        ks = kd
        kT = reg[:, 4096:6144].rearrange("p (a n) -> p a n", a=NP)
        oT1 = kT
        g1 = reg[:, 0:1024].rearrange("p (c n) -> p c n", c=4)
        r1 = reg[:, 1024:3072].rearrange("p (s c n) -> p s c n", s=2, c=4)
        bg_row = small[0:3, 0:3]

        psum = ctx.enter_context(nc.psum_tensor("psum", [P, 8, 512], f32))

        sems, count = {}, {}

        def sem(name):
            if name not in sems:
                sems[name] = ctx.enter_context(nc.semaphore(name))
            return sems[name]

        for b in range(RING):
            sem(f"bank{b}_full"), sem(f"bank{b}_free")

        def bank(use):
            return psum[:, PLAN[use][0], :]

        it = {}

        def given(eng, name, n=1, by=1):
            return sem(name), it[eng.engine] * (PER.get(name, 1) * by) + n * by

        def signals(name):
            count[name] = count.get(name, 0) + 1
            return sem(name), 1

        def chained(eng, name):
            return given(eng, name, count[name])

        def emptied(pe, use):
            b, n = PLAN[use]
            return sem(f"bank{b}_free"), it[pe.engine] * USES[b] + n

        def fills(use):
            return sem(f"bank{PLAN[use][0]}_full"), 1

        def filled(eng, use):
            b, n = PLAN[use]
            return sem(f"bank{b}_full"), it[eng.engine] * USES[b] + n

        def frees(use):
            return sem(f"bank{PLAN[use][0]}_free"), 1

        def read_out(eng, use):
            b, n = PLAN[use]
            return sem(f"bank{b}_free"), it[eng.engine] * USES[b] + n + 1

        def kd_b16(i):
            return reg[0:1, i * 512:(i + 1) * 512].bitcast(b16)

        blk = ctx.enter_context(nc.Block())
        NLOAD = [0]

        @blk.sync
        def _(sp):
            def load(dst, src):
                NLOAD[0] += 1
                sp.dma_start(dst, src).then_inc(sem("weights"), 16)

            load(wqkv0[:, :], A["wqkv0"])
            load(wrope[:, :, :], A["wrope"])
            load(ropec[:, :, :], A["ropec"])
            load(wv9[:, :], A["wv9"])
            load(wout0[:, :, :], A["wout0"])
            load(boutb[:, :], A["bout"].partition_broadcast(P))
            load(woT[:, :], A["woT"])
            load(gateT[:, :], A["gateT"])
            load(w13T[:, :, :], A["w13T"])
            load(w2T[:, :, :, :], A["w2T"])
            load(lqkvg[:, :], A["lqkvg"])
            load(lwo[:, :, :], A["lwo"])
            load(lw1[:, :], A["lw1"])
            load(lw2[:, :, :], A["lw2"])
            load(mg[:, :], A["mg"])
            load(mb2[:, :], A["mb2"])
            load(cols[:, :], A["cols"])
            load(bgb[:, :], A["bgm"].partition_broadcast(P))
            load(b2b[:, :], A["b2"].partition_broadcast(P))
            load(identb[:, :], A["identb"])
            load(cmask[:, :, :], A["cmask"])
            load(dmask[:, :, :], A["dmask"])
            load(ones3[:, :], A["ones3"])
            load(tri[:, :], A["tri"])
            load(strict[:, :], A["strict"])
            load(tri64[:, :], A["tri64"])
            load(ident[:, :], A["ident"])
            load(pairsel[:, :, :], A["pairsel"])
            load(headsel[:, :, :], A["headsel"])
            load(iota8[:, :], A["iota8"])
            load(big[0:1, 0:INNER], A["bg"])
            sp.wait_ge(sem("bg_split"), 1)
            for i in range(3):
                sp.dma_start(bg3[i:i + 1, :], kd_b16(i)).then_inc(sem("bg3_ready"), 16)
            sp.sem_inc(sem("stored"), 16)
            with sp.Fori(0, B) as i:
                it[sp.engine] = i
                sp.wait_ge(sem("x_free"), i + 1)
                sp.dma_start(x[:, :, :], A["x"][i].rearrange("(t p) d -> p t d", p=P)).then_inc(sem("x_ready"), 16)
                for e in range(E):
                    sp.wait_ge(sem(f"ew{e % 2}_free"), i * (E // 2) + e // 2 + 1)
                    sp.dma_start(ew[:, e % 2, :], A["ew"][e]).then_inc(sem(f"ew{e % 2}_ready"), 16)
                sp.wait_ge(*given(sp, "out_ready"))
                sp.dma_start(out[i].rearrange("(t p) d -> p t d", p=P), ov[:, :, :]).then_inc(sem("stored"), 16)
            sp.wait_ge(sem("stored"), 16 * (B + 1))

        @blk.gpsimd
        def _(g):
            g.memset(kvb[:, :, :], 0.0).then_inc(sem("zeros"), 1)
            g.memset(st[:, :, :, :], 0.0).then_inc(sem("zeros"), 1)
            g.memset(pbd[:, :, :, :, :], 0.0).then_inc(sem("zeros"), 1)
            g.memset(v9[:, :, :, :], 1.0).then_inc(sem("zeros"), 1)

        @blk.tensor
        def _(pe):
            mm = nc.tensor.matmul

            def tr(dst, src, idn=None):
                k = src.shape[0]
                return nc.tensor.transpose(dst, src, ident[0:k, 0:k])

            for b in range(RING):
                pe.sem_inc(sem(f"bank{b}_free"), 1)
            pe.wait_ge(sem("weights"), 16 * NLOAD[0])
            pe.wait_ge(sem("bg3_ready"), 48)
            pe.wait_ge(sem("zeros"), 4)
            with pe.Fori(0, B) as i:
                it[pe.engine] = i
                pe.wait_ge(*given(pe, "xr_ready"))
                pe.wait_ge(*emptied(pe, "xT"))
                for t in range(NT):
                    tr(bank("xT")[:, t * P:(t + 1) * P], xn[:, t, :])
                for t in range(NT):
                    last = tr(bank("xT")[:, N + t * P:N + (t + 1) * P], xr[:, t, :])
                last.then_inc(*fills("xT"))
                pe.wait_ge(*read_out(pe, "xT"))
                xnT, h1T = xT[:, 0, :], xT[:, 1, :]
                for j in range(4):
                    pe.wait_ge(*emptied(pe, f"q{j}"))
                    for a in range(2):
                        pr = 2 * j + a
                        last = mm(bank(f"q{j}")[:, a * N:(a + 1) * N], wqkv0[:, pr * P:(pr + 1) * P], xnT, start=True, stop=True)
                    last.then_inc(*fills(f"q{j}"))
                for name, off in (("k", INNER), ("v", 2 * INNER)):
                    for t in range(NT):
                        for c in range(2):
                            pe.wait_ge(*emptied(pe, f"{name}{t}{c}"))
                            mm(bank(f"{name}{t}{c}"), xnT[:, t * P:(t + 1) * P],
                                    wqkv0[:, off + c * 512:off + (c + 1) * 512], start=True, stop=True).then_inc(*fills(f"{name}{t}{c}"))
                pe.wait_ge(*read_out(pe, "xT"))
                for name, w0 in (("rq", 0), ("rs", 4)):
                    for j in range(2):
                        pe.wait_ge(*emptied(pe, f"{name}{j}"))
                        for a in range(2):
                            last = mm(bank(f"{name}{j}")[:, a * N:(a + 1) * N], wrope[:, w0 + 2 * j + a, :], h1T, start=True, stop=True)
                        last.then_inc(*fills(f"{name}{j}"))
                pe.wait_ge(*emptied(pe, "rk"))
                for a in range(2):
                    last = mm(bank("rk")[:, a * N:(a + 1) * N], wrope[:, 8 + a, :], h1T, start=True, stop=True)
                last.then_inc(*fills("rk"))
                pe.wait_ge(*emptied(pe, "v9"))
                for t in range(NT):
                    last = mm(bank("v9")[:, t * 32:(t + 1) * 32], h1T[:, t * P:(t + 1) * P], wv9[:, :], start=True, stop=True)
                last.then_inc(*fills("v9"))
                pe.wait_ge(*given(pe, "k0_ready"))
                pe.wait_ge(*read_out(pe, "v11"))
                for j in range(4):
                    pe.wait_ge(*emptied(pe, f"kv{j}"))
                    for a in range(2):
                        pr = 2 * j + a
                        for t in range(NT):
                            last = mm(bank(f"kv{j}")[:, a * N:a * N + 2 * V0], k_tok[:, t, pr * P:(pr + 1) * P],
                                      v_tok[:, t, 2 * pr:2 * pr + 2, :], start=(t == 0), stop=(t == NT - 1))
                    last.then_inc(*fills(f"kv{j}"))
                pe.wait_ge(*given(pe, "q0_ready"))
                for t in range(NT):
                    for j in range(4):
                        if t == 0:
                            pe.wait_ge(*read_out(pe, f"kv{j}"))
                        pe.wait_ge(*emptied(pe, f"num{t}{j}"))
                        for a in range(2):
                            pr = 2 * j + a
                            last = mm(bank(f"num{t}{j}")[:, a * N:a * N + 2 * V0], qt[:, pr, t * P:(t + 1) * P], kvb[:, pr, :], start=True, stop=True)
                        last.then_inc(*fills(f"num{t}{j}"))
                for t in range(NT):
                    pe.wait_ge(*read_out(pe, f"num{t}3"))
                    for c in range(2):
                        pe.wait_ge(*emptied(pe, f"oT{t}{c}"))
                        for a in range(4):
                            last = tr(bank(f"oT{t}{c}")[:, a * P:(a + 1) * P], o_tok[:, t, (4 * c + a) * P:(4 * c + a + 1) * P])
                        last.then_inc(*fills(f"oT{t}{c}"))
                pe.wait_ge(*emptied(pe, "s0"))
                pe.wait_ge(*read_out(pe, "oT11"))
                for t in range(NT):
                    for pr in range(NP):
                        last = mm(bank("s0")[:, t * P:(t + 1) * P], oT[:, pr, t * P:(t + 1) * P], wout0[:, pr, :], start=(pr == 0), stop=(pr == NP - 1))
                last.then_inc(*fills("s0"))
                pe.wait_ge(*given(pe, "rope_ready"))
                for n in range(12):
                    use = f"sc{n}"
                    pe.wait_ge(*emptied(pe, use))
                    if n < 4:
                        mm(bank(use), identb[:, :], cmask[:, 0, :], start=True, stop=False)
                        for r in range(GR):
                            p0 = 32 * n
                            last = mm(bank(use)[:, r * P:(r + 1) * P], qr[p0:p0 + HD, r, 0:P], kr[p0:p0 + HD, 0:P], start=False, stop=(r == GR - 1))
                    else:
                        grp, half = (n - 4) // 2, (n - 4) % 2
                        p0 = 32 * grp
                        mm(bank(use), identb[:, :], cmask[:, 1, :], start=True, stop=False)
                        for a in range(2):
                            last = mm(bank(use)[:, a * N:(a + 1) * N], qr[p0:p0 + HD, 2 * half + a, P:N], kr[p0:p0 + HD, :], start=False, stop=(a == 1))
                    last.then_inc(*fills(use))
                for n in range(12):
                    pe.wait_ge(*given(pe, "p_ready", n + 1))
                    pe.wait_ge(*emptied(pe, f"pT{n}"))
                    for a in range(4):
                        last = tr(bank(f"pT{n}")[:, a * P:(a + 1) * P], pp[:, n, a * P:(a + 1) * P])
                    last.then_inc(*fills(f"pT{n}"))
                pe.wait_ge(*emptied(pe, "pv"))
                pe.wait_ge(*read_out(pe, "pT10"))
                pe.wait_ge(*read_out(pe, "pT11"))
                for hd in range(NHF):
                    grp, r = hd // GR, hd % GR
                    last = mm(bank("pv")[:, hd * V1:(hd + 1) * V1], pT[:, grp, r * P:(r + 1) * P], v9[:, 0, grp, :], start=True, stop=True)
                for hd in range(NHF):
                    grp, r = hd // GR, hd % GR
                    n, a = 4 + 2 * grp + r // 2, r % 2
                    for kt in range(2):
                        last = mm(bank("pv")[:, (NHF + hd) * V1:(NHF + hd + 1) * V1], pT[:, n, (2 * a + kt) * P:(2 * a + kt + 1) * P],
                                  v9[:, kt, grp, :], start=(kt == 0), stop=(kt == 1))
                last.then_inc(*fills("pv"))
                pe.wait_ge(*read_out(pe, "pv"))
                pe.wait_ge(*emptied(pe, "aT"))
                for t in range(NT):
                    last = tr(bank("aT")[:, t * P:(t + 1) * P], ao[:, t, :])
                last.then_inc(*fills("aT"))
                pe.wait_ge(*read_out(pe, "aT"))
                pe.wait_ge(*emptied(pe, "wo"))
                for t in range(NT):
                    last = mm(bank("wo")[:, t * P:(t + 1) * P], aT[:, t * P:(t + 1) * P], woT[:, :], start=True, stop=True)
                last.then_inc(*fills("wo"))
                pe.wait_ge(*given(pe, "h2_ready"))
                pe.wait_ge(*emptied(pe, "hT"))
                for t in range(NT):
                    last = tr(bank("hT")[:, t * P:(t + 1) * P], sq[:, t, :])
                last.then_inc(*fills("hT"))
                pe.wait_ge(*read_out(pe, "hT"))
                pe.wait_ge(*emptied(pe, "gate"))
                for t in range(NT):
                    last = mm(bank("gate")[:, t * E:(t + 1) * E], hT[:, t * P:(t + 1) * P], gateT[:, :], start=True, stop=True)
                last.then_inc(*fills("gate"))
                for e in range(E + 1):
                    if e < E:
                        for name, off in (("a", 0), ("b", F0)):
                            pe.wait_ge(*emptied(pe, f"{name}{e}"))
                            for c in range(2):
                                last = mm(bank(f"{name}{e}")[:, c * N:(c + 1) * N], w13T[:, e, off + c * P:off + (c + 1) * P], hT[:, :], start=True, stop=True)
                            last.then_inc(*fills(f"{name}{e}"))
                    if e:
                        pe.wait_ge(*read_out(pe, f"b{e - 1}"))
                        pe.wait_ge(*emptied(pe, f"y{e - 1}"))
                        for t in range(NT):
                            for c in range(2):
                                last = mm(bank(f"y{e - 1}")[:, t * P:(t + 1) * P], g0[:, (e - 1) % 2, c, t * P:(t + 1) * P], w2T[:, e - 1, c, :], start=(c == 0), stop=(c == 1))
                        last.then_inc(*fills(f"y{e - 1}"))
                pe.wait_ge(*given(pe, "z1_ready"))
                pe.wait_ge(*emptied(pe, "zT"))
                for t in range(NT):
                    tr(bank("zT")[:, t * P:(t + 1) * P], xn[:, t, :])
                for t in range(NT):
                    last = tr(bank("zT")[:, N + t * P:N + (t + 1) * P], xr[:, t, :])
                last.then_inc(*fills("zT"))
                pe.wait_ge(*read_out(pe, "zT"))
                x1T, zT = xT[:, 0, :], xT[:, 1, :]
                for name, off in (("lq", 0), ("lk", INNER)):
                    for j in range(4):
                        pe.wait_ge(*emptied(pe, f"{name}{j}"))
                        for a in range(2):
                            pr = 2 * j + a
                            last = mm(bank(f"{name}{j}")[:, a * N:(a + 1) * N], lqkvg[:, off + pr * P:off + (pr + 1) * P], zT, start=True, stop=True)
                        last.then_inc(*fills(f"{name}{j}"))
                    if name == "lq":
                        pe.wait_ge(*read_out(pe, "lq3"))
                        pe.wait_ge(*emptied(pe, "ssq"))
                        for t in range(NT):
                            for pr in range(NP):
                                last = mm(bank("ssq")[:, t * H:(t + 1) * H], sqT[:, pr, t * P:(t + 1) * P], pairsel[:, pr, :], start=(pr == 0), stop=(pr == NP - 1))
                        last.then_inc(*fills("ssq"))
                for name, off in (("tk", INNER), ("z", 3 * INNER)):
                    for t in range(NT):
                        for c in range(2):
                            use = f"{name}{t}{c}"
                            pe.wait_ge(*emptied(pe, use))
                            if name == "z":
                                mm(bank(use), ones3[:, :], bg3[:, c * 512:(c + 1) * 512], start=True, stop=False)
                            mm(bank(use), zT[:, t * P:(t + 1) * P], lqkvg[:, off + c * 512:off + (c + 1) * 512],
                                    start=(name != "z"), stop=True).then_inc(*fills(use))
                pe.wait_ge(*given(pe, "rq_ready"))
                pe.wait_ge(*emptied(pe, "rqT"))
                for t in range(NT):
                    last = tr(bank("rqT")[0:H, t * P:(t + 1) * P], small[:, 64 + t * H:64 + (t + 1) * H])
                last.then_inc(*fills("rqT"))
                pe.wait_ge(*read_out(pe, "rqT"))
                for j in range(4):
                    pe.wait_ge(*emptied(pe, f"rep{j}"))
                    for a in range(2):
                        last = mm(bank(f"rep{j}")[:, a * N:(a + 1) * N], headsel[:, 2 * j + a, :], rqT[:, :], start=True, stop=True)
                    last.then_inc(*fills(f"rep{j}"))
                for t in range(NT):
                    for c in range(2):
                        pe.wait_ge(*emptied(pe, f"tv{t}{c}"))
                        mm(bank(f"tv{t}{c}"), zT[:, t * P:(t + 1) * P], lqkvg[:, 2 * INNER + c * 512:2 * INNER + (c + 1) * 512], start=True, stop=True).then_inc(*fills(f"tv{t}{c}"))
                for t in range(NT):
                    pe.wait_ge(*given(pe, "at3_ready", t + 1))
                    for c in range(2):
                        pe.wait_ge(*emptied(pe, f"d{t}{c}"))
                        mm(bank(f"d{t}{c}"), identb[:, :], dmask[:, :, :], start=True, stop=False)
                        mm(bank(f"d{t}{c}"), strict[:, :], at3[:, t, c::2, :], start=False, stop=True).then_inc(*fills(f"d{t}{c}"))
                for t in range(NT):
                    for c in range(2):
                        (_, free_at), (_, k_at), (_, q_at) = emptied(pe, f"s{t}{c}"), read_out(pe, "lk3"), read_out(pe, "rep3")
                        free_at, k_at, q_at = pe.snap(free_at), pe.snap(k_at), pe.snap(q_at)
                        pe.wait_ge(sem("weights"), 16)
                        pe.wait_ge(emptied(pe, f"s{t}{c}")[0], free_at)
                        pe.wait_ge(read_out(pe, "lk3")[0], k_at)
                        pe.wait_ge(read_out(pe, "rep3")[0], q_at)
                        for ch in range(2):
                            for pr in range(NP):
                                cc = t * P + ch * CH
                                last = mm(bank(f"s{t}{c}")[ch * CH:(ch + 1) * CH, pr * CH:(pr + 1) * CH],
                                          kT[c * DH:(c + 1) * DH, pr, cc:cc + CH], qt[c * DH:(c + 1) * DH, pr, cc:cc + CH], start=True, stop=True)
                        last.then_inc(*fills(f"s{t}{c}"))
                for t in range(NT):
                    for c in range(2):
                        pe.wait_ge(*emptied(pe, f"te{t}{c}"))
                        mm(bank(f"te{t}{c}"), strict[:, :], a_tok[:, t, c * 512:(c + 1) * 512], start=True, stop=True).then_inc(*fills(f"te{t}{c}"))
                for j in range(4):
                    pe.wait_ge(*emptied(pe, f"la{j}"))
                    for a in range(2):
                        for t in range(NT):
                            last = mm(bank(f"la{j}")[:, a * N + t * P:a * N + (t + 1) * P], a_tok[:, t, (2 * j + a) * P:(2 * j + a + 1) * P], tri[:, :], start=True, stop=True)
                    last.then_inc(*fills(f"la{j}"))
                pe.wait_ge(*given(pe, "kd_ready"))
                pe.wait_ge(*read_out(pe, "tv11"))
                for n in range(NC - 1):
                    t, r0 = n // 2, (n % 2) * CH
                    for hh in range(2):
                        pe.wait_ge(*emptied(pe, f"st{n}{hh}"))
                        for a in range(4):
                            pr = 4 * hh + a
                            last = mm(bank(f"st{n}{hh}")[:, a * P:(a + 1) * P], kd[r0:r0 + CH, t, pr * P:(pr + 1) * P],
                                      v_tok[r0:r0 + CH, t, 2 * pr:2 * pr + 2, 0:DH], start=True, stop=True)
                        last.then_inc(*fills(f"st{n}{hh}"))
                pe.wait_ge(*read_out(pe, "s11"))
                pe.wait_ge(*given(pe, "qd_ready"))
                pe.wait_ge(*read_out(pe, "st21"))
                for j in range(4):
                    pe.wait_ge(*emptied(pe, f"o{j}"))
                    for a in range(2):
                        pr = 2 * j + a
                        for t in range(NT):
                            for c in range(2):
                                mm(bank(f"o{j}")[c * DH:(c + 1) * DH, a * N + t * P:a * N + (t + 1) * P],
                                   v_tok[:, t, 2 * pr + c, 0:DH], pbd[:, t, c, pr, :], start=True, stop=False)
                            for n in range(max(1, 2 * t), 2 * t + 2):
                                last = mm(bank(f"o{j}")[:, a * N + n * CH:a * N + (n + 1) * CH], st[:, n - 1, pr, :],
                                          el[:, pr, n * CH:(n + 1) * CH], start=False, stop=(n == 2 * t + 1))
                    last.then_inc(*fills(f"o{j}"))
                pe.wait_ge(*read_out(pe, "o3"))
                pe.wait_ge(*emptied(pe, "wo1"))
                for t in range(NT):
                    for pr in range(NP):
                        last = mm(bank("wo1")[:, t * P:(t + 1) * P], oT1[:, pr, t * P:(t + 1) * P], lwo[:, pr, :], start=(pr == 0), stop=(pr == NP - 1))
                last.then_inc(*fills("wo1"))
                pe.wait_ge(*emptied(pe, "gate1"))
                for t in range(NT):
                    last = mm(bank("gate1")[:, t * E:(t + 1) * E], x1T[:, t * P:(t + 1) * P], mg[:, :], start=True, stop=True)
                last.then_inc(*fills("gate1"))
                pe.wait_ge(*given(pe, "z2_ready"))
                pe.wait_ge(*emptied(pe, "z2T"))
                for t in range(NT):
                    last = tr(bank("z2T")[:, t * P:(t + 1) * P], xr[:, t, :])
                last.then_inc(*fills("z2T"))
                pe.wait_ge(*given(pe, "oh_ready"))
                pe.wait_ge(*emptied(pe, "ohT"))
                for t in range(NT):
                    last = tr(bank("ohT")[0:E, t * P:(t + 1) * P], small[:, 256 + t * E:256 + (t + 1) * E])
                last.then_inc(*fills("ohT"))
                pe.wait_ge(*read_out(pe, "z2T"))
                for j in range(2):
                    pe.wait_ge(*emptied(pe, f"f{j}"))
                    for a in range(2):
                        last = mm(bank(f"f{j}")[:, a * N:(a + 1) * N], lw1[:, (2 * j + a) * P:(2 * j + a + 1) * P], hT[:, :], start=True, stop=True)
                    last.then_inc(*fills(f"f{j}"))
                pe.wait_ge(*read_out(pe, "f1"))
                pe.wait_ge(*emptied(pe, "w2"))
                for t in range(NT):
                    for c in range(4):
                        last = mm(bank("w2")[:, t * P:(t + 1) * P], g1[:, c, t * P:(t + 1) * P], lw2[:, c, :], start=(c == 0), stop=(c == 3))
                last.then_inc(*fills("w2"))
                pe.wait_ge(*read_out(pe, "ohT"))
                pe.wait_ge(*emptied(pe, "b2y"))
                for t in range(NT):
                    last = mm(bank("b2y")[:, t * P:(t + 1) * P], ohT[:, t * P:(t + 1) * P], mb2[:, :], start=True, stop=True)
                last.then_inc(*fills("b2y"))
                for e in range(E + 1):
                    if e < E:
                        pe.wait_ge(sem(f"ew{e % 2}_ready"), i * (16 * E // 2) + 16 * (e // 2 + 1))
                        for j in range(2):
                            pe.wait_ge(*emptied(pe, f"h{e}{j}"))
                            for a in range(2):
                                c = 2 * j + a
                                last = mm(bank(f"h{e}{j}")[:, a * N:(a + 1) * N], ew[:, e % 2, c * P:(c + 1) * P], x1T, start=True, stop=True)
                            last.then_inc(*fills(f"h{e}{j}"))
                    if e:
                        pe.wait_ge(*read_out(pe, f"h{e - 1}1"))
                        pe.wait_ge(*emptied(pe, f"yy{e - 1}"))
                        for t in range(NT):
                            for c in range(4):
                                last = mm(bank(f"yy{e - 1}")[:, t * P:(t + 1) * P], r1[:, (e - 1) % 2, c, t * P:(t + 1) * P],
                                          ew[:, (e - 1) % 2, F1 + c * D:F1 + (c + 1) * D], start=(c == 0), stop=(c == 3))
                        last.then_inc(*fills(f"yy{e - 1}"))

        @blk.scalar
        def _(act):
            af = nc.scalar.activation

            def rstd(name, src, dst, scale, bias):
                act.wait_ge(*given(act, f"{name}_stat"))
                af(dst, src, ACT.Ln, scale=scale, bias=bias).then_inc(*signals("act_chain"))
                act.wait_ge(*chained(act, "act_chain"))
                af(dst, dst, ACT.Exp, scale=-0.5).then_inc(*signals(f"{name}_rstd"))

            act.wait_ge(sem("weights"), 16 * NLOAD[0])
            with act.Fori(0, B) as i:
                it[act.engine] = i
                eps = cols[:, 42:43]
                rstd("ln0", small[:, 1:4:2], small[:, 4:6], 1.0, eps)
                rstd("rms0", small[:, 6:8], small[:, 8:10], 1.0 / D, eps)
                for j in range(4):
                    act.wait_ge(*filled(act, f"q{j}"))
                    af(e_q[:, 2 * j:2 * j + 2, :], bank(f"q{j}").rearrange("p (a n) -> p a n", a=2), ACT.Exp).then_inc(*signals("eq"))
                    af(qt[:, 2 * j:2 * j + 2, :], bank(f"q{j}").rearrange("p (a n) -> p a n", a=2), ACT.Relu).then_inc(*frees(f"q{j}"))
                for t in range(NT):
                    for c in range(2):
                        act.wait_ge(*filled(act, f"k{t}{c}"))
                        af(e_k[:, t, c * 512:(c + 1) * 512], bank(f"k{t}{c}"), ACT.Exp).then_inc(*signals("ek"))
                        af(k_tok[:, t, c * 512:(c + 1) * 512], bank(f"k{t}{c}"), ACT.Relu).then_inc(*frees(f"k{t}{c}"))
                for t in range(NT):
                    for c in range(2):
                        act.wait_ge(*filled(act, f"oT{t}{c}"))
                        src = bank(f"oT{t}{c}").rearrange("p (a n) -> p a n", a=4)
                        ins = af(oT[:, 4 * c:4 * c + 4, t * P:(t + 1) * P], src, ACT.Copy)
                        ins.then_inc(*frees(f"oT{t}{c}"))
                for n in range(12):
                    act.wait_ge(*read_out(act, f"sc{n}"))
                    af(pp[:, n, :], pp[:, n, :], ACT.Exp, scale=float(HD) ** -0.5).then_inc(*signals("p_ready"))
                for n in range(0, 12, 2):
                    act.wait_ge(*filled(act, f"pT{n}"))
                    af(pT[:, n, :], bank(f"pT{n}"), ACT.Copy).then_inc(*frees(f"pT{n}"))
                act.wait_ge(*filled(act, "aT"))
                af(aT[:, :], bank("aT")[:, 0:N], ACT.Copy).then_inc(*frees("aT"))
                for t in range(NT):
                    act.wait_ge(*read_out(act, "wo"))
                    af(sq[:, t, :], x2[:, t, :], ACT.Square, accum_out=small[:, 10 + t:11 + t]).then_inc(*signals("act_chain"))
                    act.wait_ge(*chained(act, "act_chain"))
                af(small[:, 12:14], small[:, 10:12], ACT.Ln, scale=1.0 / D, bias=eps).then_inc(*signals("act_chain"))
                act.wait_ge(*chained(act, "act_chain"))
                af(small[:, 12:14], small[:, 12:14], ACT.Exp, scale=-0.5).then_inc(*signals("rms2_rstd"))
                act.wait_ge(*filled(act, "hT"))
                af(hT[:, :], bank("hT")[:, 0:N], ACT.Copy, scale=cols[:, 1:2]).then_inc(*frees("hT"))
                act.wait_ge(*given(act, "lg_ready"))
                af(small[:, 32:48], small[:, 32:48], ACT.Exp).then_inc(*signals("eg_ready"))
                for e in range(E):
                    act.wait_ge(*filled(act, f"a{e}"))
                    if e >= 2:
                        act.wait_ge(*filled(act, f"y{e - 2}"))
                    af(g0[:, e % 2, :, :], bank(f"a{e}").rearrange("p (c n) -> p c n", c=2), ACT.Silu).then_inc(*frees(f"a{e}"))
                act.wait_ge(*read_out(act, "y7"))
                af(sg[:, :, :], acc[:, :, :], ACT.Silu).then_inc(*signals("sg_ready"))
                rstd("ln1", small[:, 1:4:2], small[:, 4:6], 1.0, eps)
                rstd("ln1b", small[:, 1:4:2], small[:, 4:6], 1.0, eps)
                for j in range(4):
                    act.wait_ge(*filled(act, f"lq{j}"))
                    src = bank(f"lq{j}").rearrange("p (a n) -> p a n", a=2)
                    af(sqT[:, 2 * j:2 * j + 2, :], src, ACT.Square).then_inc(*signals("sq_done"))
                    af(qt[:, 2 * j:2 * j + 2, :], src, ACT.Copy).then_inc(*frees(f"lq{j}"))
                for j in range(4):
                    act.wait_ge(*filled(act, f"lk{j}"))
                    af(kT[:, 2 * j:2 * j + 2, :], bank(f"lk{j}").rearrange("p (a n) -> p a n", a=2), ACT.Copy).then_inc(*frees(f"lk{j}"))
                act.wait_ge(*read_out(act, "ssq"))
                af(small[:, 64:96], small[:, 64:96], ACT.Ln, scale=1e6).then_inc(*signals("act_chain"))
                act.wait_ge(*chained(act, "act_chain"))
                af(small[:, 64:96], small[:, 64:96], ACT.Exp, scale=-0.5).then_inc(*signals("rq_ready"))
                for t in range(NT):
                    for c in range(2):
                        act.wait_ge(*filled(act, f"tk{t}{c}"))
                        af(ks[:, t, c * 512:(c + 1) * 512], bank(f"tk{t}{c}"), ACT.Square).then_inc(*signals("ks"))
                for t in range(NT):
                    for c in range(2):
                        act.wait_ge(*filled(act, f"z{t}{c}"))
                        af(a_tok[:, t, c * 512:(c + 1) * 512], bank(f"z{t}{c}"), ACT.Exp, scale=-1.0).then_inc(*frees(f"z{t}{c}"))
                act.wait_ge(*given(act, "ssk_ready"))
                af(small[:, 96:128], small[:, 96:128], ACT.Ln, scale=1e6).then_inc(*signals("act_chain"))
                act.wait_ge(*chained(act, "act_chain"))
                af(small[:, 96:128], small[:, 96:128], ACT.Exp, scale=-0.5).then_inc(*signals("rk_ready"))
                for t in range(NT):
                    act.wait_ge(*given(act, "ez_clamped", t + 1))
                    af(a_tok[:, t, :], a_tok[:, t, :], ACT.Ln, bias=1.0).then_inc(*signals("a_ready"))
                for t in range(NT):
                    for c in range(2):
                        act.wait_ge(*filled(act, f"d{t}{c}"))
                        for ch in range(2):
                            rows = slice(ch * CH, (ch + 1) * CH)
                            src = bank(f"d{t}{c}")[rows, :].rearrange("p (a n) -> p a n", a=NP)
                            ins = af(pbd[rows, t, c, :, ch * CH:(ch + 1) * CH], src, ACT.Exp, scale=-1.0 / DH)
                            if ch == 0:
                                ins.then_inc(*signals("dec_half"))
                        ins.then_inc(*frees(f"d{t}{c}"))
                for t in range(NT):
                    for c in range(2):
                        act.wait_ge(*filled(act, f"te{t}{c}"))
                        af(kd[:, t, c * 512:(c + 1) * 512], bank(f"te{t}{c}"), ACT.Exp, scale=-1.0).then_inc(*frees(f"te{t}{c}"))
                for j in range(4):
                    act.wait_ge(*filled(act, f"la{j}"))
                    af(el[:, 2 * j:2 * j + 2, :], bank(f"la{j}").rearrange("p (a n) -> p a n", a=2), ACT.Exp, scale=-1.0).then_inc(*frees(f"la{j}"))
                for j in range(4):
                    act.wait_ge(*filled(act, f"o{j}"))
                    af(oT1[:, 2 * j:2 * j + 2, :], bank(f"o{j}").rearrange("p (a n) -> p a n", a=2), ACT.Copy).then_inc(*frees(f"o{j}"))
                rstd("ln2", small[:, 1:4:2], small[:, 4:6], 1.0, eps)
                for j in range(2):
                    act.wait_ge(*filled(act, f"f{j}"))
                    for a in range(2):
                        c = 2 * j + a
                        ins = af(g1[:, c, :], bank(f"f{j}")[:, a * N:(a + 1) * N], ACT.Gelu, bias=cols[:, 4 + c:5 + c])
                        if a == 0:
                            ins.then_inc(*signals("gelu_half"))
                    ins.then_inc(*frees(f"f{j}"))
                for e in range(E):
                    for j in range(2):
                        act.wait_ge(*filled(act, f"h{e}{j}"))
                        if e >= 2 and j == 0:
                            act.wait_ge(*filled(act, f"yy{e - 2}"))
                        for a in range(2):
                            c = 2 * j + a
                            ins = af(r1[:, e % 2, c, :], bank(f"h{e}{j}")[:, a * N:(a + 1) * N], ACT.Relu,
                                     bias=cols[:, 8 + 4 * e + c:9 + 4 * e + c])
                        ins.then_inc(*frees(f"h{e}{j}"))
                act.wait_ge(*read_out(act, "yy7"))
                af(sg[:, :, :], acc[:, :, :], ACT.Silu).then_inc(*signals("sg1_ready"))

        @blk.vector
        def _(dve):
            v = nc.vector

            def carry():
                v.memset(small[:, 511:512], 0.0)

            def stats(src, name):
                for t in range(NT):
                    v.bn_stats(small[:, 16 + 6 * t:22 + 6 * t], src[:, t, :]).then_inc(*signals("dve_chain"))
                    dve.wait_ge(*chained(dve, "dve_chain"))
                    if t == NT - 1:
                        carry()
                for t in range(NT):
                    ins = v.bn_aggr(small[:, 2 * t:2 * t + 2], small[:, 16 + 6 * t:22 + 6 * t])
                ins.then_inc(*signals(f"{name}_stat"))
                dve.wait_ge(*given(dve, f"{name}_stat"))

            def normed(dst, src, name, ready=None):
                stats(src, name)
                dve.wait_ge(*given(dve, f"{name}_rstd"))
                for t in range(NT):
                    ins = v.tensor_scalar(dst[:, t, :], src[:, t, :], small[:, 2 * t:2 * t + 1], small[:, 4 + t:5 + t], ALU.subtract, ALU.mult)
                    if t == NT - 1 and ready:
                        ins.then_inc(*signals(ready))
                    else:
                        ins.then_inc(*signals("dve_chain"))
                        dve.wait_ge(*chained(dve, "dve_chain"))

            def tok(ap):
                return ap.rearrange("p (t d) -> p t d", t=NT)

            dve.wait_ge(sem("weights"), 16 * NLOAD[0])
            ch0 = [0]

            def step(ins):
                ch0[0] += 1
                ins.then_inc(sem("setup_chain"), 1)
                dve.wait_ge(sem("setup_chain"), ch0[0])

            row, rest = big[0:1, 0:INNER], big[0:1, INNER:2 * INNER]
            step(v.tensor_copy(kd_b16(0), row))
            step(v.tensor_tensor(rest, row, kd_b16(0), ALU.subtract))
            step(v.tensor_copy(kd_b16(1), rest))
            step(v.tensor_tensor(rest, rest, kd_b16(1), ALU.subtract))
            v.tensor_copy(kd_b16(2), rest).then_inc(sem("bg_split"), 1)
            
            dve.wait_ge(sem("bg3_ready"), 48)
            dve.wait_ge(sem("zeros"), 4)
            dve.sem_inc(sem("x_free"), 1)
            dve.sem_inc(sem("ew0_free"), 1)
            dve.sem_inc(sem("ew1_free"), 1)
            with dve.Fori(0, B) as i:
                it[dve.engine] = i
                dve.wait_ge(*given(dve, "x_ready", 1, 16))
                normed(xn, x, "ln0")
                for t in range(NT):
                    v.scalar_tensor_tensor(out=xr[:, t, :], in0=xn[:, t, :], scalar=1.0, in1=xn[:, t, :], op0=ALU.mult, op1=ALU.mult).then_inc(*signals("dve_chain"))
                    dve.wait_ge(*chained(dve, "dve_chain"))
                v.tensor_reduce(small[:, 6:8], xr[:, :, :], AX.X, ALU.add).then_inc(*signals("rms0_stat"))
                dve.wait_ge(*given(dve, "rms0_rstd"))
                for t in range(NT):
                    ins = v.tensor_scalar(xr[:, t, :], xn[:, t, :], small[:, 8 + t:9 + t], None, ALU.mult)
                    if t == 0:
                        ins.then_inc(*signals("dve_chain"))
                        dve.wait_ge(*chained(dve, "dve_chain"))
                ins.then_inc(*signals("xr_ready"))
                dve.wait_ge(*filled(dve, "xT"))
                v.tensor_copy(xT[:, 0, :], bank("xT")[:, 0:N]).then_inc(*signals("xT_ready"))
                v.tensor_scalar(xT[:, 1, :], bank("xT")[:, N:2 * N], cols[:, 0:1], None, ALU.mult).then_inc(*frees("xT"))
                v.memset(v_tok[:, :, :, DH:V0], 1.0).then_inc(*signals("ones_ready"))
                for j in range(4):
                    dve.wait_ge(*read_out(dve, f"q{j}"))
                    s = slice(2 * j, 2 * j + 2)
                    ins = v.scalar_tensor_tensor(out=qt[:, s, :], in0=e_q[:, s, :], scalar=1.0, in1=qt[:, s, :], op0=ALU.min, op1=ALU.add)
                    ins.then_inc(*signals("q0_ready" if j == 3 else "q0_part"))
                for t in range(NT):
                    for c in range(2):
                        dve.wait_ge(*read_out(dve, f"k{t}{c}"))
                        s = slice(c * 512, (c + 1) * 512)
                        ins = v.scalar_tensor_tensor(out=k_tok[:, t, s], in0=e_k[:, t, s], scalar=1.0, in1=k_tok[:, t, s], op0=ALU.min, op1=ALU.add)
                        ins.then_inc(*signals("k0_ready" if 2 * t + c == 3 else "k0_part"))
                for t in range(NT):
                    for c in range(2):
                        dve.wait_ge(*filled(dve, f"v{t}{c}"))
                        v.tensor_copy(v_tok[:, t, 8 * c:8 * c + 8, 0:DH], bank(f"v{t}{c}").rearrange("p (h d) -> p h d", d=DH)).then_inc(*frees(f"v{t}{c}"))
                for j in range(2):
                    dve.wait_ge(*filled(dve, f"rq{j}"))
                    cb = ropec[:, 0:1, :].to_broadcast([P, 2, N])
                    v.tensor_tensor(rp[:, 2 * j:2 * j + 2, :], bank(f"rq{j}").rearrange("p (a n) -> p a n", a=2), cb, ALU.mult).then_inc(*frees(f"rq{j}"))
                for j in range(2):
                    dve.wait_ge(*filled(dve, f"rs{j}"))
                    sbc = ropec[:, 1:2, :].to_broadcast([P, 2, N])
                    v.tensor_tensor(rp[:, 4 + 2 * j:6 + 2 * j, :], bank(f"rs{j}").rearrange("p (a n) -> p a n", a=2), sbc, ALU.mult).then_inc(*frees(f"rs{j}"))
                dve.wait_ge(*filled(dve, "rk"))
                v.tensor_tensor(kr[:, :], bank("rk")[:, 0:N], ropec[:, 0, :], ALU.mult).then_inc(*signals("dve_chain"))
                dve.wait_ge(*chained(dve, "dve_chain"))
                v.tensor_tensor(krs, bank("rk")[:, N:2 * N], ropec[:, 1, :], ALU.mult).then_inc(*frees("rk"))
                dve.wait_ge(*filled(dve, "v9"))
                v.tensor_copy(v9[:, :, :, 0:HD], bank("v9")[:, 0:64].rearrange("p (t g d) -> p t g d", t=NT, g=NKV)).then_inc(*frees("v9"))
                dve.wait_ge(*read_out(dve, "rk"))
                v.tensor_tensor(kr[:, :], kr[:, :], krs, ALU.add).then_inc(*signals("dve_chain"))
                dve.wait_ge(*chained(dve, "dve_chain"))
                for j in range(4):
                    dve.wait_ge(*filled(dve, f"kv{j}"))
                    for c in range(2):
                        rows, cs = slice(c * DH, (c + 1) * DH), slice(c * V0, (c + 1) * V0)
                        src = bank(f"kv{j}").rearrange("p (a n) -> p a n", a=2)[rows, :, cs]
                        ins = v.tensor_copy(kvb[rows, 2 * j:2 * j + 2, cs], src)
                        if c == 0:
                            ins.then_inc(*signals("dve_chain"))
                            dve.wait_ge(*chained(dve, "dve_chain"))
                    ins.then_inc(*frees(f"kv{j}"))
                for t in range(NT):
                    for j in range(4):
                        dve.wait_ge(*filled(dve, f"num{t}{j}"))
                        nm = bank(f"num{t}{j}").rearrange("p (a n) -> p a n", a=2)[:, :, 0:2 * V0].rearrange("p a (h v) -> p a h v", v=V0)
                        dn = small[:, 304 + 4 * (j % 2):308 + 4 * (j % 2)]
                        den = dn.rearrange("p (a h) -> p a h", a=2)
                        v.tensor_scalar(den, nm[:, :, :, DH], 1e-6, None, ALU.add).then_inc(*signals("dve_chain"))
                        dve.wait_ge(*chained(dve, "dve_chain"))
                        v.reciprocal(dn, dn).then_inc(*signals("dve_chain"))
                        dve.wait_ge(*chained(dve, "dve_chain"))
                        ot = o_tok[:, t, 256 * j:256 * (j + 1)].rearrange("p (a h v) -> p a h v", a=2, v=DH)
                        rb = dn.rearrange("p (a h o) -> p a h o", a=2, o=1).to_broadcast([P, 2, 2, DH])
                        v.tensor_tensor(ot, nm[:, :, :, 0:DH], rb, ALU.mult).then_inc(*frees(f"num{t}{j}"))
                v.tensor_tensor(qt[:, 0:4, :], rp[:, 0:4, :], rp[:, 4:8, :], ALU.add).then_inc(*signals("rope_ready"))
                dve.wait_ge(*filled(dve, "s0"))
                v.tensor_tensor(s0[:, :, :], tok(bank("s0")[:, 0:N]), boutb[:, :].rearrange("p (o d) -> p o d", o=1).to_broadcast([P, NT, D]), ALU.add).then_inc(*frees("s0"))
                for n in range(12):
                    hs = 4 if n < 4 else 2
                    dve.wait_ge(*filled(dve, f"sc{n}"))
                    sc = bank(f"sc{n}").rearrange("p (h k) -> p h k", h=hs)
                    nm = small[:, 320 + 4 * (n % 2):320 + 4 * (n % 2) + hs]
                    v.tensor_reduce(nm, sc, AX.X, ALU.max, negate=True).then_inc(*signals("dve_chain"))
                    dve.wait_ge(*chained(dve, "dve_chain"))
                    nb = nm.rearrange("p (h o) -> p h o", o=1).to_broadcast([P, hs, 512 // hs])
                    if n == 0:
                        dve.wait_ge(*given(dve, "rope_ready"))
                    v.tensor_tensor(pp[:, n, :].rearrange("p (h k) -> p h k", h=hs), sc, nb, ALU.add).then_inc(*frees(f"sc{n}"))
                for n in range(1, 12, 2):
                    dve.wait_ge(*filled(dve, f"pT{n}"))
                    v.tensor_copy(pT[:, n, :], bank(f"pT{n}")).then_inc(*frees(f"pT{n}"))
                dve.wait_ge(*filled(dve, "pv"))
                pv = bank("pv")[:, 0:2 * NHF * V1].rearrange("p (h v) -> p h v", v=V1)
                v.reciprocal(small[:, 128:160].rearrange("p (h o) -> p h o", o=1), pv[:, :, HD:V1]).then_inc(*signals("dve_chain"))
                dve.wait_ge(*chained(dve, "dve_chain"))
                v.tensor_tensor(ao[:, :, :].rearrange("p t (h d) -> p (t h) d", d=HD), pv[:, :, 0:HD],
                                     small[:, 128:160].rearrange("p (h o) -> p h o", o=1).to_broadcast([P, 2 * NHF, HD]), ALU.mult).then_inc(*frees("pv"))
                dve.wait_ge(*filled(dve, "wo"))
                v.tensor_tensor(x2[:, :, :], xn[:, :, :], tok(bank("wo")[:, 0:N]), ALU.add).then_inc(*frees("wo"))
                dve.wait_ge(*given(dve, "rms2_rstd"))
                for t in range(NT):
                    ins = v.tensor_scalar(sq[:, t, :], x2[:, t, :], small[:, 12 + t:13 + t], None, ALU.mult)
                    if t == 0:
                        ins.then_inc(*signals("dve_chain"))
                        dve.wait_ge(*chained(dve, "dve_chain"))
                ins.then_inc(*signals("h2_ready"))
                dve.wait_ge(*filled(dve, "gate"))
                lg = small[:, 160:176].rearrange("p (t e) -> p t e", t=NT)
                v.tensor_copy(small[:, 160:176], bank("gate")[:, 0:NT * E]).then_inc(*frees("gate"))
                dve.wait_ge(*read_out(dve, "gate"))
                carry()
                m8 = small[:, 176:192].rearrange("p (t e) -> p t e", t=NT)
                for t in range(NT):
                    ins = v.max(m8[:, t, :], lg[:, t, :])
                ins.then_inc(*signals("dve_chain"))
                dve.wait_ge(*chained(dve, "dve_chain"))
                carry()
                for t in range(NT):
                    ins = v.max_index(idx8[:, t, :], m8[:, t, :], lg[:, t, :])
                ins.then_inc(*signals("dve_chain"))
                dve.wait_ge(*chained(dve, "dve_chain"))
                v.tensor_tensor(small[:, 32:48].rearrange("p (t e) -> p t e", t=NT), lg, m8[:, :, 0:1].to_broadcast([P, NT, E]), ALU.subtract).then_inc(*signals("lg_ready"))
                idf = small[:, 192:208].rearrange("p (t e) -> p t e", t=NT)
                v.tensor_copy(idf, idx8[:, :, :]).then_inc(*signals("dve_chain"))
                dve.wait_ge(*chained(dve, "dve_chain"))
                io = iota8[:, :].rearrange("p (o e) -> p o e", o=1).to_broadcast([P, NT, E])
                oh = small[:, 208:240].rearrange("p (k t e) -> p k t e", k=2, t=NT)
                for k in range(2):
                    v.tensor_tensor(oh[:, k, :, :], io, idf[:, :, k:k + 1].to_broadcast([P, NT, E]), ALU.is_equal).then_inc(*signals("dve_chain"))
                    dve.wait_ge(*chained(dve, "dve_chain"))
                v.tensor_tensor(oh[:, 0, :, :], oh[:, 0, :, :], oh[:, 1, :, :], ALU.add).then_inc(*signals("dve_chain"))
                dve.wait_ge(*chained(dve, "dve_chain"))
                dve.wait_ge(*given(dve, "eg_ready"))
                gw = small[:, 240:256].rearrange("p (t e) -> p t e", t=NT)
                v.tensor_tensor(gw, small[:, 32:48].rearrange("p (t e) -> p t e", t=NT), oh[:, 0, :, :], ALU.mult).then_inc(*signals("dve_chain"))
                dve.wait_ge(*chained(dve, "dve_chain"))
                v.tensor_reduce(small[:, 56:58], gw, AX.X, ALU.add).then_inc(*signals("dve_chain"))
                dve.wait_ge(*chained(dve, "dve_chain"))
                v.reciprocal(small[:, 56:58], small[:, 56:58]).then_inc(*signals("dve_chain"))
                dve.wait_ge(*chained(dve, "dve_chain"))
                v.tensor_tensor(gw, gw, small[:, 56:58].rearrange("p (t o) -> p t o", o=1).to_broadcast([P, NT, E]), ALU.mult).then_inc(*signals("dve_chain"))
                dve.wait_ge(*chained(dve, "dve_chain"))
                for e in range(E + 1):
                    if e < E:
                        dve.wait_ge(*filled(dve, f"b{e}"))
                        dve.wait_ge(*read_out(dve, f"a{e}"))
                        gs = g0[:, e % 2, :, :]
                        v.tensor_tensor(gs, gs, bank(f"b{e}").rearrange("p (c n) -> p c n", c=2), ALU.mult).then_inc(*frees(f"b{e}"))
                    if e:
                        dve.wait_ge(*filled(dve, f"y{e - 1}"))
                        for t in range(NT):
                            ins = v.scalar_tensor_tensor(out=acc[:, t, :], in0=bank(f"y{e - 1}")[:, t * P:(t + 1) * P], scalar=gw[:, t, e - 1:e],
                                                         in1=(x2 if e == 1 else acc)[:, t, :], op0=ALU.mult, op1=ALU.add)
                            if t == 0:
                                ins.then_inc(*signals("dve_chain"))
                                dve.wait_ge(*chained(dve, "dve_chain"))
                        ins.then_inc(*frees(f"y{e - 1}"))
                        dve.wait_ge(*read_out(dve, f"y{e - 1}"))
                dve.wait_ge(*given(dve, "sg_ready"))
                v.tensor_tensor(x1[:, :, :], s0[:, :, :], sg[:, :, :], ALU.mult).then_inc(*signals("dve_chain"))
                dve.wait_ge(*chained(dve, "dve_chain"))
                v.tensor_tensor(x1[:, :, :], x1[:, :, :], x[:, :, :], ALU.add).then_inc(*signals("x_free"))
                dve.wait_ge(*given(dve, "x_free", 2))
                normed(xn, x1, "ln1")
                normed(xr, xn, "ln1b", "z1_ready")
                dve.wait_ge(*filled(dve, "zT"))
                v.tensor_copy(xT[:, 0, :], bank("zT")[:, 0:N]).then_inc(*signals("dve_chain"))
                dve.wait_ge(*chained(dve, "dve_chain"))
                v.tensor_scalar(xT[:, 1, :], bank("zT")[:, N:2 * N], cols[:, 2:3], cols[:, 40:41], ALU.mult, ALU.add).then_inc(*frees("zT"))
                dve.wait_ge(*filled(dve, "ssq"))
                v.tensor_scalar(small[:, 64:96], bank("ssq")[:, 0:2 * H], 1e-24, None, ALU.max).then_inc(*frees("ssq"))
                for t in range(NT):
                    for c in range(2):
                        dve.wait_ge(*filled(dve, f"tk{t}{c}"))
                        dve.wait_ge(*given(dve, "ks", 2 * t + c + 1))
                        v.tensor_copy(k_tok[:, t, c * 512:(c + 1) * 512], bank(f"tk{t}{c}")).then_inc(*frees(f"tk{t}{c}"))
                v.tensor_reduce(small[:, 96:128], reg[:, 0:2048].rearrange("p (h d) -> p h d", d=DH), AX.X, ALU.add).then_inc(*signals("dve_chain"))
                dve.wait_ge(*chained(dve, "dve_chain"))
                v.tensor_scalar(small[:, 96:128], small[:, 96:128], 1e-24, None, ALU.max).then_inc(*signals("ssk_ready"))
                for t in range(NT):
                    dve.wait_ge(*read_out(dve, f"z{t}1"))
                    v.tensor_scalar(a_tok[:, t, :], a_tok[:, t, :], 999999.0, None, ALU.min).then_inc(*signals("ez_clamped"))
                dve.wait_ge(*filled(dve, "rqT"))
                v.tensor_copy(rqT[:, :], bank("rqT")[0:H, 0:N]).then_inc(*frees("rqT"))
                for j in range(4):
                    dve.wait_ge(*filled(dve, f"rep{j}"))
                    s = slice(2 * j, 2 * j + 2)
                    v.scalar_tensor_tensor(out=qt[:, s, :], in0=bank(f"rep{j}").rearrange("p (a n) -> p a n", a=2), scalar=1e3, in1=qt[:, s, :], op0=ALU.mult, op1=ALU.mult).then_inc(*frees(f"rep{j}"))
                dve.wait_ge(*given(dve, "rk_ready"))
                for t in range(NT):
                    for c in range(2):
                        dve.wait_ge(*filled(dve, f"tv{t}{c}"))
                        rb = small[:, 96 + t * H + 8 * c:96 + t * H + 8 * c + 8].rearrange("p (h o) -> p h o", o=1).to_broadcast([P, 8, DH])
                        v.scalar_tensor_tensor(out=v_tok[:, t, 8 * c:8 * c + 8, 0:DH], in0=bank(f"tv{t}{c}").rearrange("p (h d) -> p h d", d=DH),
                                                    scalar=1e3, in1=rb, op0=ALU.mult, op1=ALU.mult).then_inc(*frees(f"tv{t}{c}"))
                for t in range(NT):
                    dve.wait_ge(*given(dve, "a_ready", t + 1))
                    am = small[:, 272 + t * H:272 + (t + 1) * H]
                    v.tensor_reduce(am, a_tok[:, t, :].rearrange("p (h d) -> p h d", d=DH), AX.X, ALU.add).then_inc(*signals("dve_chain"))
                    dve.wait_ge(*chained(dve, "dve_chain"))
                    v.tensor_tensor(at3[:, t, :, :], am.rearrange("p (h o) -> p h o", o=1).to_broadcast([P, H, CH]),
                                         tri64[:, :].rearrange("p (o c) -> p o c", o=1).to_broadcast([P, H, CH]), ALU.mult).then_inc(*signals("at3_ready"))
                for t in range(NT):
                    for c in range(2):
                        dve.wait_ge(*filled(dve, f"s{t}{c}"))
                        dve.wait_ge(*read_out(dve, f"d{t}{c}"))
                        for ch in range(2):
                            rows = slice(ch * CH, (ch + 1) * CH)
                            w = pbd[rows, t, c, :, ch * CH:(ch + 1) * CH]
                            ins = v.tensor_tensor(w, bank(f"s{t}{c}")[rows, :].rearrange("p (a n) -> p a n", a=NP), w, ALU.mult)
                            if ch == 0:
                                ins.then_inc(*signals("dve_chain"))
                                dve.wait_ge(*chained(dve, "dve_chain"))
                        ins.then_inc(*frees(f"s{t}{c}"))
                for t in range(NT):
                    for c in range(2):
                        dve.wait_ge(*read_out(dve, f"te{t}{c}"))
                        s = slice(c * 512, (c + 1) * 512)
                        ins = v.tensor_tensor(kd[:, t, s], kd[:, t, s], k_tok[:, t, s], ALU.mult)
                        ins.then_inc(*signals("kd_ready" if 2 * t + c == 3 else "kd_part"))
                dve.wait_ge(*read_out(dve, "la3"))
                v.tensor_copy(cd[:, :, :], el[:, :, CH - 1::CH]).then_inc(*signals("dve_chain"))
                dve.wait_ge(*chained(dve, "dve_chain"))
                v.tensor_tensor(el[:, :, :], el[:, :, :], qt[:, :, :], ALU.mult).then_inc(*signals("qd_ready"))
                for n in range(NC - 1):
                    for hh in range(2):
                        dve.wait_ge(*filled(dve, f"st{n}{hh}"))
                        ps = slice(4 * hh, 4 * hh + 4)
                        for c in range(2):
                            rows = slice(c * DH, (c + 1) * DH)
                            src = bank(f"st{n}{hh}").rearrange("p (a n) -> p a n", a=4)[rows, :, rows]
                            dst = st[rows, n, ps, rows]
                            if n == 0:
                                ins = v.tensor_copy(dst, src)
                            else:
                                v.tensor_tensor(dst, st[rows, n - 1, ps, rows], cd[rows, ps, n:n + 1].to_broadcast([DH, 4, DH]), ALU.mult).then_inc(*signals("dve_chain"))
                                dve.wait_ge(*chained(dve, "dve_chain"))
                                ins = v.tensor_tensor(dst, dst, src, ALU.add)
                            if c == 0:
                                ins.then_inc(*signals("dve_chain"))
                                dve.wait_ge(*chained(dve, "dve_chain"))
                        ins.then_inc(*frees(f"st{n}{hh}"))
                        dve.wait_ge(*read_out(dve, f"st{n}{hh}"))
                dve.wait_ge(*filled(dve, "wo1"))
                v.tensor_tensor(x2[:, :, :], xn[:, :, :], tok(bank("wo1")[:, 0:N]), ALU.add).then_inc(*frees("wo1"))
                dve.wait_ge(*read_out(dve, "wo1"))
                normed(xr, x2, "ln2", "z2_ready")
                dve.wait_ge(*filled(dve, "gate1"))
                v.tensor_tensor(lg, bank("gate1")[:, 0:NT * E].rearrange("p (t e) -> p t e", t=NT),
                                     bgb[:, :].rearrange("p (o e) -> p o e", o=1).to_broadcast([P, NT, E]), ALU.add).then_inc(*frees("gate1"))
                dve.wait_ge(*read_out(dve, "gate1"))
                carry()
                for t in range(NT):
                    ins = v.max(m8[:, t, :], lg[:, t, :])
                ins.then_inc(*signals("dve_chain"))
                dve.wait_ge(*chained(dve, "dve_chain"))
                carry()
                for t in range(NT):
                    ins = v.max_index(idx8[:, t, :], m8[:, t, :], lg[:, t, :])
                ins.then_inc(*signals("dve_chain"))
                dve.wait_ge(*chained(dve, "dve_chain"))
                v.tensor_copy(idf, idx8[:, :, :]).then_inc(*signals("dve_chain"))
                dve.wait_ge(*chained(dve, "dve_chain"))
                oh1 = small[:, 256:272].rearrange("p (t e) -> p t e", t=NT)
                v.tensor_tensor(oh1, io, idf[:, :, 0:1].to_broadcast([P, NT, E]), ALU.is_equal).then_inc(*signals("oh_ready"))
                dve.wait_ge(*filled(dve, "z2T"))
                v.tensor_scalar(hT[:, :], bank("z2T")[:, 0:N], cols[:, 3:4], cols[:, 41:42], ALU.mult, ALU.add).then_inc(*frees("z2T"))
                dve.wait_ge(*filled(dve, "ohT"))
                v.tensor_copy(ohT[:, :], bank("ohT")[0:E, 0:N]).then_inc(*frees("ohT"))
                b2bb = b2b[:, :].rearrange("p (o d) -> p o d", o=1).to_broadcast([P, NT, D])
                v.tensor_tensor(x2[:, :, :], x2[:, :, :], b2bb, ALU.add).then_inc(*signals("dve_chain"))
                dve.wait_ge(*chained(dve, "dve_chain"))
                dve.wait_ge(*filled(dve, "w2"))
                v.tensor_tensor(x2[:, :, :], x2[:, :, :], tok(bank("w2")[:, 0:N]), ALU.add).then_inc(*frees("w2"))
                dve.wait_ge(*filled(dve, "b2y"))
                v.tensor_copy(acc[:, :, :], tok(bank("b2y")[:, 0:N])).then_inc(*frees("b2y"))
                dve.wait_ge(*read_out(dve, "b2y"))
                for e in range(E):
                    dve.wait_ge(*filled(dve, f"yy{e}"))
                    for t in range(NT):
                        ins = v.scalar_tensor_tensor(out=acc[:, t, :], in0=bank(f"yy{e}")[:, t * P:(t + 1) * P], scalar=oh1[:, t, e:e + 1],
                                                     in1=acc[:, t, :], op0=ALU.mult, op1=ALU.add)
                        if t == 0:
                            ins.then_inc(*signals(f"ew{e % 2}_free"))
                    ins.then_inc(*frees(f"yy{e}"))
                    dve.wait_ge(*read_out(dve, f"yy{e}"))
                dve.wait_ge(*given(dve, "sg1_ready"))
                v.tensor_tensor(x2[:, :, :], x2[:, :, :], sg[:, :, :], ALU.mult).then_inc(*signals("dve_chain"))
                dve.wait_ge(*chained(dve, "dve_chain"))
                dve.wait_ge(sem("stored"), i * 16 + 16)
                with_out = v.tensor_tensor(ov[:, :, :], x2[:, :, :], x1[:, :, :], ALU.add)
                with_out.then_inc(*signals("out_ready"))
        bad = {k: n for k, n in count.items() if PER.get(k, 1) != n}
        assert not bad


SHAPES = {}


def kernel(**inputs):
    import concourse.bacc as bacc
    from concourse.bass_utils import run_bass_kernel_spmd

    I = {k: np.asarray(v) for k, v in inputs.items()}
    ca = np.ascontiguousarray
    bf = mybir.dt.np(mybir.dt.bfloat16)

    def split_k(w):
        return ca(w.reshape(-1, P, w.shape[-1]).transpose(1, 0, 2))

    wq = I["L0_ffn_wqkv"]
    q = wq[:NHF * HD].reshape(NKV, GR, HD, D)
    k = wq[NHF * HD:(NHF + NKV) * HD].reshape(NKV, 1, HD, D)
    turn = np.r_[HD // 2:HD, 0:HD // 2]
    wrope = np.zeros((D, 10, P), np.float32)
    for g in range(NKV):
        for a in range(GR):
            wrope[:, a, 32 * g:32 * g + HD] = q[g, a].T
            wrope[:, 4 + a, 32 * g:32 * g + HD] = q[g, a][turn].T
        wrope[:, 8, 32 * g:32 * g + HD] = k[g, 0].T
        wrope[:, 9, 32 * g:32 * g + HD] = k[g, 0][turn].T
    inv = (1.0 / np.float32(10000.0) ** (np.arange(0, HD, 2, dtype=np.float32) / np.float32(HD))).astype(np.float32)
    ang = np.arange(N, dtype=np.float32)[:, None] * inv[None, :]
    ang = np.concatenate([ang, ang], -1).T
    ropec = np.zeros((P, 2, N), np.float32)
    for g in range(NKV):
        ropec[32 * g:32 * g + HD, 0] = np.cos(ang)
        ropec[32 * g:32 * g + HD, 1] = np.sin(ang) * np.r_[-np.ones(HD // 2), np.ones(HD // 2)].astype(np.float32)[:, None]
    ew = np.concatenate([I["L1_ffn_W1"], I["L1_ffn_W2"].reshape(E, 4, P, D).transpose(0, 2, 1, 3).reshape(E, P, 4 * D)], -1)
    cols = np.concatenate([
        I["L0_ffn_ln1_w"][:, None], I["L0_ffn_ln2_w"][:, None], I["L1_attn_ln1_w"][:, None], I["L1_attn_ln2_w"][:, None],
        I["L1_attn_b1"].reshape(4, P).T, I["L1_ffn_b1"].reshape(E * 4, P).T,
        I["L1_attn_ln1_b"][:, None], I["L1_attn_ln2_b"][:, None], np.full((P, 1), 1e-5, np.float32)], 1)
    r = np.arange(P)
    same = (r[:, None] // CH) == (r[None, :] // CH)
    keep = r[None, :] <= r[:, None]
    cmask = np.zeros((P, 2, 512), np.float32)
    cmask[:, 0] = np.tile(np.where(keep, 0, NEG), (1, 4))
    cmask[:, 1] = np.tile(np.concatenate([np.zeros((P, P)), np.where(keep, 0, NEG)], 1), (1, 2))
    dmask = np.tile(np.where(np.arange(CH)[None, :] < (r % CH)[:, None], -NEG, 0)[:, None, :], (1, 8, 1))
    h = np.arange(H)
    arrays = {
        "x": I["L0_attn_x"],
        "wqkv0": I["L0_attn_Wqkv"], "wout0": split_k(I["L0_attn_Wout"]), "bout": I["L0_attn_bout"],
        "wrope": wrope, "ropec": ropec, "wv9": ca(wq[(NHF + NKV) * HD:].T), "woT": ca(I["L0_ffn_wo"].T), "gateT": ca(I["L0_ffn_gate_w"].T),
        "w13T": ca(I["L0_ffn_w13"].transpose(2, 0, 1)),
        "w2T": ca(I["L0_ffn_w2"].reshape(E, D, 2, P).transpose(3, 0, 2, 1)),
        "lqkvg": ca(np.concatenate([I["L1_attn_Wq"], I["L1_attn_Wk"], I["L1_attn_Wv"], I["L1_attn_Wg"]], 1)),
        "bg": I["L1_attn_bg"].reshape(1, -1), "lwo": split_k(I["L1_attn_Wo"]), "lw1": I["L1_attn_W1"], "lw2": split_k(I["L1_attn_W2"]),
        "mg": I["L1_ffn_Wg"], "mb2": I["L1_ffn_b2"], "cols": ca(cols), "bgm": I["L1_ffn_bg"], "b2": I["L1_attn_b2"], "ew": ca(ew),
        "identb": np.eye(P, dtype=np.float32).astype(bf), "cmask": cmask.astype(bf), "dmask": dmask.astype(bf), "ones3": np.ones((3, P), bf),
        "tri": (same & (r[:, None] <= r[None, :])).astype(np.float32), "strict": (same & (r[:, None] > r[None, :])).astype(np.float32),
        "tri64": ((r % CH)[:, None] <= np.arange(CH)[None, :]).astype(np.float32), "ident": np.eye(P, dtype=np.float32),
        "pairsel": (h[None, None, :] == 2 * np.arange(NP)[None, :, None] + (r // DH)[:, None, None]).astype(np.float32),
        "headsel": (h[:, None, None] == 2 * np.arange(NP)[None, :, None] + (r // DH)[None, None, :]).astype(np.float32),
        "iota8": np.tile(np.arange(E, dtype=np.float32), (P, 1)),
    }
    nc = bacc.Bacc("TRN2", target_bir_lowering=False, num_devices=1)
    feeds = {f"in_{n}": ca(a) for n, a in arrays.items()}
    A = {n: nc.dram_tensor(f"in_{n}", a.shape, mybir.dt.from_np(a.dtype), kind="ExternalInput").ap() for n, a in arrays.items()}
    out = nc.dram_tensor("out", (B, N, D), mybir.dt.float32, kind="ExternalOutput").ap()
    build(nc, A, out)
    r = run_bass_kernel_spmd(nc, [feeds], core_ids=[0])
    return r.results[0]["out"]
```

```python
from contextlib import ExitStack

import concourse.bass as bass
import numpy as np
from concourse import mybir

B, N, D = 16, 256, 128
P = 128
NT = N // P
H, DH = 16, 64
NP = H // 2
INNER = H * DH
NHF, NKV, HD = 16, 4, 8
GR = NHF // NKV
E = 8
F0 = 256
F1 = 512
CH = 64
NC = N // CH
V1 = HD + 1
V0 = DH + 1
NEG = -3.0e38

SEGMENTS = [("AB", 1), ("ABC", 1), ("ABCD", B - 2), ("CD", 1), ("D", 1)]

RING = 7

def uses_in_order(stages):
    names = []

    def moe0(e):
        if "B" in stages:
            if e < E:
                names.extend([f"a{e}", f"b{e}"])
            if e:
                names.append(f"y{e - 1}")

    def moe1(e):
        if "D" in stages:
            if e < E:
                names.extend([f"h{e}0", f"h{e}1"])
            if e:
                names.append(f"yy{e - 1}")

    if "A" in stages:
        moe1(0)
        names += ["xT"]
        moe1(1)
        names += [f"q{j}" for j in range(4)]
        names += [f"k{t}{c}" for t in range(NT) for c in range(2)]
        names += [f"v{t}{c}" for t in range(NT) for c in range(2)]
        names += [f"rq{j}" for j in range(2)] + [f"rs{j}" for j in range(2)] + ["rk", "v9"]
        moe1(2)
        names += [f"kv{j}" for j in range(4)]
        moe1(3)
        names += [f"num{t}{j}" for t in range(NT) for j in range(4)]
        moe1(4)
        names += [f"oT{t}{c}" for t in range(NT) for c in range(2)] + ["s0"]
        for n in range(12):
            names += [f"sc{n}"]
            if n == 5:
                moe1(5)
        moe1(6)
        for n in range(12):
            names += [f"pT{n}"]
            if n == 5:
                moe1(7)
        moe1(8)
        names += ["pv", "aT", "wo", "hT", "gate"]
    else:
        for e in range(E + 1):
            moe1(e)
    if "C" in stages:
        moe0(0)
        moe0(1)
        names += ["zT"]
        moe0(2)
        names += [f"lq{j}" for j in range(4)] + ["ssq"] + [f"lk{j}" for j in range(4)]
        names += [f"tk{t}{c}" for t in range(NT) for c in range(2)]
        names += [f"z{t}{c}" for t in range(NT) for c in range(2)]
        moe0(3)
        names += ["rqT"] + [f"rep{j}" for j in range(4)]
        names += [f"tv{t}{c}" for t in range(NT) for c in range(2)]
        moe0(4)
        names += [f"d{t}{c}" for t in range(NT) for c in range(2)]
        names += [f"s{t}{c}" for t in range(NT) for c in range(2)]
        names += [f"te{t}{c}" for t in range(NT) for c in range(2)]
        names += [f"la{j}" for j in range(4)]
        moe0(5)
        names += [f"st{n}{hh}" for n in range(NC - 1) for hh in range(2)]
        moe0(6)
        names += [f"o{j}" for j in range(4)]
        names += ["wo1", "gate1"]
        moe0(7)
        names += ["z2T", "ohT", "f0", "f1"]
        moe0(8)
        names += ["w2", "b2y"]
    else:
        for e in range(E + 1):
            moe0(e)
    return names

def psum_plan():
    plans, uses, nxt, total = [], [], 0, [0] * RING
    for stages, times in SEGMENTS:
        plan, n = {}, [0] * RING
        for i, name in enumerate(uses_in_order(stages)):
            b = (nxt + i) % RING
            n[b] += 1
            plan[name] = (b, total[b] + n[b])
        if times == 1:
            nxt = (nxt + len(plan)) % RING
        plans.append(plan)
        uses.append(n)
        total = [total[b] + n[b] * times for b in range(RING)]
    return plans, uses

PLANS, USES = psum_plan()

PER = {
    "A": {"act_chain": 5, "dve_chain": 53, "eg_ready": 1, "ek": 4, "eq": 4, "h2_ready": 1, "k0_part": 3, "k0_ready": 1,
          "lg_ready": 1, "ln0_rstd": 1, "ln0_stat": 1, "ones_ready": 1, "p_ready": 12, "q0_part": 3, "q0_ready": 1, "rms0_rstd": 1,
          "rms0_stat": 1, "rms2_rstd": 1, "rope_ready": 1, "xT_ready": 1, "x_free": 1, "x_ready": 1, "xr_ready": 1},
    "B": {"dve_chain": 10, "sg_ready": 1},
    "C": {"a_ready": 2, "act_chain": 5, "at3_ready": 2, "dec_half": 4, "dve_chain": 38, "ez_clamped": 2, "gelu_half": 2,
          "kd_part": 3, "kd_ready": 1, "ks": 4, "ln1_rstd": 1, "ln1_stat": 1, "ln1b_rstd": 1, "ln1b_stat": 1, "ln2_rstd": 1,
          "ln2_stat": 1, "oh_ready": 1, "qd_ready": 1, "rk_ready": 1, "rq_ready": 1, "sq_done": 4, "ssk_ready": 1, "z1_ready": 1,
          "z2_ready": 1},
    "D": {"dve_chain": 1, "ew0_free": 4, "ew0_ready": 4, "ew1_free": 4, "ew1_ready": 4, "out_ready": 1, "sg1_ready": 1},
}

def in_body(stages, name):
    return sum(PER[s].get(name, 0) for s in stages)

def build(nc, A, out, debug=None):
    dt = mybir.dt
    f32, b16 = dt.float32, dt.bfloat16
    ALU, ACT, AX = mybir.AluOpType, mybir.ActivationFunctionType, mybir.AxisListType
    ctx = ExitStack()
    with ctx:
        def sb(name, shape, d=f32):
            return ctx.enter_context(nc.sbuf_tensor(name, shape, d))

        wqkv0 = sb("wqkv0", [P, 3 * INNER])
        wout0 = sb("wout0", [P, NP, D])
        boutb = sb("boutb", [P, D])
        wrope = sb("wrope", [P, 10, P])
        wv9 = sb("wv9", [P, NKV * HD])
        woT = sb("woT", [P, D])
        gateT = sb("gateT", [P, E])
        w13T = sb("w13T", [P, E, 2 * F0])
        w2T = sb("w2T", [P, E, 2, D])
        lqkvg = sb("lqkvg", [P, 4 * INNER])
        bg3 = sb("bg3", [3, INNER], b16)
        lwo = sb("lwo", [P, NP, D])
        lw1 = sb("lw1", [P, F1])
        lw2 = sb("lw2", [P, 4, D])
        mg = sb("mg", [P, E])
        mb2 = sb("mb2", [E, D])
        cols = sb("cols", [P, 43])
        bgb = sb("bgb", [P, E])
        b2b = sb("b2b", [P, D])
        ropec = sb("ropec", [P, 2, N])
        tri = sb("tri", [P, P])
        strict = sb("strict", [P, P])
        tri64 = sb("tri64", [P, CH])
        ident = sb("ident", [P, P])
        identb = sb("identb", [P, P], b16)
        cmask = sb("cmask", [P, 2, 2 * N], b16)
        dmask = sb("dmask", [P, 8, CH], b16)
        ones3 = sb("ones3", [3, P], b16)
        pairsel = sb("pairsel", [P, NP, H])
        headsel = sb("headsel", [H, NP, P])
        iota8 = sb("iota8", [P, E])
        ew = sb("ew", [P, 2, 2 * F1 * 1])
        x = sb("x", [P, NT, D])
        xn = sb("xn", [P, NT, D])
        xr = sb("xr", [P, NT, D])
        xT = sb("xT_s", [P, 2, N])
        x2 = sb("x2", [P, NT, D])
        hT = sb("hT_s", [P, N])
        acc0 = sb("acc0", [P, NT, D])
        acc1 = sb("acc1", [P, NT, D])
        x_keep = sb("x_keep", [P, NT, D])
        x1_keep = sb("x1_keep", [P, NT, D])
        y2 = sb("y2", [P, NT, D])
        x1T = sb("x1T_s", [P, N])
        gbuf = sb("gbuf", [P, 4 * N])
        s0 = sb("s0_s", [P, NT, D])
        sg = sb("sg", [P, NT, D])
        x1 = sb("x1", [P, NT, D])
        sq = sb("sq", [P, NT, D])
        small = sb("small", [P, 512])
        idx8 = sb("idx8", [P, NT, 8], dt.uint32)
        qt = sb("qt", [P, NP, N])
        big = sb("big", [P, 2 * INNER + NT * H * V0 + 2 * INNER])
        reg = sb("reg", [P, 12 * 512])
        kvb = sb("kvb", [P, NP, 2 * V0])
        pbd = sb("pbd", [P, NT, 2, NP, P])
        st = sb("st", [P, NC - 1, NP, P])
        cd = sb("cd", [P, NP, NC])
        v9 = sb("v9_s", [P, NT, NKV, V1])
        kr = sb("kr", [P, N])

        k_tok = big[:, 0:2 * INNER].rearrange("p (t f) -> p t f", t=NT)
        v_tok = big[:, 2 * INNER:2 * INNER + NT * H * V0].rearrange("p (t h v) -> p t h v", t=NT, v=V0)
        o_tok = big[:, 2 * INNER + NT * H * V0:].rearrange("p (t f) -> p t f", t=NT)
        oT = big[:, 0:2 * INNER].rearrange("p (a n) -> p a n", a=NP)
        a_tok = o_tok
        pT = big[:, 0:12 * 512].rearrange("p (n k) -> p n k", n=12)
        e_q = reg[:, 0:2048].rearrange("p (a n) -> p a n", a=NP)
        e_k = reg[:, 2048:4096].rearrange("p (t f) -> p t f", t=NT)
        qr = qt[:, 0:4, :]
        qs = qt[:, 4:8, :]
        krs = sq[:, :, :].rearrange("p t d -> p (t d)")
        rp = reg[:, 4096:6144].rearrange("p (a n) -> p a n", a=8)
        pp = reg[:, :].rearrange("p (n k) -> p n k", n=12)
        ao = reg[:, 0:256].rearrange("p (t d) -> p t d", t=NT)
        aT = reg[:, 256:512]
        g0 = gbuf[:, :].rearrange("p (s c n) -> p s c n", s=2, c=2)
        kd = reg[:, 0:2048].rearrange("p (t f) -> p t f", t=NT)
        at3 = reg[:, 0:2048].rearrange("p (t h c) -> p t h c", t=NT, h=H)
        el = reg[:, 2048:4096].rearrange("p (a n) -> p a n", a=NP)
        sqT = el
        ks = kd
        kT = reg[:, 4096:6144].rearrange("p (a n) -> p a n", a=NP)
        oT1 = kT
        g1 = reg[:, 0:1024].rearrange("p (c n) -> p c n", c=4)
        r1 = gbuf[:, :].rearrange("p (c n) -> p c n", c=4)
        rqT = sq[0:H, :, :].rearrange("p t d -> p (t d)")
        ohT = sq[0:E, :, :].rearrange("p t d -> p (t d)")
        bg_row = small[0:3, 0:3]

        psum = ctx.enter_context(nc.psum_tensor("psum", [P, 8, 512], f32))

        sems = {}

        def sem(name):
            if name not in sems:
                sems[name] = ctx.enter_context(nc.semaphore(name))
            return sems[name]

        for b in range(RING):
            sem(f"bank{b}_full"), sem(f"bank{b}_free")

        now = {}

        def segment(n, i):
            now.update(n=n, i=i, plan=PLANS[n], stages=SEGMENTS[n][0], count={})

        def rows_before(stage):
            return sum(times for stages, times in SEGMENTS[:now["n"]] if stage in stages)

        def row(stage):
            return now["i"] + rows_before(stage)

        def bank(use):
            return psum[:, now["plan"][use][0], :]

        def given(name, n=1, by=1):
            before = sum(times * in_body(stages, name) for stages, times in SEGMENTS[:now["n"]])
            return sem(name), now["i"] * (in_body(now["stages"], name) * by) + (before + n) * by

        def signals(name):
            now["count"][name] = now["count"].get(name, 0) + 1
            return sem(name), 1

        def chained(name):
            return given(name, now["count"][name])

        def bank_uses(use, more):
            b, n = now["plan"][use]
            return now["i"] * USES[now["n"]][b] + n + more

        def fills(use):
            return sem(f"bank{now['plan'][use][0]}_full"), 1

        def filled(use):
            return sem(f"bank{now['plan'][use][0]}_full"), bank_uses(use, 0)

        def frees(use):
            return sem(f"bank{now['plan'][use][0]}_free"), 1

        def emptied(use):
            return sem(f"bank{now['plan'][use][0]}_free"), bank_uses(use, 0)

        def read_out(use):
            return sem(f"bank{now['plan'][use][0]}_free"), bank_uses(use, 1)

        def checked():
            for name, n in now["count"].items():
                assert n == in_body(now["stages"], name), (now["stages"], name, n)

        def kd_b16(i):
            return reg[0:1, i * 512:(i + 1) * 512].bitcast(b16)

        blk = ctx.enter_context(nc.Block())
        NLOAD = [0]

        @blk.sync
        def _(sp):
            def load(dst, src):
                NLOAD[0] += 1
                sp.dma_start(dst, src).then_inc(sem("weights"), 16)

            load(wqkv0[:, :], A["wqkv0"])
            load(wrope[:, :, :], A["wrope"])
            load(ropec[:, :, :], A["ropec"])
            load(wv9[:, :], A["wv9"])
            load(wout0[:, :, :], A["wout0"])
            load(boutb[:, :], A["bout"].partition_broadcast(P))
            load(woT[:, :], A["woT"])
            load(gateT[:, :], A["gateT"])
            load(w13T[:, :, :], A["w13T"])
            load(w2T[:, :, :, :], A["w2T"])
            load(lqkvg[:, :], A["lqkvg"])
            load(lwo[:, :, :], A["lwo"])
            load(lw1[:, :], A["lw1"])
            load(lw2[:, :, :], A["lw2"])
            load(mg[:, :], A["mg"])
            load(mb2[:, :], A["mb2"])
            load(cols[:, :], A["cols"])
            load(bgb[:, :], A["bgm"].partition_broadcast(P))
            load(b2b[:, :], A["b2"].partition_broadcast(P))
            load(identb[:, :], A["identb"])
            load(cmask[:, :, :], A["cmask"])
            load(dmask[:, :, :], A["dmask"])
            load(ones3[:, :], A["ones3"])
            load(tri[:, :], A["tri"])
            load(strict[:, :], A["strict"])
            load(tri64[:, :], A["tri64"])
            load(ident[:, :], A["ident"])
            load(pairsel[:, :, :], A["pairsel"])
            load(headsel[:, :, :], A["headsel"])
            load(iota8[:, :], A["iota8"])
            load(big[0:1, 0:INNER], A["bg"])
            sp.wait_ge(sem("bg_split"), 1)
            for i in range(3):
                sp.dma_start(bg3[i:i + 1, :], kd_b16(i)).then_inc(sem("bg3_ready"), 16)
            sp.sem_inc(sem("stored"), 16)

            def body():
                if "A" in now["stages"]:
                    sp.wait_ge(*given("x_free"))
                    sp.dma_start(x[:, :, :], A["x"][row("A")].rearrange("(t p) d -> p t d", p=P)).then_inc(sem("x_ready"), 16)
                if "D" in now["stages"]:
                    for e in range(E):
                        sp.wait_ge(*given(f"ew{e % 2}_free", e // 2 + 1))
                        sp.dma_start(ew[:, e % 2, :], A["ew"][e]).then_inc(sem(f"ew{e % 2}_ready"), 16)
                    sp.wait_ge(*given("out_ready"))
                    sp.dma_start(out[row("D")].rearrange("(t p) d -> p t d", p=P), y2[:, :, :]).then_inc(sem("stored"), 16)

            for n, (stages, times) in enumerate(SEGMENTS):
                if times == 1:
                    segment(n, 0)
                    body()
                else:
                    with sp.Fori(0, times) as i:
                        segment(n, i)
                        body()
            sp.wait_ge(sem("stored"), 16 * (B + 1))

        @blk.gpsimd
        def _(g):
            g.memset(kvb[:, :, :], 0.0).then_inc(sem("zeros"), 1)
            g.memset(st[:, :, :, :], 0.0).then_inc(sem("zeros"), 1)
            g.memset(pbd[:, :, :, :, :], 0.0).then_inc(sem("zeros"), 1)
            g.memset(v9[:, :, :, :], 1.0).then_inc(sem("zeros"), 1)

        @blk.tensor
        def _(pe):
            mm = nc.tensor.matmul

            def tr(dst, src, idn=None):
                k = src.shape[0]
                return nc.tensor.transpose(dst, src, ident[0:k, 0:k])

            for b in range(RING):
                pe.sem_inc(sem(f"bank{b}_free"), 1)
            pe.wait_ge(sem("weights"), 16 * NLOAD[0])
            pe.wait_ge(sem("bg3_ready"), 48)
            pe.wait_ge(sem("zeros"), 4)
            def moe0(e):
                if "B" not in now["stages"]:
                    return
                if e < E:
                    for name, off in (("a", 0), ("b", F0)):
                        pe.wait_ge(*emptied(f"{name}{e}"))
                        for c in range(2):
                            last = mm(bank(f"{name}{e}")[:, c * N:(c + 1) * N], w13T[:, e, off + c * P:off + (c + 1) * P], hT[:, :], start=True, stop=True)
                        last.then_inc(*fills(f"{name}{e}"))
                if e:
                    pe.wait_ge(*read_out(f"b{e - 1}"))
                    pe.wait_ge(*emptied(f"y{e - 1}"))
                    for t in range(NT):
                        for c in range(2):
                            last = mm(bank(f"y{e - 1}")[:, t * P:(t + 1) * P], g0[:, (e - 1) % 2, c, t * P:(t + 1) * P], w2T[:, e - 1, c, :], start=(c == 0), stop=(c == 1))
                    last.then_inc(*fills(f"y{e - 1}"))

            def moe1(e):
                if "D" not in now["stages"]:
                    return
                if e < E:
                    pe.wait_ge(*given(f"ew{e % 2}_ready", e // 2 + 1, 16))
                    for j in range(2):
                        pe.wait_ge(*emptied(f"h{e}{j}"))
                        for a in range(2):
                            c = 2 * j + a
                            last = mm(bank(f"h{e}{j}")[:, a * N:(a + 1) * N], ew[:, e % 2, c * P:(c + 1) * P], x1T[:, :], start=True, stop=True)
                        last.then_inc(*fills(f"h{e}{j}"))
                if e:
                    pe.wait_ge(*read_out(f"h{e - 1}1"))
                    pe.wait_ge(*emptied(f"yy{e - 1}"))
                    for t in range(NT):
                        for c in range(4):
                            last = mm(bank(f"yy{e - 1}")[:, t * P:(t + 1) * P], r1[:, c, t * P:(t + 1) * P],
                                      ew[:, (e - 1) % 2, F1 + c * D:F1 + (c + 1) * D], start=(c == 0), stop=(c == 3))
                    last.then_inc(*fills(f"yy{e - 1}"))

            def attention0():
                moe1(0)
                pe.wait_ge(*given("xr_ready"))
                pe.wait_ge(*emptied("xT"))
                for t in range(NT):
                    tr(bank("xT")[:, t * P:(t + 1) * P], xn[:, t, :])
                for t in range(NT):
                    last = tr(bank("xT")[:, N + t * P:N + (t + 1) * P], xr[:, t, :])
                last.then_inc(*fills("xT"))
                moe1(1)
                pe.wait_ge(*read_out("xT"))
                xnT, h1T = xT[:, 0, :], xT[:, 1, :]
                for j in range(4):
                    pe.wait_ge(*emptied(f"q{j}"))
                    for a in range(2):
                        pr = 2 * j + a
                        last = mm(bank(f"q{j}")[:, a * N:(a + 1) * N], wqkv0[:, pr * P:(pr + 1) * P], xnT, start=True, stop=True)
                    last.then_inc(*fills(f"q{j}"))
                for name, off in (("k", INNER), ("v", 2 * INNER)):
                    for t in range(NT):
                        for c in range(2):
                            pe.wait_ge(*emptied(f"{name}{t}{c}"))
                            mm(bank(f"{name}{t}{c}"), xnT[:, t * P:(t + 1) * P],
                                    wqkv0[:, off + c * 512:off + (c + 1) * 512], start=True, stop=True).then_inc(*fills(f"{name}{t}{c}"))
                pe.wait_ge(*read_out("xT"))
                for name, w0 in (("rq", 0), ("rs", 4)):
                    for j in range(2):
                        pe.wait_ge(*emptied(f"{name}{j}"))
                        for a in range(2):
                            last = mm(bank(f"{name}{j}")[:, a * N:(a + 1) * N], wrope[:, w0 + 2 * j + a, :], h1T, start=True, stop=True)
                        last.then_inc(*fills(f"{name}{j}"))
                pe.wait_ge(*emptied("rk"))
                for a in range(2):
                    last = mm(bank("rk")[:, a * N:(a + 1) * N], wrope[:, 8 + a, :], h1T, start=True, stop=True)
                last.then_inc(*fills("rk"))
                pe.wait_ge(*emptied("v9"))
                for t in range(NT):
                    last = mm(bank("v9")[:, t * 32:(t + 1) * 32], h1T[:, t * P:(t + 1) * P], wv9[:, :], start=True, stop=True)
                last.then_inc(*fills("v9"))
                moe1(2)
                pe.wait_ge(*given("k0_ready"))
                pe.wait_ge(*read_out("v11"))
                for j in range(4):
                    pe.wait_ge(*emptied(f"kv{j}"))
                    for a in range(2):
                        pr = 2 * j + a
                        for t in range(NT):
                            last = mm(bank(f"kv{j}")[:, a * N:a * N + 2 * V0], k_tok[:, t, pr * P:(pr + 1) * P],
                                      v_tok[:, t, 2 * pr:2 * pr + 2, :], start=(t == 0), stop=(t == NT - 1))
                    last.then_inc(*fills(f"kv{j}"))
                moe1(3)
                pe.wait_ge(*given("q0_ready"))
                for t in range(NT):
                    for j in range(4):
                        if t == 0:
                            pe.wait_ge(*read_out(f"kv{j}"))
                        pe.wait_ge(*emptied(f"num{t}{j}"))
                        for a in range(2):
                            pr = 2 * j + a
                            last = mm(bank(f"num{t}{j}")[:, a * N:a * N + 2 * V0], qt[:, pr, t * P:(t + 1) * P], kvb[:, pr, :], start=True, stop=True)
                        last.then_inc(*fills(f"num{t}{j}"))
                moe1(4)
                for t in range(NT):
                    pe.wait_ge(*read_out(f"num{t}3"))
                    for c in range(2):
                        pe.wait_ge(*emptied(f"oT{t}{c}"))
                        for a in range(4):
                            last = tr(bank(f"oT{t}{c}")[:, a * P:(a + 1) * P], o_tok[:, t, (4 * c + a) * P:(4 * c + a + 1) * P])
                        last.then_inc(*fills(f"oT{t}{c}"))
                pe.wait_ge(*emptied("s0"))
                pe.wait_ge(*read_out("oT11"))
                for t in range(NT):
                    for pr in range(NP):
                        last = mm(bank("s0")[:, t * P:(t + 1) * P], oT[:, pr, t * P:(t + 1) * P], wout0[:, pr, :], start=(pr == 0), stop=(pr == NP - 1))
                last.then_inc(*fills("s0"))
                pe.wait_ge(*given("rope_ready"))
                for n in range(12):
                    use = f"sc{n}"
                    pe.wait_ge(*emptied(use))
                    if n < 4:
                        mm(bank(use), identb[:, :], cmask[:, 0, :], start=True, stop=False)
                        for r in range(GR):
                            p0 = 32 * n
                            last = mm(bank(use)[:, r * P:(r + 1) * P], qr[p0:p0 + HD, r, 0:P], kr[p0:p0 + HD, 0:P], start=False, stop=(r == GR - 1))
                    else:
                        grp, half = (n - 4) // 2, (n - 4) % 2
                        p0 = 32 * grp
                        mm(bank(use), identb[:, :], cmask[:, 1, :], start=True, stop=False)
                        for a in range(2):
                            last = mm(bank(use)[:, a * N:(a + 1) * N], qr[p0:p0 + HD, 2 * half + a, P:N], kr[p0:p0 + HD, :], start=False, stop=(a == 1))
                    last.then_inc(*fills(use))
                    if n == 5:
                        moe1(5)
                moe1(6)
                for n in range(12):
                    pe.wait_ge(*given("p_ready", n + 1))
                    pe.wait_ge(*emptied(f"pT{n}"))
                    for a in range(4):
                        last = tr(bank(f"pT{n}")[:, a * P:(a + 1) * P], pp[:, n, a * P:(a + 1) * P])
                    last.then_inc(*fills(f"pT{n}"))
                    if n == 5:
                        moe1(7)
                moe1(8)
                pe.wait_ge(*emptied("pv"))
                pe.wait_ge(*read_out("pT10"))
                pe.wait_ge(*read_out("pT11"))
                for hd in range(NHF):
                    grp, r = hd // GR, hd % GR
                    last = mm(bank("pv")[:, hd * V1:(hd + 1) * V1], pT[:, grp, r * P:(r + 1) * P], v9[:, 0, grp, :], start=True, stop=True)
                for hd in range(NHF):
                    grp, r = hd // GR, hd % GR
                    n, a = 4 + 2 * grp + r // 2, r % 2
                    for kt in range(2):
                        last = mm(bank("pv")[:, (NHF + hd) * V1:(NHF + hd + 1) * V1], pT[:, n, (2 * a + kt) * P:(2 * a + kt + 1) * P],
                                  v9[:, kt, grp, :], start=(kt == 0), stop=(kt == 1))
                last.then_inc(*fills("pv"))
                pe.wait_ge(*read_out("pv"))
                pe.wait_ge(*emptied("aT"))
                for t in range(NT):
                    last = tr(bank("aT")[:, t * P:(t + 1) * P], ao[:, t, :])
                last.then_inc(*fills("aT"))
                pe.wait_ge(*read_out("aT"))
                pe.wait_ge(*emptied("wo"))
                for t in range(NT):
                    last = mm(bank("wo")[:, t * P:(t + 1) * P], aT[:, t * P:(t + 1) * P], woT[:, :], start=True, stop=True)
                last.then_inc(*fills("wo"))
                pe.wait_ge(*given("h2_ready"))
                pe.wait_ge(*emptied("hT"))
                for t in range(NT):
                    last = tr(bank("hT")[:, t * P:(t + 1) * P], sq[:, t, :])
                last.then_inc(*fills("hT"))
                pe.wait_ge(*read_out("hT"))
                pe.wait_ge(*emptied("gate"))
                for t in range(NT):
                    last = mm(bank("gate")[:, t * E:(t + 1) * E], hT[:, t * P:(t + 1) * P], gateT[:, :], start=True, stop=True)
                last.then_inc(*fills("gate"))

            def attention1():
                moe0(0)
                moe0(1)
                pe.wait_ge(*given("z1_ready"))
                pe.wait_ge(*emptied("zT"))
                for t in range(NT):
                    tr(bank("zT")[:, t * P:(t + 1) * P], xn[:, t, :])
                for t in range(NT):
                    last = tr(bank("zT")[:, N + t * P:N + (t + 1) * P], xr[:, t, :])
                last.then_inc(*fills("zT"))
                moe0(2)
                pe.wait_ge(*read_out("zT"))
                zT = xT[:, 1, :]
                for name, off in (("lq", 0), ("lk", INNER)):
                    for j in range(4):
                        pe.wait_ge(*emptied(f"{name}{j}"))
                        for a in range(2):
                            pr = 2 * j + a
                            last = mm(bank(f"{name}{j}")[:, a * N:(a + 1) * N], lqkvg[:, off + pr * P:off + (pr + 1) * P], zT, start=True, stop=True)
                        last.then_inc(*fills(f"{name}{j}"))
                    if name == "lq":
                        pe.wait_ge(*read_out("lq3"))
                        pe.wait_ge(*emptied("ssq"))
                        for t in range(NT):
                            for pr in range(NP):
                                last = mm(bank("ssq")[:, t * H:(t + 1) * H], sqT[:, pr, t * P:(t + 1) * P], pairsel[:, pr, :], start=(pr == 0), stop=(pr == NP - 1))
                        last.then_inc(*fills("ssq"))
                for name, off in (("tk", INNER), ("z", 3 * INNER)):
                    for t in range(NT):
                        for c in range(2):
                            use = f"{name}{t}{c}"
                            pe.wait_ge(*emptied(use))
                            if name == "z":
                                mm(bank(use), ones3[:, :], bg3[:, c * 512:(c + 1) * 512], start=True, stop=False)
                            mm(bank(use), zT[:, t * P:(t + 1) * P], lqkvg[:, off + c * 512:off + (c + 1) * 512],
                                    start=(name != "z"), stop=True).then_inc(*fills(use))
                moe0(3)
                pe.wait_ge(*read_out("lk3"))
                pe.wait_ge(*given("rq_ready"))
                pe.wait_ge(*emptied("rqT"))
                for t in range(NT):
                    last = tr(bank("rqT")[0:H, t * P:(t + 1) * P], small[:, 64 + t * H:64 + (t + 1) * H])
                last.then_inc(*fills("rqT"))
                pe.wait_ge(*read_out("rqT"))
                for j in range(4):
                    pe.wait_ge(*emptied(f"rep{j}"))
                    for a in range(2):
                        last = mm(bank(f"rep{j}")[:, a * N:(a + 1) * N], headsel[:, 2 * j + a, :], rqT[:, :], start=True, stop=True)
                    last.then_inc(*fills(f"rep{j}"))
                for t in range(NT):
                    for c in range(2):
                        pe.wait_ge(*emptied(f"tv{t}{c}"))
                        mm(bank(f"tv{t}{c}"), zT[:, t * P:(t + 1) * P], lqkvg[:, 2 * INNER + c * 512:2 * INNER + (c + 1) * 512], start=True, stop=True).then_inc(*fills(f"tv{t}{c}"))
                moe0(4)
                pe.wait_ge(*read_out("rep3"))
                for t in range(NT):
                    pe.wait_ge(*given("at3_ready", t + 1))
                    for c in range(2):
                        pe.wait_ge(*emptied(f"d{t}{c}"))
                        mm(bank(f"d{t}{c}"), identb[:, :], dmask[:, :, :], start=True, stop=False)
                        mm(bank(f"d{t}{c}"), strict[:, :], at3[:, t, c::2, :], start=False, stop=True).then_inc(*fills(f"d{t}{c}"))
                for t in range(NT):
                    for c in range(2):
                        free_at = emptied(f"s{t}{c}")[1]
                        if SEGMENTS[now["n"]][1] > 1:
                            free_at = pe.snap(free_at)
                        pe.wait_ge(sem("weights"), 16)
                        pe.wait_ge(emptied(f"s{t}{c}")[0], free_at)
                        for ch in range(2):
                            for pr in range(NP):
                                cc = t * P + ch * CH
                                last = mm(bank(f"s{t}{c}")[ch * CH:(ch + 1) * CH, pr * CH:(pr + 1) * CH],
                                          kT[c * DH:(c + 1) * DH, pr, cc:cc + CH], qt[c * DH:(c + 1) * DH, pr, cc:cc + CH], start=True, stop=True)
                        last.then_inc(*fills(f"s{t}{c}"))
                for t in range(NT):
                    for c in range(2):
                        pe.wait_ge(*emptied(f"te{t}{c}"))
                        mm(bank(f"te{t}{c}"), strict[:, :], a_tok[:, t, c * 512:(c + 1) * 512], start=True, stop=True).then_inc(*fills(f"te{t}{c}"))
                for j in range(4):
                    pe.wait_ge(*emptied(f"la{j}"))
                    for a in range(2):
                        for t in range(NT):
                            last = mm(bank(f"la{j}")[:, a * N + t * P:a * N + (t + 1) * P], a_tok[:, t, (2 * j + a) * P:(2 * j + a + 1) * P], tri[:, :], start=True, stop=True)
                    last.then_inc(*fills(f"la{j}"))
                moe0(5)
                pe.wait_ge(*given("kd_ready"))
                pe.wait_ge(*read_out("tv11"))
                for n in range(NC - 1):
                    t, r0 = n // 2, (n % 2) * CH
                    for hh in range(2):
                        pe.wait_ge(*emptied(f"st{n}{hh}"))
                        for a in range(4):
                            pr = 4 * hh + a
                            last = mm(bank(f"st{n}{hh}")[:, a * P:(a + 1) * P], kd[r0:r0 + CH, t, pr * P:(pr + 1) * P],
                                      v_tok[r0:r0 + CH, t, 2 * pr:2 * pr + 2, 0:DH], start=True, stop=True)
                        last.then_inc(*fills(f"st{n}{hh}"))
                moe0(6)
                pe.wait_ge(*read_out("s11"))
                pe.wait_ge(*given("qd_ready"))
                pe.wait_ge(*read_out("st21"))
                for j in range(4):
                    pe.wait_ge(*emptied(f"o{j}"))
                    for a in range(2):
                        pr = 2 * j + a
                        for t in range(NT):
                            for c in range(2):
                                mm(bank(f"o{j}")[c * DH:(c + 1) * DH, a * N + t * P:a * N + (t + 1) * P],
                                   v_tok[:, t, 2 * pr + c, 0:DH], pbd[:, t, c, pr, :], start=True, stop=False)
                            for n in range(max(1, 2 * t), 2 * t + 2):
                                last = mm(bank(f"o{j}")[:, a * N + n * CH:a * N + (n + 1) * CH], st[:, n - 1, pr, :],
                                          el[:, pr, n * CH:(n + 1) * CH], start=False, stop=(n == 2 * t + 1))
                    last.then_inc(*fills(f"o{j}"))
                pe.wait_ge(*read_out("o3"))
                pe.wait_ge(*emptied("wo1"))
                for t in range(NT):
                    for pr in range(NP):
                        last = mm(bank("wo1")[:, t * P:(t + 1) * P], oT1[:, pr, t * P:(t + 1) * P], lwo[:, pr, :], start=(pr == 0), stop=(pr == NP - 1))
                last.then_inc(*fills("wo1"))
                pe.wait_ge(*emptied("gate1"))
                for t in range(NT):
                    last = mm(bank("gate1")[:, t * E:(t + 1) * E], x1T[:, t * P:(t + 1) * P], mg[:, :], start=True, stop=True)
                last.then_inc(*fills("gate1"))
                moe0(7)
                pe.wait_ge(*given("z2_ready"))
                pe.wait_ge(*emptied("z2T"))
                for t in range(NT):
                    last = tr(bank("z2T")[:, t * P:(t + 1) * P], xr[:, t, :])
                last.then_inc(*fills("z2T"))
                pe.wait_ge(*given("oh_ready"))
                pe.wait_ge(*emptied("ohT"))
                for t in range(NT):
                    last = tr(bank("ohT")[0:E, t * P:(t + 1) * P], small[:, 256 + t * E:256 + (t + 1) * E])
                last.then_inc(*fills("ohT"))
                pe.wait_ge(*read_out("z2T"))
                for j in range(2):
                    pe.wait_ge(*emptied(f"f{j}"))
                    for a in range(2):
                        last = mm(bank(f"f{j}")[:, a * N:(a + 1) * N], lw1[:, (2 * j + a) * P:(2 * j + a + 1) * P], xT[:, 1, :], start=True, stop=True)
                    last.then_inc(*fills(f"f{j}"))
                moe0(8)
                pe.wait_ge(*read_out("f1"))
                pe.wait_ge(*emptied("w2"))
                for t in range(NT):
                    for c in range(4):
                        last = mm(bank("w2")[:, t * P:(t + 1) * P], g1[:, c, t * P:(t + 1) * P], lw2[:, c, :], start=(c == 0), stop=(c == 3))
                last.then_inc(*fills("w2"))
                pe.wait_ge(*read_out("ohT"))
                pe.wait_ge(*emptied("b2y"))
                for t in range(NT):
                    last = mm(bank("b2y")[:, t * P:(t + 1) * P], ohT[:, t * P:(t + 1) * P], mb2[:, :], start=True, stop=True)
                last.then_inc(*fills("b2y"))

            def body():
                if "A" in now["stages"]:
                    attention0()
                else:
                    for e in range(E + 1):
                        moe1(e)
                if "C" in now["stages"]:
                    attention1()
                else:
                    for e in range(E + 1):
                        moe0(e)

            for n, (stages, times) in enumerate(SEGMENTS):
                if times == 1:
                    segment(n, 0)
                    body()
                else:
                    with pe.Fori(0, times) as i:
                        segment(n, i)
                        body()

        @blk.scalar
        def _(act):
            af = nc.scalar.activation

            def rstd(name, src, dst, scale, bias):
                act.wait_ge(*given(f"{name}_stat"))
                af(dst, src, ACT.Ln, scale=scale, bias=bias).then_inc(*signals("act_chain"))
                act.wait_ge(*chained("act_chain"))
                af(dst, dst, ACT.Exp, scale=-0.5).then_inc(*signals(f"{name}_rstd"))

            act.wait_ge(sem("weights"), 16 * NLOAD[0])
            act.preload_act_table_set("natural_log_exp_and_others")
            eps = cols[:, 42:43]

            def moe0(e):
                if "B" not in now["stages"]:
                    return
                if e < E:
                    act.wait_ge(*filled(f"a{e}"))
                    if e >= 2:
                        act.wait_ge(*filled(f"y{e - 2}"))
                    af(g0[:, e % 2, :, :], bank(f"a{e}").rearrange("p (c n) -> p c n", c=2), ACT.Silu).then_inc(*frees(f"a{e}"))
                else:
                    act.wait_ge(*read_out(f"y{E - 1}"))
                    af(sg[:, :, :], acc0[:, :, :], ACT.Silu).then_inc(*signals("sg_ready"))
                act.preload_act_table_set("natural_log_exp_and_others")

            def moe1(e):
                if "D" not in now["stages"]:
                    return
                if e < E:
                    if e:
                        act.wait_ge(*filled(f"yy{e - 1}"))
                    for j in range(2):
                        act.wait_ge(*filled(f"h{e}{j}"))
                        for a in range(2):
                            c = 2 * j + a
                            ins = af(r1[:, c, :], bank(f"h{e}{j}")[:, a * N:(a + 1) * N], ACT.Relu,
                                     bias=cols[:, 8 + 4 * e + c:9 + 4 * e + c])
                        ins.then_inc(*frees(f"h{e}{j}"))
                else:
                    act.wait_ge(*read_out(f"yy{E - 1}"))
                    af(sg[:, :, :], acc1[:, :, :], ACT.Silu).then_inc(*signals("sg1_ready"))
                    act.preload_act_table_set("natural_log_exp_and_others")

            def attention0():
                moe1(0)
                rstd("ln0", small[:, 1:4:2], small[:, 4:6], 1.0, eps)
                rstd("rms0", small[:, 6:8], small[:, 8:10], 1.0 / D, eps)
                moe1(1)
                for j in range(4):
                    act.wait_ge(*filled(f"q{j}"))
                    af(e_q[:, 2 * j:2 * j + 2, :], bank(f"q{j}").rearrange("p (a n) -> p a n", a=2), ACT.Exp).then_inc(*signals("eq"))
                    af(qt[:, 2 * j:2 * j + 2, :], bank(f"q{j}").rearrange("p (a n) -> p a n", a=2), ACT.Relu).then_inc(*frees(f"q{j}"))
                for t in range(NT):
                    for c in range(2):
                        act.wait_ge(*filled(f"k{t}{c}"))
                        af(e_k[:, t, c * 512:(c + 1) * 512], bank(f"k{t}{c}"), ACT.Exp).then_inc(*signals("ek"))
                        af(k_tok[:, t, c * 512:(c + 1) * 512], bank(f"k{t}{c}"), ACT.Relu).then_inc(*frees(f"k{t}{c}"))
                moe1(2)
                moe1(3)
                moe1(4)
                for t in range(NT):
                    for c in range(2):
                        act.wait_ge(*filled(f"oT{t}{c}"))
                        src = bank(f"oT{t}{c}").rearrange("p (a n) -> p a n", a=4)
                        ins = af(oT[:, 4 * c:4 * c + 4, t * P:(t + 1) * P], src, ACT.Copy)
                        ins.then_inc(*frees(f"oT{t}{c}"))
                for n in range(12):
                    act.wait_ge(*read_out(f"sc{n}"))
                    af(pp[:, n, :], pp[:, n, :], ACT.Exp, scale=float(HD) ** -0.5).then_inc(*signals("p_ready"))
                    if n == 5:
                        moe1(5)
                moe1(6)
                for n in range(0, 12, 2):
                    act.wait_ge(*filled(f"pT{n}"))
                    af(pT[:, n, :], bank(f"pT{n}"), ACT.Copy).then_inc(*frees(f"pT{n}"))
                    if n == 4:
                        moe1(7)
                moe1(8)
                act.wait_ge(*filled("aT"))
                af(aT[:, :], bank("aT")[:, 0:N], ACT.Copy).then_inc(*frees("aT"))
                for t in range(NT):
                    act.wait_ge(*read_out("wo"))
                    af(sq[:, t, :], x2[:, t, :], ACT.Square, accum_out=small[:, 10 + t:11 + t]).then_inc(*signals("act_chain"))
                    act.wait_ge(*chained("act_chain"))
                af(small[:, 12:14], small[:, 10:12], ACT.Ln, scale=1.0 / D, bias=eps).then_inc(*signals("act_chain"))
                act.wait_ge(*chained("act_chain"))
                af(small[:, 12:14], small[:, 12:14], ACT.Exp, scale=-0.5).then_inc(*signals("rms2_rstd"))
                act.wait_ge(*filled("hT"))
                af(hT[:, :], bank("hT")[:, 0:N], ACT.Copy, scale=cols[:, 1:2]).then_inc(*frees("hT"))
                act.wait_ge(*given("lg_ready"))
                af(small[:, 32:48], small[:, 32:48], ACT.Exp).then_inc(*signals("eg_ready"))

            def attention1():
                moe0(0)
                moe0(1)
                rstd("ln1", small[:, 1:4:2], small[:, 4:6], 1.0, eps)
                rstd("ln1b", small[:, 1:4:2], small[:, 4:6], 1.0, eps)
                moe0(2)
                for j in range(4):
                    act.wait_ge(*filled(f"lq{j}"))
                    src = bank(f"lq{j}").rearrange("p (a n) -> p a n", a=2)
                    af(sqT[:, 2 * j:2 * j + 2, :], src, ACT.Square).then_inc(*signals("sq_done"))
                    af(qt[:, 2 * j:2 * j + 2, :], src, ACT.Copy).then_inc(*frees(f"lq{j}"))
                for j in range(4):
                    act.wait_ge(*filled(f"lk{j}"))
                    af(kT[:, 2 * j:2 * j + 2, :], bank(f"lk{j}").rearrange("p (a n) -> p a n", a=2), ACT.Copy).then_inc(*frees(f"lk{j}"))
                act.wait_ge(*read_out("ssq"))
                af(small[:, 64:96], small[:, 64:96], ACT.Ln, scale=1e6).then_inc(*signals("act_chain"))
                act.wait_ge(*chained("act_chain"))
                af(small[:, 64:96], small[:, 64:96], ACT.Exp, scale=-0.5).then_inc(*signals("rq_ready"))
                for t in range(NT):
                    for c in range(2):
                        act.wait_ge(*filled(f"tk{t}{c}"))
                        af(ks[:, t, c * 512:(c + 1) * 512], bank(f"tk{t}{c}"), ACT.Square).then_inc(*signals("ks"))
                for t in range(NT):
                    for c in range(2):
                        act.wait_ge(*filled(f"z{t}{c}"))
                        af(a_tok[:, t, c * 512:(c + 1) * 512], bank(f"z{t}{c}"), ACT.Exp, scale=-1.0).then_inc(*frees(f"z{t}{c}"))
                moe0(3)
                act.wait_ge(*given("ssk_ready"))
                af(small[:, 96:128], small[:, 96:128], ACT.Ln, scale=1e6).then_inc(*signals("act_chain"))
                act.wait_ge(*chained("act_chain"))
                af(small[:, 96:128], small[:, 96:128], ACT.Exp, scale=-0.5).then_inc(*signals("rk_ready"))
                for t in range(NT):
                    act.wait_ge(*given("ez_clamped", t + 1))
                    af(a_tok[:, t, :], a_tok[:, t, :], ACT.Ln, bias=1.0).then_inc(*signals("a_ready"))
                moe0(4)
                for t in range(NT):
                    for c in range(2):
                        act.wait_ge(*filled(f"d{t}{c}"))
                        for ch in range(2):
                            rows = slice(ch * CH, (ch + 1) * CH)
                            src = bank(f"d{t}{c}")[rows, :].rearrange("p (a n) -> p a n", a=NP)
                            ins = af(pbd[rows, t, c, :, ch * CH:(ch + 1) * CH], src, ACT.Exp, scale=-1.0 / DH)
                            if ch == 0:
                                ins.then_inc(*signals("dec_half"))
                        ins.then_inc(*frees(f"d{t}{c}"))
                for t in range(NT):
                    for c in range(2):
                        act.wait_ge(*filled(f"te{t}{c}"))
                        af(kd[:, t, c * 512:(c + 1) * 512], bank(f"te{t}{c}"), ACT.Exp, scale=-1.0).then_inc(*frees(f"te{t}{c}"))
                for j in range(4):
                    act.wait_ge(*filled(f"la{j}"))
                    af(el[:, 2 * j:2 * j + 2, :], bank(f"la{j}").rearrange("p (a n) -> p a n", a=2), ACT.Exp, scale=-1.0).then_inc(*frees(f"la{j}"))
                moe0(5)
                moe0(6)
                for j in range(4):
                    act.wait_ge(*filled(f"o{j}"))
                    af(oT1[:, 2 * j:2 * j + 2, :], bank(f"o{j}").rearrange("p (a n) -> p a n", a=2), ACT.Copy).then_inc(*frees(f"o{j}"))
                moe0(7)
                rstd("ln2", small[:, 1:4:2], small[:, 4:6], 1.0, eps)
                for j in range(2):
                    act.wait_ge(*filled(f"f{j}"))
                    for a in range(2):
                        c = 2 * j + a
                        ins = af(g1[:, c, :], bank(f"f{j}")[:, a * N:(a + 1) * N], ACT.Gelu, bias=cols[:, 4 + c:5 + c])
                        if a == 0:
                            ins.then_inc(*signals("gelu_half"))
                    ins.then_inc(*frees(f"f{j}"))
                act.preload_act_table_set("natural_log_exp_and_others")
                moe0(8)

            def body():
                if "A" in now["stages"]:
                    attention0()
                else:
                    for e in range(E + 1):
                        moe1(e)
                if "C" in now["stages"]:
                    attention1()
                else:
                    for e in range(E + 1):
                        moe0(e)
                checked()

            for n, (stages, times) in enumerate(SEGMENTS):
                if times == 1:
                    segment(n, 0)
                    body()
                else:
                    with act.Fori(0, times) as i:
                        segment(n, i)
                        body()

        @blk.vector
        def _(dve):
            v = nc.vector

            def carry():
                v.memset(small[:, 511:512], 0.0)

            def stats(src, name):
                for t in range(NT):
                    v.bn_stats(small[:, 16 + 6 * t:22 + 6 * t], src[:, t, :]).then_inc(*signals("dve_chain"))
                    dve.wait_ge(*chained("dve_chain"))
                    if t == NT - 1:
                        carry()
                for t in range(NT):
                    ins = v.bn_aggr(small[:, 2 * t:2 * t + 2], small[:, 16 + 6 * t:22 + 6 * t])
                ins.then_inc(*signals(f"{name}_stat"))
                dve.wait_ge(*given(f"{name}_stat"))

            def normed(dst, src, name, ready=None):
                stats(src, name)
                dve.wait_ge(*given(f"{name}_rstd"))
                for t in range(NT):
                    ins = v.tensor_scalar(dst[:, t, :], src[:, t, :], small[:, 2 * t:2 * t + 1], small[:, 4 + t:5 + t], ALU.subtract, ALU.mult)
                    if t == NT - 1 and ready:
                        ins.then_inc(*signals(ready))
                    else:
                        ins.then_inc(*signals("dve_chain"))
                        dve.wait_ge(*chained("dve_chain"))

            def tok(ap):
                return ap.rearrange("p (t d) -> p t d", t=NT)

            dve.wait_ge(sem("weights"), 16 * NLOAD[0])
            ch0 = [0]

            def step(ins):
                ch0[0] += 1
                ins.then_inc(sem("setup_chain"), 1)
                dve.wait_ge(sem("setup_chain"), ch0[0])

            bg_whole, rest = big[0:1, 0:INNER], big[0:1, INNER:2 * INNER]
            step(v.tensor_copy(kd_b16(0), bg_whole))
            step(v.tensor_tensor(rest, bg_whole, kd_b16(0), ALU.subtract))
            step(v.tensor_copy(kd_b16(1), rest))
            step(v.tensor_tensor(rest, rest, kd_b16(1), ALU.subtract))
            v.tensor_copy(kd_b16(2), rest).then_inc(sem("bg_split"), 1)
            
            dve.wait_ge(sem("bg3_ready"), 48)
            dve.wait_ge(sem("zeros"), 4)
            dve.sem_inc(sem("x_free"), 1)
            dve.sem_inc(sem("ew0_free"), 1)
            dve.sem_inc(sem("ew1_free"), 1)
            lg = small[:, 160:176].rearrange("p (t e) -> p t e", t=NT)
            m8 = small[:, 176:192].rearrange("p (t e) -> p t e", t=NT)
            idf = small[:, 192:208].rearrange("p (t e) -> p t e", t=NT)
            io = iota8[:, :].rearrange("p (o e) -> p o e", o=1).to_broadcast([P, NT, E])
            gw = small[:, 240:256].rearrange("p (t e) -> p t e", t=NT)
            oh1 = small[:, 256:272].rearrange("p (t e) -> p t e", t=NT)

            def moe0(e):
                if "B" not in now["stages"]:
                    return
                if e < E:
                    dve.wait_ge(*filled(f"b{e}"))
                    dve.wait_ge(*read_out(f"a{e}"))
                    gs = g0[:, e % 2, :, :]
                    v.tensor_tensor(gs, gs, bank(f"b{e}").rearrange("p (c n) -> p c n", c=2), ALU.mult).then_inc(*frees(f"b{e}"))
                if e:
                    dve.wait_ge(*filled(f"y{e - 1}"))
                    for t in range(NT):
                        ins = v.scalar_tensor_tensor(out=acc0[:, t, :], in0=bank(f"y{e - 1}")[:, t * P:(t + 1) * P], scalar=gw[:, t, e - 1:e],
                                                     in1=(x2 if e == 1 else acc0)[:, t, :], op0=ALU.mult, op1=ALU.add)
                        if t == 0:
                            ins.then_inc(*signals("dve_chain"))
                            dve.wait_ge(*chained("dve_chain"))
                    ins.then_inc(*frees(f"y{e - 1}"))
                    dve.wait_ge(*read_out(f"y{e - 1}"))
                if e == E:
                    dve.wait_ge(*given("sg_ready"))
                    v.tensor_tensor(x1[:, :, :], s0[:, :, :], sg[:, :, :], ALU.mult).then_inc(*signals("dve_chain"))
                    dve.wait_ge(*chained("dve_chain"))
                    v.tensor_tensor(x1[:, :, :], x1[:, :, :], x_keep[:, :, :], ALU.add).then_inc(*signals("dve_chain"))
                    dve.wait_ge(*chained("dve_chain"))

            def moe1(e):
                if "D" not in now["stages"]:
                    return
                if e:
                    dve.wait_ge(*filled(f"yy{e - 1}"))
                    for t in range(NT):
                        ins = v.scalar_tensor_tensor(out=acc1[:, t, :], in0=bank(f"yy{e - 1}")[:, t * P:(t + 1) * P], scalar=oh1[:, t, e - 1:e],
                                                     in1=acc1[:, t, :], op0=ALU.mult, op1=ALU.add)
                        if t == 0:
                            ins.then_inc(*signals(f"ew{(e - 1) % 2}_free"))
                    ins.then_inc(*frees(f"yy{e - 1}"))
                    dve.wait_ge(*read_out(f"yy{e - 1}"))
                if e == E:
                    dve.wait_ge(*given("sg1_ready"))
                    v.tensor_tensor(y2[:, :, :], y2[:, :, :], sg[:, :, :], ALU.mult).then_inc(*signals("dve_chain"))
                    dve.wait_ge(*chained("dve_chain"))
                    v.tensor_tensor(y2[:, :, :], y2[:, :, :], x1_keep[:, :, :], ALU.add).then_inc(*signals("out_ready"))

            def attention0():
                moe1(0)
                dve.wait_ge(*given("x_ready", 1, 16))
                normed(xn, x, "ln0")
                v.tensor_copy(x_keep[:, :, :], x[:, :, :]).then_inc(*signals("x_free"))
                for t in range(NT):
                    v.scalar_tensor_tensor(out=xr[:, t, :], in0=xn[:, t, :], scalar=1.0, in1=xn[:, t, :], op0=ALU.mult, op1=ALU.mult).then_inc(*signals("dve_chain"))
                    dve.wait_ge(*chained("dve_chain"))
                v.tensor_reduce(small[:, 6:8], xr[:, :, :], AX.X, ALU.add).then_inc(*signals("rms0_stat"))
                dve.wait_ge(*given("rms0_rstd"))
                for t in range(NT):
                    ins = v.tensor_scalar(xr[:, t, :], xn[:, t, :], small[:, 8 + t:9 + t], None, ALU.mult)
                    if t == 0:
                        ins.then_inc(*signals("dve_chain"))
                        dve.wait_ge(*chained("dve_chain"))
                ins.then_inc(*signals("xr_ready"))
                dve.wait_ge(*filled("xT"))
                v.tensor_copy(xT[:, 0, :], bank("xT")[:, 0:N]).then_inc(*signals("xT_ready"))
                v.tensor_scalar(xT[:, 1, :], bank("xT")[:, N:2 * N], cols[:, 0:1], None, ALU.mult).then_inc(*frees("xT"))
                v.memset(v_tok[:, :, :, DH:V0], 1.0).then_inc(*signals("ones_ready"))
                moe1(1)
                for j in range(4):
                    dve.wait_ge(*read_out(f"q{j}"))
                    s = slice(2 * j, 2 * j + 2)
                    ins = v.scalar_tensor_tensor(out=qt[:, s, :], in0=e_q[:, s, :], scalar=1.0, in1=qt[:, s, :], op0=ALU.min, op1=ALU.add)
                    ins.then_inc(*signals("q0_ready" if j == 3 else "q0_part"))
                for t in range(NT):
                    for c in range(2):
                        dve.wait_ge(*read_out(f"k{t}{c}"))
                        s = slice(c * 512, (c + 1) * 512)
                        ins = v.scalar_tensor_tensor(out=k_tok[:, t, s], in0=e_k[:, t, s], scalar=1.0, in1=k_tok[:, t, s], op0=ALU.min, op1=ALU.add)
                        ins.then_inc(*signals("k0_ready" if 2 * t + c == 3 else "k0_part"))
                for t in range(NT):
                    for c in range(2):
                        dve.wait_ge(*filled(f"v{t}{c}"))
                        v.tensor_copy(v_tok[:, t, 8 * c:8 * c + 8, 0:DH], bank(f"v{t}{c}").rearrange("p (h d) -> p h d", d=DH)).then_inc(*frees(f"v{t}{c}"))
                for j in range(2):
                    dve.wait_ge(*filled(f"rq{j}"))
                    cb = ropec[:, 0:1, :].to_broadcast([P, 2, N])
                    v.tensor_tensor(rp[:, 2 * j:2 * j + 2, :], bank(f"rq{j}").rearrange("p (a n) -> p a n", a=2), cb, ALU.mult).then_inc(*frees(f"rq{j}"))
                for j in range(2):
                    dve.wait_ge(*filled(f"rs{j}"))
                    sbc = ropec[:, 1:2, :].to_broadcast([P, 2, N])
                    v.tensor_tensor(rp[:, 4 + 2 * j:6 + 2 * j, :], bank(f"rs{j}").rearrange("p (a n) -> p a n", a=2), sbc, ALU.mult).then_inc(*frees(f"rs{j}"))
                dve.wait_ge(*filled("rk"))
                v.tensor_tensor(kr[:, :], bank("rk")[:, 0:N], ropec[:, 0, :], ALU.mult).then_inc(*signals("dve_chain"))
                dve.wait_ge(*chained("dve_chain"))
                v.tensor_tensor(krs, bank("rk")[:, N:2 * N], ropec[:, 1, :], ALU.mult).then_inc(*frees("rk"))
                dve.wait_ge(*filled("v9"))
                v.tensor_copy(v9[:, :, :, 0:HD], bank("v9")[:, 0:64].rearrange("p (t g d) -> p t g d", t=NT, g=NKV)).then_inc(*frees("v9"))
                dve.wait_ge(*read_out("rk"))
                v.tensor_tensor(kr[:, :], kr[:, :], krs, ALU.add).then_inc(*signals("dve_chain"))
                dve.wait_ge(*chained("dve_chain"))
                moe1(2)
                for j in range(4):
                    dve.wait_ge(*filled(f"kv{j}"))
                    for c in range(2):
                        rows, cs = slice(c * DH, (c + 1) * DH), slice(c * V0, (c + 1) * V0)
                        src = bank(f"kv{j}").rearrange("p (a n) -> p a n", a=2)[rows, :, cs]
                        ins = v.tensor_copy(kvb[rows, 2 * j:2 * j + 2, cs], src)
                        if c == 0:
                            ins.then_inc(*signals("dve_chain"))
                            dve.wait_ge(*chained("dve_chain"))
                    ins.then_inc(*frees(f"kv{j}"))
                moe1(3)
                for t in range(NT):
                    for j in range(4):
                        dve.wait_ge(*filled(f"num{t}{j}"))
                        nm = bank(f"num{t}{j}").rearrange("p (a n) -> p a n", a=2)[:, :, 0:2 * V0].rearrange("p a (h v) -> p a h v", v=V0)
                        dn = small[:, 304 + 4 * (j % 2):308 + 4 * (j % 2)]
                        den = dn.rearrange("p (a h) -> p a h", a=2)
                        v.tensor_scalar(den, nm[:, :, :, DH], 1e-6, None, ALU.add).then_inc(*signals("dve_chain"))
                        dve.wait_ge(*chained("dve_chain"))
                        v.reciprocal(dn, dn).then_inc(*signals("dve_chain"))
                        dve.wait_ge(*chained("dve_chain"))
                        ot = o_tok[:, t, 256 * j:256 * (j + 1)].rearrange("p (a h v) -> p a h v", a=2, v=DH)
                        rb = dn.rearrange("p (a h o) -> p a h o", a=2, o=1).to_broadcast([P, 2, 2, DH])
                        v.tensor_tensor(ot, nm[:, :, :, 0:DH], rb, ALU.mult).then_inc(*frees(f"num{t}{j}"))
                moe1(4)
                v.tensor_tensor(qt[:, 0:4, :], rp[:, 0:4, :], rp[:, 4:8, :], ALU.add).then_inc(*signals("rope_ready"))
                dve.wait_ge(*filled("s0"))
                v.tensor_tensor(s0[:, :, :], tok(bank("s0")[:, 0:N]), boutb[:, :].rearrange("p (o d) -> p o d", o=1).to_broadcast([P, NT, D]), ALU.add).then_inc(*frees("s0"))
                for n in range(12):
                    hs = 4 if n < 4 else 2
                    dve.wait_ge(*filled(f"sc{n}"))
                    sc = bank(f"sc{n}").rearrange("p (h k) -> p h k", h=hs)
                    nm = small[:, 320 + 4 * (n % 2):320 + 4 * (n % 2) + hs]
                    v.tensor_reduce(nm, sc, AX.X, ALU.max, negate=True).then_inc(*signals("dve_chain"))
                    dve.wait_ge(*chained("dve_chain"))
                    nb = nm.rearrange("p (h o) -> p h o", o=1).to_broadcast([P, hs, 512 // hs])
                    if n == 0:
                        dve.wait_ge(*given("rope_ready"))
                    v.tensor_tensor(pp[:, n, :].rearrange("p (h k) -> p h k", h=hs), sc, nb, ALU.add).then_inc(*frees(f"sc{n}"))
                    if n == 5:
                        moe1(5)
                moe1(6)
                for n in range(1, 12, 2):
                    dve.wait_ge(*filled(f"pT{n}"))
                    v.tensor_copy(pT[:, n, :], bank(f"pT{n}")).then_inc(*frees(f"pT{n}"))
                    if n == 5:
                        moe1(7)
                moe1(8)
                dve.wait_ge(*filled("pv"))
                pv = bank("pv")[:, 0:2 * NHF * V1].rearrange("p (h v) -> p h v", v=V1)
                v.reciprocal(small[:, 128:160].rearrange("p (h o) -> p h o", o=1), pv[:, :, HD:V1]).then_inc(*signals("dve_chain"))
                dve.wait_ge(*chained("dve_chain"))
                v.tensor_tensor(ao[:, :, :].rearrange("p t (h d) -> p (t h) d", d=HD), pv[:, :, 0:HD],
                                     small[:, 128:160].rearrange("p (h o) -> p h o", o=1).to_broadcast([P, 2 * NHF, HD]), ALU.mult).then_inc(*frees("pv"))
                dve.wait_ge(*filled("wo"))
                v.tensor_tensor(x2[:, :, :], xn[:, :, :], tok(bank("wo")[:, 0:N]), ALU.add).then_inc(*frees("wo"))
                dve.wait_ge(*given("rms2_rstd"))
                for t in range(NT):
                    ins = v.tensor_scalar(sq[:, t, :], x2[:, t, :], small[:, 12 + t:13 + t], None, ALU.mult)
                    if t == 0:
                        ins.then_inc(*signals("dve_chain"))
                        dve.wait_ge(*chained("dve_chain"))
                ins.then_inc(*signals("h2_ready"))
                dve.wait_ge(*filled("gate"))
                v.tensor_copy(small[:, 160:176], bank("gate")[:, 0:NT * E]).then_inc(*frees("gate"))
                dve.wait_ge(*read_out("gate"))
                carry()
                for t in range(NT):
                    ins = v.max(m8[:, t, :], lg[:, t, :])
                ins.then_inc(*signals("dve_chain"))
                dve.wait_ge(*chained("dve_chain"))
                carry()
                for t in range(NT):
                    ins = v.max_index(idx8[:, t, :], m8[:, t, :], lg[:, t, :])
                ins.then_inc(*signals("dve_chain"))
                dve.wait_ge(*chained("dve_chain"))
                v.tensor_tensor(small[:, 32:48].rearrange("p (t e) -> p t e", t=NT), lg, m8[:, :, 0:1].to_broadcast([P, NT, E]), ALU.subtract).then_inc(*signals("lg_ready"))
                v.tensor_copy(idf, idx8[:, :, :]).then_inc(*signals("dve_chain"))
                dve.wait_ge(*chained("dve_chain"))
                oh = small[:, 208:240].rearrange("p (k t e) -> p k t e", k=2, t=NT)
                for k in range(2):
                    v.tensor_tensor(oh[:, k, :, :], io, idf[:, :, k:k + 1].to_broadcast([P, NT, E]), ALU.is_equal).then_inc(*signals("dve_chain"))
                    dve.wait_ge(*chained("dve_chain"))
                v.tensor_tensor(oh[:, 0, :, :], oh[:, 0, :, :], oh[:, 1, :, :], ALU.add).then_inc(*signals("dve_chain"))
                dve.wait_ge(*chained("dve_chain"))
                dve.wait_ge(*given("eg_ready"))
                v.tensor_tensor(gw, small[:, 32:48].rearrange("p (t e) -> p t e", t=NT), oh[:, 0, :, :], ALU.mult).then_inc(*signals("dve_chain"))
                dve.wait_ge(*chained("dve_chain"))
                v.tensor_reduce(small[:, 56:58], gw, AX.X, ALU.add).then_inc(*signals("dve_chain"))
                dve.wait_ge(*chained("dve_chain"))
                v.reciprocal(small[:, 56:58], small[:, 56:58]).then_inc(*signals("dve_chain"))
                dve.wait_ge(*chained("dve_chain"))
                v.tensor_tensor(gw, gw, small[:, 56:58].rearrange("p (t o) -> p t o", o=1).to_broadcast([P, NT, E]), ALU.mult).then_inc(*signals("dve_chain"))
                dve.wait_ge(*chained("dve_chain"))

            def attention1():
                moe0(0)
                moe0(1)
                if "D" in now["stages"]:
                    dve.wait_ge(*given("out_ready"))
                v.tensor_copy(x1_keep[:, :, :], x1[:, :, :]).then_inc(*signals("dve_chain"))
                dve.wait_ge(*chained("dve_chain"))
                normed(xn, x1, "ln1")
                normed(xr, xn, "ln1b", "z1_ready")
                dve.wait_ge(*filled("zT"))
                v.tensor_copy(x1T[:, :], bank("zT")[:, 0:N]).then_inc(*signals("dve_chain"))
                dve.wait_ge(*chained("dve_chain"))
                v.tensor_scalar(xT[:, 1, :], bank("zT")[:, N:2 * N], cols[:, 2:3], cols[:, 40:41], ALU.mult, ALU.add).then_inc(*frees("zT"))
                moe0(2)
                dve.wait_ge(*filled("ssq"))
                v.tensor_scalar(small[:, 64:96], bank("ssq")[:, 0:2 * H], 1e-24, None, ALU.max).then_inc(*frees("ssq"))
                for t in range(NT):
                    for c in range(2):
                        dve.wait_ge(*filled(f"tk{t}{c}"))
                        dve.wait_ge(*given("ks", 2 * t + c + 1))
                        v.tensor_copy(k_tok[:, t, c * 512:(c + 1) * 512], bank(f"tk{t}{c}")).then_inc(*frees(f"tk{t}{c}"))
                v.tensor_reduce(small[:, 96:128], reg[:, 0:2048].rearrange("p (h d) -> p h d", d=DH), AX.X, ALU.add).then_inc(*signals("dve_chain"))
                dve.wait_ge(*chained("dve_chain"))
                v.tensor_scalar(small[:, 96:128], small[:, 96:128], 1e-24, None, ALU.max).then_inc(*signals("ssk_ready"))
                for t in range(NT):
                    dve.wait_ge(*read_out(f"z{t}1"))
                    v.tensor_scalar(a_tok[:, t, :], a_tok[:, t, :], 999999.0, None, ALU.min).then_inc(*signals("ez_clamped"))
                moe0(3)
                dve.wait_ge(*filled("rqT"))
                v.tensor_copy(rqT[:, :], bank("rqT")[0:H, 0:N]).then_inc(*frees("rqT"))
                for j in range(4):
                    dve.wait_ge(*filled(f"rep{j}"))
                    s = slice(2 * j, 2 * j + 2)
                    v.scalar_tensor_tensor(out=qt[:, s, :], in0=bank(f"rep{j}").rearrange("p (a n) -> p a n", a=2), scalar=1e3, in1=qt[:, s, :], op0=ALU.mult, op1=ALU.mult).then_inc(*frees(f"rep{j}"))
                dve.wait_ge(*given("rk_ready"))
                for t in range(NT):
                    for c in range(2):
                        dve.wait_ge(*filled(f"tv{t}{c}"))
                        rb = small[:, 96 + t * H + 8 * c:96 + t * H + 8 * c + 8].rearrange("p (h o) -> p h o", o=1).to_broadcast([P, 8, DH])
                        v.scalar_tensor_tensor(out=v_tok[:, t, 8 * c:8 * c + 8, 0:DH], in0=bank(f"tv{t}{c}").rearrange("p (h d) -> p h d", d=DH),
                                                    scalar=1e3, in1=rb, op0=ALU.mult, op1=ALU.mult).then_inc(*frees(f"tv{t}{c}"))
                moe0(4)
                for t in range(NT):
                    dve.wait_ge(*given("a_ready", t + 1))
                    am = small[:, 272 + t * H:272 + (t + 1) * H]
                    v.tensor_reduce(am, a_tok[:, t, :].rearrange("p (h d) -> p h d", d=DH), AX.X, ALU.add).then_inc(*signals("dve_chain"))
                    dve.wait_ge(*chained("dve_chain"))
                    v.tensor_tensor(at3[:, t, :, :], am.rearrange("p (h o) -> p h o", o=1).to_broadcast([P, H, CH]),
                                         tri64[:, :].rearrange("p (o c) -> p o c", o=1).to_broadcast([P, H, CH]), ALU.mult).then_inc(*signals("at3_ready"))
                for t in range(NT):
                    for c in range(2):
                        dve.wait_ge(*filled(f"s{t}{c}"))
                        dve.wait_ge(*read_out(f"d{t}{c}"))
                        for ch in range(2):
                            rows = slice(ch * CH, (ch + 1) * CH)
                            w = pbd[rows, t, c, :, ch * CH:(ch + 1) * CH]
                            ins = v.tensor_tensor(w, bank(f"s{t}{c}")[rows, :].rearrange("p (a n) -> p a n", a=NP), w, ALU.mult)
                            if ch == 0:
                                ins.then_inc(*signals("dve_chain"))
                                dve.wait_ge(*chained("dve_chain"))
                        ins.then_inc(*frees(f"s{t}{c}"))
                for t in range(NT):
                    for c in range(2):
                        dve.wait_ge(*read_out(f"te{t}{c}"))
                        s = slice(c * 512, (c + 1) * 512)
                        ins = v.tensor_tensor(kd[:, t, s], kd[:, t, s], k_tok[:, t, s], ALU.mult)
                        ins.then_inc(*signals("kd_ready" if 2 * t + c == 3 else "kd_part"))
                dve.wait_ge(*read_out("la3"))
                v.tensor_copy(cd[:, :, :], el[:, :, CH - 1::CH]).then_inc(*signals("dve_chain"))
                dve.wait_ge(*chained("dve_chain"))
                v.tensor_tensor(el[:, :, :], el[:, :, :], qt[:, :, :], ALU.mult).then_inc(*signals("qd_ready"))
                moe0(5)
                for n in range(NC - 1):
                    for hh in range(2):
                        dve.wait_ge(*filled(f"st{n}{hh}"))
                        ps = slice(4 * hh, 4 * hh + 4)
                        for c in range(2):
                            rows = slice(c * DH, (c + 1) * DH)
                            src = bank(f"st{n}{hh}").rearrange("p (a n) -> p a n", a=4)[rows, :, rows]
                            dst = st[rows, n, ps, rows]
                            if n == 0:
                                ins = v.tensor_copy(dst, src)
                            else:
                                v.tensor_tensor(dst, st[rows, n - 1, ps, rows], cd[rows, ps, n:n + 1].to_broadcast([DH, 4, DH]), ALU.mult).then_inc(*signals("dve_chain"))
                                dve.wait_ge(*chained("dve_chain"))
                                ins = v.tensor_tensor(dst, dst, src, ALU.add)
                            if c == 0:
                                ins.then_inc(*signals("dve_chain"))
                                dve.wait_ge(*chained("dve_chain"))
                        ins.then_inc(*frees(f"st{n}{hh}"))
                        dve.wait_ge(*read_out(f"st{n}{hh}"))
                moe0(6)
                dve.wait_ge(sem("stored"), 16 * row("C") + 16)
                dve.wait_ge(*filled("wo1"))
                v.tensor_tensor(y2[:, :, :], xn[:, :, :], tok(bank("wo1")[:, 0:N]), ALU.add).then_inc(*frees("wo1"))
                dve.wait_ge(*read_out("wo1"))
                normed(xr, y2, "ln2", "z2_ready")
                dve.wait_ge(*filled("gate1"))
                v.tensor_tensor(lg, bank("gate1")[:, 0:NT * E].rearrange("p (t e) -> p t e", t=NT),
                                     bgb[:, :].rearrange("p (o e) -> p o e", o=1).to_broadcast([P, NT, E]), ALU.add).then_inc(*frees("gate1"))
                dve.wait_ge(*read_out("gate1"))
                carry()
                for t in range(NT):
                    ins = v.max(m8[:, t, :], lg[:, t, :])
                ins.then_inc(*signals("dve_chain"))
                dve.wait_ge(*chained("dve_chain"))
                carry()
                for t in range(NT):
                    ins = v.max_index(idx8[:, t, :], m8[:, t, :], lg[:, t, :])
                ins.then_inc(*signals("dve_chain"))
                dve.wait_ge(*chained("dve_chain"))
                v.tensor_copy(idf, idx8[:, :, :]).then_inc(*signals("dve_chain"))
                dve.wait_ge(*chained("dve_chain"))
                v.tensor_tensor(oh1, io, idf[:, :, 0:1].to_broadcast([P, NT, E]), ALU.is_equal).then_inc(*signals("oh_ready"))
                moe0(7)
                dve.wait_ge(*filled("z2T"))
                v.tensor_scalar(xT[:, 1, :], bank("z2T")[:, 0:N], cols[:, 3:4], cols[:, 41:42], ALU.mult, ALU.add).then_inc(*frees("z2T"))
                dve.wait_ge(*filled("ohT"))
                v.tensor_copy(ohT[:, :], bank("ohT")[0:E, 0:N]).then_inc(*frees("ohT"))
                b2bb = b2b[:, :].rearrange("p (o d) -> p o d", o=1).to_broadcast([P, NT, D])
                v.tensor_tensor(y2[:, :, :], y2[:, :, :], b2bb, ALU.add).then_inc(*signals("dve_chain"))
                dve.wait_ge(*chained("dve_chain"))
                moe0(8)
                dve.wait_ge(*filled("w2"))
                v.tensor_tensor(y2[:, :, :], y2[:, :, :], tok(bank("w2")[:, 0:N]), ALU.add).then_inc(*frees("w2"))
                dve.wait_ge(*filled("b2y"))
                v.tensor_copy(acc1[:, :, :], tok(bank("b2y")[:, 0:N])).then_inc(*frees("b2y"))
                dve.wait_ge(*read_out("b2y"))

            def body():
                if "A" in now["stages"]:
                    attention0()
                else:
                    for e in range(E + 1):
                        moe1(e)
                if "C" in now["stages"]:
                    attention1()
                else:
                    for e in range(E + 1):
                        moe0(e)
                checked()

            for n, (stages, times) in enumerate(SEGMENTS):
                if times == 1:
                    segment(n, 0)
                    body()
                else:
                    with dve.Fori(0, times) as i:
                        segment(n, i)
                        body()

def kernel(**inputs):
    import concourse.bacc as bacc
    from concourse.bass_utils import run_bass_kernel_spmd

    I = {k: np.asarray(v) for k, v in inputs.items()}
    ca = np.ascontiguousarray
    bf = mybir.dt.np(mybir.dt.bfloat16)

    def split_k(w):
        return ca(w.reshape(-1, P, w.shape[-1]).transpose(1, 0, 2))

    wq = I["L0_ffn_wqkv"]
    q = wq[:NHF * HD].reshape(NKV, GR, HD, D)
    k = wq[NHF * HD:(NHF + NKV) * HD].reshape(NKV, 1, HD, D)
    turn = np.r_[HD // 2:HD, 0:HD // 2]
    wrope = np.zeros((D, 10, P), np.float32)
    for g in range(NKV):
        for a in range(GR):
            wrope[:, a, 32 * g:32 * g + HD] = q[g, a].T
            wrope[:, 4 + a, 32 * g:32 * g + HD] = q[g, a][turn].T
        wrope[:, 8, 32 * g:32 * g + HD] = k[g, 0].T
        wrope[:, 9, 32 * g:32 * g + HD] = k[g, 0][turn].T
    inv = (1.0 / np.float32(10000.0) ** (np.arange(0, HD, 2, dtype=np.float32) / np.float32(HD))).astype(np.float32)
    ang = np.arange(N, dtype=np.float32)[:, None] * inv[None, :]
    ang = np.concatenate([ang, ang], -1).T
    ropec = np.zeros((P, 2, N), np.float32)
    for g in range(NKV):
        ropec[32 * g:32 * g + HD, 0] = np.cos(ang)
        ropec[32 * g:32 * g + HD, 1] = np.sin(ang) * np.r_[-np.ones(HD // 2), np.ones(HD // 2)].astype(np.float32)[:, None]
    ew = np.concatenate([I["L1_ffn_W1"], I["L1_ffn_W2"].reshape(E, 4, P, D).transpose(0, 2, 1, 3).reshape(E, P, 4 * D)], -1)
    cols = np.concatenate([
        I["L0_ffn_ln1_w"][:, None], I["L0_ffn_ln2_w"][:, None], I["L1_attn_ln1_w"][:, None], I["L1_attn_ln2_w"][:, None],
        I["L1_attn_b1"].reshape(4, P).T, I["L1_ffn_b1"].reshape(E * 4, P).T,
        I["L1_attn_ln1_b"][:, None], I["L1_attn_ln2_b"][:, None], np.full((P, 1), 1e-5, np.float32)], 1)
    r = np.arange(P)
    same = (r[:, None] // CH) == (r[None, :] // CH)
    keep = r[None, :] <= r[:, None]
    cmask = np.zeros((P, 2, 512), np.float32)
    cmask[:, 0] = np.tile(np.where(keep, 0, NEG), (1, 4))
    cmask[:, 1] = np.tile(np.concatenate([np.zeros((P, P)), np.where(keep, 0, NEG)], 1), (1, 2))
    dmask = np.tile(np.where(np.arange(CH)[None, :] < (r % CH)[:, None], -NEG, 0)[:, None, :], (1, 8, 1))
    h = np.arange(H)
    arrays = {
        "x": I["L0_attn_x"],
        "wqkv0": I["L0_attn_Wqkv"], "wout0": split_k(I["L0_attn_Wout"]), "bout": I["L0_attn_bout"],
        "wrope": wrope, "ropec": ropec, "wv9": ca(wq[(NHF + NKV) * HD:].T), "woT": ca(I["L0_ffn_wo"].T), "gateT": ca(I["L0_ffn_gate_w"].T),
        "w13T": ca(I["L0_ffn_w13"].transpose(2, 0, 1)),
        "w2T": ca(I["L0_ffn_w2"].reshape(E, D, 2, P).transpose(3, 0, 2, 1)),
        "lqkvg": ca(np.concatenate([I["L1_attn_Wq"], I["L1_attn_Wk"], I["L1_attn_Wv"], I["L1_attn_Wg"]], 1)),
        "bg": I["L1_attn_bg"].reshape(1, -1), "lwo": split_k(I["L1_attn_Wo"]), "lw1": I["L1_attn_W1"], "lw2": split_k(I["L1_attn_W2"]),
        "mg": I["L1_ffn_Wg"], "mb2": I["L1_ffn_b2"], "cols": ca(cols), "bgm": I["L1_ffn_bg"], "b2": I["L1_attn_b2"], "ew": ca(ew),
        "identb": np.eye(P, dtype=np.float32).astype(bf), "cmask": cmask.astype(bf), "dmask": dmask.astype(bf), "ones3": np.ones((3, P), bf),
        "tri": (same & (r[:, None] <= r[None, :])).astype(np.float32), "strict": (same & (r[:, None] > r[None, :])).astype(np.float32),
        "tri64": ((r % CH)[:, None] <= np.arange(CH)[None, :]).astype(np.float32), "ident": np.eye(P, dtype=np.float32),
        "pairsel": (h[None, None, :] == 2 * np.arange(NP)[None, :, None] + (r // DH)[:, None, None]).astype(np.float32),
        "headsel": (h[:, None, None] == 2 * np.arange(NP)[None, :, None] + (r // DH)[None, None, :]).astype(np.float32),
        "iota8": np.tile(np.arange(E, dtype=np.float32), (P, 1)),
    }
    nc = bacc.Bacc("TRN2", target_bir_lowering=False, num_devices=1)
    feeds = {f"in_{n}": ca(a) for n, a in arrays.items()}
    A = {n: nc.dram_tensor(f"in_{n}", a.shape, mybir.dt.from_np(a.dtype), kind="ExternalInput").ap() for n, a in arrays.items()}
    out = nc.dram_tensor("out", (B, N, D), mybir.dt.float32, kind="ExternalOutput").ap()
    build(nc, A, out)
    r = run_bass_kernel_spmd(nc, [feeds], core_ids=[0])
    return r.results[0]["out"]
```

```python
from contextlib import ExitStack

import concourse.bass as bass
import numpy as np
from concourse import mybir

B, N, D = 16, 256, 128
P = 128
NT = N // P
H, DH = 16, 64
NP = H // 2
INNER = H * DH
NHF, NKV, HD = 16, 4, 8
GR = NHF // NKV
E = 8
F0 = 256
F1 = 512
CH = 64
NC = N // CH
V1 = HD + 1
V0 = DH + 1
NEG = -3.0e38

SEGMENTS = [("AB", 1), ("ABC", 1), ("ABCD", B - 2), ("CD", 1), ("D", 1)]

RING = 7

def uses_in_order(stages):
    names = []

    def moe0(e):
        if "B" in stages:
            if e < E:
                names.extend([f"a{e}", f"b{e}"])
            if e:
                names.append(f"y{e - 1}")

    def moe1(e):
        if "D" in stages:
            if e < E:
                names.extend([f"h{e}0", f"h{e}1"])
            if e:
                names.append(f"yy{e - 1}")

    def z_inputs():
        if "C" in stages:
            names.append("zT")

    def z_products(t):
        if "C" in stages:
            names.extend([f"z{t}0", f"z{t}1"])

    if "A" in stages:
        moe1(0)
        moe1(1)
        names += ["xT"]
        names += [f"q{j}" for j in range(4)]
        names += [f"k{t}{c}" for t in range(NT) for c in range(2)]
        names += ["rT"]
        names += [f"v{t}{c}" for t in range(NT) for c in range(2)]
        names += [f"rq{j}" for j in range(2)] + [f"rs{j}" for j in range(2)] + ["rk", "v9"]
        moe1(2)
        names += [f"kv{j}" for j in range(4)]
        moe1(3)
        names += [f"num{t}{j}" for t in range(NT) for j in range(4)]
        moe1(4)
        names += [f"oT{t}{c}" for t in range(NT) for c in range(2)] 
        for n in range(12):
            names += [f"sc{n}"]
            if n == 1:
                names += ["s0"]
            if n == 5:
                moe1(5)
        for n in range(12):
            names += [f"pT{n}"]
            if n == 5:
                moe1(6)
        names += ["pv"]
        moe1(7)
        names += ["aT", "wo"]
        z_inputs()
        moe1(8)
        names += ["hT"]
        z_products(0)
        names += ["gate"]
        z_products(1)
    else:
        for e in range(E + 1):
            moe1(e)
    if "C" in stages:
        if "A" not in stages:
            z_inputs()
            z_products(0)
            z_products(1)
        moe0(0)
        moe0(1)
        moe0(2)
        names += [f"lq{j}" for j in range(4)] + [f"lk{j}" for j in range(4)] + [f"nq{j}" for j in range(4)]
        names += [f"tk{t}{c}" for t in range(NT) for c in range(2)]
        moe0(3)
        names += [f"d{t}{c}" for t in range(NT) for c in range(2)]
        names += [f"te{t}{c}" for t in range(NT) for c in range(2)]
        names += [f"tv{t}{c}" for t in range(NT) for c in range(2)]
        moe0(4)
        names += [f"s{t}{c}" for t in range(NT) for c in range(2)]
        names += [f"la{j}" for j in range(4)]
        moe0(5)
        names += [f"st{n}{hh}" for n in range(NC - 1) for hh in range(2)]
        names += ["gate1"]
        moe0(6)
        names += [f"o{j}" for j in range(4)]
        names += ["wo1", "ohT"]
        moe0(7)
        names += ["z2T", "b2y", "f0", "f1"]
        moe0(8)
        names += ["w2"]
    else:
        for e in range(E + 1):
            moe0(e)
    return names

def psum_plan():
    plans, uses, nxt, total = [], [], 0, [0] * RING
    for stages, times in SEGMENTS:
        plan, n = {}, [0] * RING
        for i, name in enumerate(uses_in_order(stages)):
            b = (nxt + i) % RING
            n[b] += 1
            plan[name] = (b, total[b] + n[b])
        if times == 1:
            nxt = (nxt + len(plan)) % RING
        plans.append(plan)
        uses.append(n)
        total = [total[b] + n[b] * times for b in range(RING)]
    return plans, uses

PLANS, USES = psum_plan()

PER = {
    "A": {"act_chain": 5, "dve_chain": 52, "eg_ready": 1, "ek": 4, "eq": 4, "h2_ready": 1, "k0_part": 3, "k0_ready": 1,
          "lg_ready": 1, "ln0_rstd": 1, "ln0_stat": 1, "ones_ready": 1, "p_ready": 12, "q0_part": 3, "q0_ready": 1, "rms0_rstd": 1,
          "rms0_stat": 1, "rms2_rstd": 1, "rope_ready": 1, "x_free": 1, "x_ready": 1, "xn_ready": 1, "xr_ready": 1},
    "B": {"dve_chain": 10, "sg_ready": 1},
    "C": {"a_ready": 2, "act_chain": 8, "at3_ready": 2, "cd_ready": 1, "dec_half": 4, "dve_chain": 37, "ez_clamped": 2,
          "gelu_half": 2, "kd_part": 3, "kd_ready": 1, "ks": 4, "ln1_rstd": 1, "ln1_stat": 1, "ln1b_rstd": 1, "ln1b_stat": 1,
          "ln2_rstd": 1, "ln2_stat": 1, "oh_ready": 1, "qd_part": 1, "qd_ready": 1, "qn_part": 3, "qn_ready": 1, "rk_ready": 1,
          "rq_ready": 4, "sq_done": 4, "ssk_ready": 1, "z1_ready": 1, "z2_ready": 1},
    "D": {"dve_chain": 1, "ew0_free": 4, "ew0_ready": 4, "ew1_free": 4, "ew1_ready": 4, "out_ready": 1, "sg1_ready": 1},
}

def in_body(stages, name):
    return sum(PER[s].get(name, 0) for s in stages)

def build(nc, A, out, debug=None):
    dt = mybir.dt
    f32, b16 = dt.float32, dt.bfloat16
    ALU, ACT, AX = mybir.AluOpType, mybir.ActivationFunctionType, mybir.AxisListType
    ctx = ExitStack()
    with ctx:
        def sb(name, shape, d=f32):
            return ctx.enter_context(nc.sbuf_tensor(name, shape, d))

        wqkv0 = sb("wqkv0", [P, 3 * INNER])
        wout0 = sb("wout0", [P, NP, D])
        boutb = sb("boutb", [P, D])
        wrope = sb("wrope", [P, 10, P])
        wv9 = sb("wv9", [P, NKV * HD])
        woT = sb("woT", [P, D])
        gateT = sb("gateT", [P, E])
        w13T = sb("w13T", [P, E, 2 * F0])
        w2T = sb("w2T", [P, E, 2, D])
        lqkvg = sb("lqkvg", [P, 4 * INNER])
        bg3 = sb("bg3", [3, INNER], b16)
        lwo = sb("lwo", [P, NP, D])
        lw1 = sb("lw1", [P, F1])
        lw2 = sb("lw2", [P, 4, D])
        mg = sb("mg", [P, E])
        mb2 = sb("mb2", [E, D])
        cols = sb("cols", [P, 43])
        bgb = sb("bgb", [P, E])
        b2b = sb("b2b", [P, D])
        ropec = sb("ropec", [P, 2, N])
        tri = sb("tri", [P, P])
        strict = sb("strict", [P, P])
        tri64 = sb("tri64", [P, CH])
        ident = sb("ident", [P, P])
        identb = sb("identb", [P, P], b16)
        cmask = sb("cmask", [P, 2, 2 * N], b16)
        dmask = sb("dmask", [P, 8, CH], b16)
        zerob = sb("zerob", [P, 512], b16)
        ones3 = sb("ones3", [3, P], b16)
        samehead = sb("samehead", [P, P])
        iota8 = sb("iota8", [P, E])
        ew = sb("ew", [P, 2, 2 * F1 * 1])
        x = sb("x", [P, NT, D])
        xn = sb("xn", [P, NT, D])
        xr = sb("xr", [P, NT, D])
        xn1 = sb("xn1", [P, NT, D])
        xr1 = sb("xr1", [P, NT, D])
        xT = sb("xT_s", [P, 2, N])
        x2 = sb("x2", [P, NT, D])
        hT = sb("hT_s", [P, N])
        acc0 = sb("acc0", [P, NT, D])
        acc1 = sb("acc1", [P, NT, D])
        x_keep = sb("x_keep", [P, NT, D])
        x1_keep = sb("x1_keep", [P, NT, D])
        y2 = sb("y2", [P, NT, D])
        x1T = sb("x1T_s", [P, N])
        gbuf = sb("gbuf", [P, 4 * N])
        s0 = sb("s0_s", [P, NT, D])
        sg = sb("sg", [P, NT, D])
        x1 = sb("x1", [P, NT, D])
        sq = sb("sq", [P, NT, D])
        small = sb("small", [P, 512])
        idx8 = sb("idx8", [P, NT, 8], dt.uint32)
        qt = sb("qt", [P, NP, N])
        big = sb("big", [P, 2 * INNER + NT * H * V0 + 2 * INNER])
        reg = sb("reg", [P, 12 * 512])
        kvb = sb("kvb", [P, NP, 2 * V0])
        pbd = sb("pbd", [P, NT, 2, NP, P])
        st = sb("st", [P, NC - 1, NP, P])
        cd = sb("cd", [P, NP, NC])
        v9 = sb("v9_s", [P, NT, NKV, V1])
        kr = sb("kr", [P, N])

        k_tok = big[:, 0:2 * INNER].rearrange("p (t f) -> p t f", t=NT)
        v_tok = big[:, 2 * INNER:2 * INNER + NT * H * V0].rearrange("p (t h v) -> p t h v", t=NT, v=V0)
        o_tok = big[:, 2 * INNER + NT * H * V0:].rearrange("p (t f) -> p t f", t=NT)
        oT = big[:, 0:2 * INNER].rearrange("p (a n) -> p a n", a=NP)
        a_tok = o_tok
        pT = big[:, 0:12 * 512].rearrange("p (n k) -> p n k", n=12)
        e_q = reg[:, 0:2048].rearrange("p (a n) -> p a n", a=NP)
        e_k = reg[:, 2048:4096].rearrange("p (t f) -> p t f", t=NT)
        qr = qt[:, 0:4, :]
        qs = qt[:, 4:8, :]
        krs = sq[:, :, :].rearrange("p t d -> p (t d)")
        rp = reg[:, 4096:6144].rearrange("p (a n) -> p a n", a=8)
        pp = reg[:, :].rearrange("p (n k) -> p n k", n=12)
        ao = reg[:, 0:256].rearrange("p (t d) -> p t d", t=NT)
        aT = reg[:, 256:512]
        g0 = gbuf[:, :].rearrange("p (s c n) -> p s c n", s=2, c=2)
        kd = reg[:, 0:2048].rearrange("p (t f) -> p t f", t=NT)
        at3 = reg[:, 0:2048].rearrange("p (t h c) -> p t h c", t=NT, h=H)
        el = reg[:, 2048:4096].rearrange("p (a n) -> p a n", a=NP)
        sqT = el
        ks_row = big[:, 2048:4096]
        ks = ks_row.rearrange("p (t f) -> p t f", t=NT)
        kT = reg[:, 4096:6144].rearrange("p (a n) -> p a n", a=NP)
        oT1 = kT
        g1 = reg[:, 0:1024].rearrange("p (c n) -> p c n", c=4)
        r1 = gbuf[:, :].rearrange("p (c n) -> p c n", c=4)
        ohT = sq[0:E, :, :].rearrange("p t d -> p (t d)")
        bg_row = small[0:3, 0:3]

        psum = ctx.enter_context(nc.psum_tensor("psum", [P, 8, 512], f32))

        sems = {}

        def sem(name):
            if name not in sems:
                sems[name] = ctx.enter_context(nc.semaphore(name))
            return sems[name]

        for b in range(RING):
            sem(f"bank{b}_full"), sem(f"bank{b}_free")

        now = {}

        def segment(n, i):
            now.update(n=n, i=i, plan=PLANS[n], stages=SEGMENTS[n][0], count={})

        def rows_before(stage):
            return sum(times for stages, times in SEGMENTS[:now["n"]] if stage in stages)

        def row(stage):
            return now["i"] + rows_before(stage)

        def bank(use):
            return psum[:, now["plan"][use][0], :]

        def given(name, n=1, by=1):
            before = sum(times * in_body(stages, name) for stages, times in SEGMENTS[:now["n"]])
            return sem(name), now["i"] * (in_body(now["stages"], name) * by) + (before + n) * by

        def signals(name):
            now["count"][name] = now["count"].get(name, 0) + 1
            return sem(name), 1

        def chained(name):
            return given(name, now["count"][name])

        def bank_uses(use, more):
            b, n = now["plan"][use]
            return now["i"] * USES[now["n"]][b] + n + more

        def fills(use):
            return sem(f"bank{now['plan'][use][0]}_full"), 1

        def filled(use):
            return sem(f"bank{now['plan'][use][0]}_full"), bank_uses(use, 0)

        def frees(use):
            return sem(f"bank{now['plan'][use][0]}_free"), 1

        def emptied(use):
            return sem(f"bank{now['plan'][use][0]}_free"), bank_uses(use, 0)

        def read_out(use):
            return sem(f"bank{now['plan'][use][0]}_free"), bank_uses(use, 1)

        def checked():
            for name, n in now["count"].items():
                assert n == in_body(now["stages"], name), (now["stages"], name, n)

        def kd_b16(i):
            return reg[0:1, i * 512:(i + 1) * 512].bitcast(b16)

        blk = ctx.enter_context(nc.Block())
        NLOAD, NFIRST = [0], [0]

        @blk.sync
        def _(sp):
            def load_first(dst, src):
                NFIRST[0] += 1
                sp.dma_start(dst, src).then_inc(sem("first_weights"), 16)

            def load(dst, src):
                NLOAD[0] += 1
                sp.dma_start(dst, src).then_inc(sem("weights"), 16)

            sp.dma_start(big[0:1, 0:INNER], A["bg"]).then_inc(sem("bg_loaded"), 16)
            sp.dma_start(x[:, :, :], A["x"][0].rearrange("(t p) d -> p t d", p=P)).then_inc(sem("x_ready"), 16)
            load_first(cols[:, :], A["cols"])
            load_first(ident[:, :], A["ident"])
            load_first(wqkv0[:, :], A["wqkv0"])
            load_first(wrope[:, :, :], A["wrope"])
            load_first(ropec[:, :, :], A["ropec"])
            load_first(wv9[:, :], A["wv9"])
            load_first(wout0[:, :, :], A["wout0"])
            load_first(boutb[:, :], A["bout"].partition_broadcast(P))
            load_first(identb[:, :], A["identb"])
            load_first(cmask[:, :, :], A["cmask"])
            load_first(woT[:, :], A["woT"])
            load_first(gateT[:, :], A["gateT"])
            load_first(iota8[:, :], A["iota8"])
            load(w13T[:, :, :], A["w13T"])
            load(w2T[:, :, :, :], A["w2T"])
            load(lqkvg[:, :], A["lqkvg"])
            load(lwo[:, :, :], A["lwo"])
            load(lw1[:, :], A["lw1"])
            load(lw2[:, :, :], A["lw2"])
            load(mg[:, :], A["mg"])
            load(mb2[:, :], A["mb2"])
            load(bgb[:, :], A["bgm"].partition_broadcast(P))
            load(b2b[:, :], A["b2"].partition_broadcast(P))
            load(dmask[:, :, :], A["dmask"])
            load(ones3[:, :], A["ones3"])
            load(tri[:, :], A["tri"])
            load(strict[:, :], A["strict"])
            load(tri64[:, :], A["tri64"])
            load(samehead[:, :], A["samehead"])
            sp.wait_ge(sem("bg_split"), 1)
            for i in range(3):
                sp.dma_start(bg3[i:i + 1, :], kd_b16(i)).then_inc(sem("bg3_ready"), 16)
            sp.sem_inc(sem("stored"), 16)

            def body():
                if "A" in now["stages"] and now["n"]:
                    sp.wait_ge(*given("x_free"))
                    sp.dma_start(x[:, :, :], A["x"][row("A")].rearrange("(t p) d -> p t d", p=P)).then_inc(sem("x_ready"), 16)
                if "D" in now["stages"]:
                    for e in range(E):
                        sp.wait_ge(*given(f"ew{e % 2}_free", e // 2 + 1))
                        sp.dma_start(ew[:, e % 2, :], A["ew"][e]).then_inc(sem(f"ew{e % 2}_ready"), 16)
                    sp.wait_ge(*given("out_ready"))
                    sp.dma_start(out[row("D")].rearrange("(t p) d -> p t d", p=P), y2[:, :, :]).then_inc(sem("stored"), 16)

            for n, (stages, times) in enumerate(SEGMENTS):
                if times == 1:
                    segment(n, 0)
                    body()
                else:
                    with sp.Fori(0, times) as i:
                        segment(n, i)
                        body()
            sp.wait_ge(sem("stored"), 16 * (B + 1))

        @blk.gpsimd
        def _(g):
            g.memset(kvb[:, :, :], 0.0).then_inc(sem("zeros"), 1)
            g.memset(st[:, :, :, :], 0.0).then_inc(sem("zeros"), 1)
            g.memset(pbd[:, :, :, :, :], 0.0).then_inc(sem("zeros"), 1)
            g.memset(zerob[:, :], 0.0).then_inc(sem("zeros"), 1)
            g.memset(v9[:, :, :, :], 1.0).then_inc(sem("zeros"), 1)

            def attention1():
                g.wait_ge(*given("cd_ready"))
                for half in range(2):
                    s = slice(4 * half, 4 * half + 4)
                    ins = nc.gpsimd.tensor_tensor(el[:, s, :], el[:, s, :], qt[:, s, :], ALU.mult)
                    ins.then_inc(*signals("qd_ready" if half else "qd_part"))

            def body():
                if "C" in now["stages"]:
                    attention1()
                checked()

            for n, (stages, times) in enumerate(SEGMENTS):
                if times == 1:
                    segment(n, 0)
                    body()
                else:
                    with g.Fori(0, times) as i:
                        segment(n, i)
                        body()

        @blk.tensor
        def _(pe):
            mm = nc.tensor.matmul

            def tr(dst, src, idn=None):
                k = src.shape[0]
                return nc.tensor.transpose(dst, src, ident[0:k, 0:k])

            for b in range(RING):
                pe.sem_inc(sem(f"bank{b}_free"), 1)
            pe.wait_ge(sem("first_weights"), 16 * NFIRST[0])
            pe.wait_ge(sem("zeros"), 5)
            def moe0(e):
                if "B" not in now["stages"]:
                    return
                if e < E:
                    for name, off in (("a", 0), ("b", F0)):
                        pe.wait_ge(*emptied(f"{name}{e}"))
                        for c in range(2):
                            last = mm(bank(f"{name}{e}")[:, c * N:(c + 1) * N], w13T[:, e, off + c * P:off + (c + 1) * P], hT[:, :], start=True, stop=True)
                        last.then_inc(*fills(f"{name}{e}"))
                if e:
                    pe.wait_ge(*read_out(f"b{e - 1}"))
                    pe.wait_ge(*emptied(f"y{e - 1}"))
                    for t in range(NT):
                        for c in range(2):
                            last = mm(bank(f"y{e - 1}")[:, t * P:(t + 1) * P], g0[:, (e - 1) % 2, c, t * P:(t + 1) * P], w2T[:, e - 1, c, :], start=(c == 0), stop=(c == 1))
                    last.then_inc(*fills(f"y{e - 1}"))

            def moe1(e):
                if "D" not in now["stages"]:
                    return
                if e < E:
                    pe.wait_ge(*given(f"ew{e % 2}_ready", e // 2 + 1, 16))
                    for j in range(2):
                        pe.wait_ge(*emptied(f"h{e}{j}"))
                        for a in range(2):
                            c = 2 * j + a
                            last = mm(bank(f"h{e}{j}")[:, a * N:(a + 1) * N], ew[:, e % 2, c * P:(c + 1) * P], x1T[:, :], start=True, stop=True)
                        last.then_inc(*fills(f"h{e}{j}"))
                if e:
                    pe.wait_ge(*read_out(f"h{e - 1}1"))
                    pe.wait_ge(*emptied(f"yy{e - 1}"))
                    for t in range(NT):
                        for c in range(4):
                            last = mm(bank(f"yy{e - 1}")[:, t * P:(t + 1) * P], r1[:, c, t * P:(t + 1) * P],
                                      ew[:, (e - 1) % 2, F1 + c * D:F1 + (c + 1) * D], start=(c == 0), stop=(c == 3))
                    last.then_inc(*fills(f"yy{e - 1}"))

            def z_inputs():
                if "C" not in now["stages"]:
                    return
                pe.wait_ge(*given("z1_ready"))
                pe.wait_ge(*emptied("zT"))
                for t in range(NT):
                    tr(bank("zT")[:, t * P:(t + 1) * P], xn1[:, t, :])
                for t in range(NT):
                    last = tr(bank("zT")[:, N + t * P:N + (t + 1) * P], xr1[:, t, :])
                last.then_inc(*fills("zT"))

            def z_products(t):
                if "C" not in now["stages"]:
                    return
                if t == 0:
                    pe.wait_ge(*read_out("zT"))
                for c in range(2):
                    pe.wait_ge(*emptied(f"z{t}{c}"))
                    mm(bank(f"z{t}{c}"), ones3[:, :], bg3[:, c * 512:(c + 1) * 512], start=True, stop=False)
                    mm(bank(f"z{t}{c}"), xT[:, 1, t * P:(t + 1) * P], lqkvg[:, 3 * INNER + c * 512:3 * INNER + (c + 1) * 512],
                       start=False, stop=True).then_inc(*fills(f"z{t}{c}"))

            def attention0():
                moe1(0)
                moe1(1)
                pe.wait_ge(*given("xn_ready"))
                pe.wait_ge(*emptied("xT"))
                for t in range(NT):
                    last = tr(bank("xT")[:, t * P:(t + 1) * P], xn[:, t, :])
                last.then_inc(*fills("xT"))
                pe.wait_ge(*read_out("xT"))
                xnT, h1T = xT[:, 0, :], xT[:, 1, :]
                for j in range(4):
                    pe.wait_ge(*emptied(f"q{j}"))
                    for a in range(2):
                        pr = 2 * j + a
                        last = mm(bank(f"q{j}")[:, a * N:(a + 1) * N], wqkv0[:, pr * P:(pr + 1) * P], xnT, start=True, stop=True)
                    last.then_inc(*fills(f"q{j}"))
                for name, off in (("k", INNER), ("v", 2 * INNER)):
                    if name == "v":
                        pe.wait_ge(*given("xr_ready"))
                        pe.wait_ge(*emptied("rT"))
                        for t in range(NT):
                            last = tr(bank("rT")[:, t * P:(t + 1) * P], xr[:, t, :])
                        last.then_inc(*fills("rT"))
                    for t in range(NT):
                        for c in range(2):
                            pe.wait_ge(*emptied(f"{name}{t}{c}"))
                            mm(bank(f"{name}{t}{c}"), xnT[:, t * P:(t + 1) * P],
                                    wqkv0[:, off + c * 512:off + (c + 1) * 512], start=True, stop=True).then_inc(*fills(f"{name}{t}{c}"))
                pe.wait_ge(*read_out("rT"))
                for name, w0 in (("rq", 0), ("rs", 4)):
                    for j in range(2):
                        pe.wait_ge(*emptied(f"{name}{j}"))
                        for a in range(2):
                            last = mm(bank(f"{name}{j}")[:, a * N:(a + 1) * N], wrope[:, w0 + 2 * j + a, :], h1T, start=True, stop=True)
                        last.then_inc(*fills(f"{name}{j}"))
                pe.wait_ge(*emptied("rk"))
                for a in range(2):
                    last = mm(bank("rk")[:, a * N:(a + 1) * N], wrope[:, 8 + a, :], h1T, start=True, stop=True)
                last.then_inc(*fills("rk"))
                pe.wait_ge(*emptied("v9"))
                for t in range(NT):
                    last = mm(bank("v9")[:, t * 32:(t + 1) * 32], h1T[:, t * P:(t + 1) * P], wv9[:, :], start=True, stop=True)
                last.then_inc(*fills("v9"))
                moe1(2)
                pe.wait_ge(*given("k0_ready"))
                pe.wait_ge(*read_out("v11"))
                for j in range(4):
                    pe.wait_ge(*emptied(f"kv{j}"))
                    for a in range(2):
                        pr = 2 * j + a
                        for t in range(NT):
                            last = mm(bank(f"kv{j}")[:, a * N:a * N + 2 * V0], k_tok[:, t, pr * P:(pr + 1) * P],
                                      v_tok[:, t, 2 * pr:2 * pr + 2, :], start=(t == 0), stop=(t == NT - 1))
                    last.then_inc(*fills(f"kv{j}"))
                moe1(3)
                pe.wait_ge(*given("q0_ready"))
                for t in range(NT):
                    for j in range(4):
                        if t == 0:
                            pe.wait_ge(*read_out(f"kv{j}"))
                        pe.wait_ge(*emptied(f"num{t}{j}"))
                        for a in range(2):
                            pr = 2 * j + a
                            last = mm(bank(f"num{t}{j}")[:, a * N:a * N + 2 * V0], qt[:, pr, t * P:(t + 1) * P], kvb[:, pr, :], start=True, stop=True)
                        last.then_inc(*fills(f"num{t}{j}"))
                moe1(4)
                for t in range(NT):
                    pe.wait_ge(*read_out(f"num{t}3"))
                    for c in range(2):
                        pe.wait_ge(*emptied(f"oT{t}{c}"))
                        for a in range(4):
                            last = tr(bank(f"oT{t}{c}")[:, a * P:(a + 1) * P], o_tok[:, t, (4 * c + a) * P:(4 * c + a + 1) * P])
                        last.then_inc(*fills(f"oT{t}{c}"))
                pe.wait_ge(*given("rope_ready"))
                for n in range(12):
                    use = f"sc{n}"
                    pe.wait_ge(*emptied(use))
                    if n < 4:
                        mm(bank(use), identb[:, :], cmask[:, 0, :], start=True, stop=False)
                        for r in range(GR):
                            p0 = 32 * n
                            last = mm(bank(use)[:, r * P:(r + 1) * P], qr[p0:p0 + HD, r, 0:P], kr[p0:p0 + HD, 0:P], start=False, stop=(r == GR - 1))
                    else:
                        grp, half = (n - 4) // 2, (n - 4) % 2
                        p0 = 32 * grp
                        mm(bank(use), identb[:, :], cmask[:, 1, :], start=True, stop=False)
                        for a in range(2):
                            last = mm(bank(use)[:, a * N:(a + 1) * N], qr[p0:p0 + HD, 2 * half + a, P:N], kr[p0:p0 + HD, :], start=False, stop=(a == 1))
                    last.then_inc(*fills(use))
                    if n == 1:
                        pe.wait_ge(*emptied("s0"))
                        pe.wait_ge(*read_out("oT11"))
                        for t in range(NT):
                            for pr in range(NP):
                                last = mm(bank("s0")[:, t * P:(t + 1) * P], oT[:, pr, t * P:(t + 1) * P], wout0[:, pr, :], start=(pr == 0), stop=(pr == NP - 1))
                        last.then_inc(*fills("s0"))
                    if n == 5:
                        moe1(5)
                for n in range(12):
                    pe.wait_ge(*given("p_ready", n + 1))
                    pe.wait_ge(*emptied(f"pT{n}"))
                    for a in range(4):
                        last = tr(bank(f"pT{n}")[:, a * P:(a + 1) * P], pp[:, n, a * P:(a + 1) * P])
                    last.then_inc(*fills(f"pT{n}"))
                    if n == 5:
                        moe1(6)
                pe.wait_ge(*emptied("pv"))
                pe.wait_ge(*read_out("pT10"))
                pe.wait_ge(*read_out("pT11"))
                for hd in range(NHF):
                    grp, r = hd // GR, hd % GR
                    last = mm(bank("pv")[:, hd * V1:(hd + 1) * V1], pT[:, grp, r * P:(r + 1) * P], v9[:, 0, grp, :], start=True, stop=True)
                for hd in range(NHF):
                    grp, r = hd // GR, hd % GR
                    n, a = 4 + 2 * grp + r // 2, r % 2
                    for kt in range(2):
                        last = mm(bank("pv")[:, (NHF + hd) * V1:(NHF + hd + 1) * V1], pT[:, n, (2 * a + kt) * P:(2 * a + kt + 1) * P],
                                  v9[:, kt, grp, :], start=(kt == 0), stop=(kt == 1))
                last.then_inc(*fills("pv"))
                moe1(7)
                pe.wait_ge(*read_out("pv"))
                pe.wait_ge(*emptied("aT"))
                for t in range(NT):
                    last = tr(bank("aT")[:, t * P:(t + 1) * P], ao[:, t, :])
                last.then_inc(*fills("aT"))
                pe.wait_ge(*read_out("aT"))
                pe.wait_ge(*emptied("wo"))
                for t in range(NT):
                    last = mm(bank("wo")[:, t * P:(t + 1) * P], aT[:, t * P:(t + 1) * P], woT[:, :], start=True, stop=True)
                last.then_inc(*fills("wo"))
                z_inputs()
                moe1(8)
                pe.wait_ge(*given("h2_ready"))
                pe.wait_ge(*emptied("hT"))
                for t in range(NT):
                    last = tr(bank("hT")[:, t * P:(t + 1) * P], sq[:, t, :])
                last.then_inc(*fills("hT"))
                z_products(0)
                pe.wait_ge(*read_out("hT"))
                pe.wait_ge(*emptied("gate"))
                for t in range(NT):
                    last = mm(bank("gate")[:, t * E:(t + 1) * E], hT[:, t * P:(t + 1) * P], gateT[:, :], start=True, stop=True)
                last.then_inc(*fills("gate"))
                z_products(1)

            def attention1():
                if "A" not in now["stages"]:
                    z_inputs()
                    z_products(0)
                    z_products(1)
                moe0(0)
                moe0(1)
                moe0(2)
                zT = xT[:, 1, :]
                for name, off in (("lq", 0), ("lk", INNER)):
                    for j in range(4):
                        pe.wait_ge(*emptied(f"{name}{j}"))
                        for a in range(2):
                            pr = 2 * j + a
                            last = mm(bank(f"{name}{j}")[:, a * N:(a + 1) * N], lqkvg[:, off + pr * P:off + (pr + 1) * P], zT, start=True, stop=True)
                        last.then_inc(*fills(f"{name}{j}"))
                pe.wait_ge(*read_out("lq3"))
                for j in range(4):
                    pe.wait_ge(*emptied(f"nq{j}"))
                    for a in range(2):
                        last = mm(bank(f"nq{j}")[:, a * N:(a + 1) * N], samehead[:, :], sqT[:, 2 * j + a, :], start=True, stop=True)
                    last.then_inc(*fills(f"nq{j}"))
                for t in range(NT):
                    for c in range(2):
                        pe.wait_ge(*emptied(f"tk{t}{c}"))
                        mm(bank(f"tk{t}{c}"), zT[:, t * P:(t + 1) * P], lqkvg[:, INNER + c * 512:INNER + (c + 1) * 512],
                           start=True, stop=True).then_inc(*fills(f"tk{t}{c}"))
                moe0(3)
                for t in range(NT):
                    pe.wait_ge(*given("at3_ready", t + 1))
                    for c in range(2):
                        pe.wait_ge(*emptied(f"d{t}{c}"))
                        mm(bank(f"d{t}{c}"), identb[:, :], dmask[:, :, :], start=True, stop=False)
                        mm(bank(f"d{t}{c}"), strict[:, :], at3[:, t, c::2, :], start=False, stop=True).then_inc(*fills(f"d{t}{c}"))
                for t in range(NT):
                    for c in range(2):
                        pe.wait_ge(*emptied(f"te{t}{c}"))
                        mm(bank(f"te{t}{c}"), strict[:, :], a_tok[:, t, c * 512:(c + 1) * 512], start=True, stop=True).then_inc(*fills(f"te{t}{c}"))
                for t in range(NT):
                    for c in range(2):
                        pe.wait_ge(*emptied(f"tv{t}{c}"))
                        mm(bank(f"tv{t}{c}"), zT[:, t * P:(t + 1) * P], lqkvg[:, 2 * INNER + c * 512:2 * INNER + (c + 1) * 512], start=True, stop=True).then_inc(*fills(f"tv{t}{c}"))
                moe0(4)
                pe.wait_ge(*read_out("lk3"))
                pe.wait_ge(*given("qn_ready"))
                for t in range(NT):
                    for c in range(2):
                        pe.wait_ge(*emptied(f"s{t}{c}"))
                        mm(bank(f"s{t}{c}"), identb[:, :], zerob[:, :], start=True, stop=False)
                        for ch in range(2):
                            for pr in range(NP):
                                cc = t * P + ch * CH
                                last = mm(bank(f"s{t}{c}")[ch * CH:(ch + 1) * CH, pr * CH:(pr + 1) * CH],
                                          kT[c * DH:(c + 1) * DH, pr, cc:cc + CH], qt[c * DH:(c + 1) * DH, pr, cc:cc + CH],
                                          start=False, stop=(pr == NP - 1))
                        last.then_inc(*fills(f"s{t}{c}"))
                for j in range(4):
                    pe.wait_ge(*emptied(f"la{j}"))
                    for a in range(2):
                        for t in range(NT):
                            last = mm(bank(f"la{j}")[:, a * N + t * P:a * N + (t + 1) * P], a_tok[:, t, (2 * j + a) * P:(2 * j + a + 1) * P], tri[:, :], start=True, stop=True)
                    last.then_inc(*fills(f"la{j}"))
                moe0(5)
                pe.wait_ge(*given("kd_ready"))
                pe.wait_ge(*read_out("tv11"))
                for n in range(NC - 1):
                    t, r0 = n // 2, (n % 2) * CH
                    for hh in range(2):
                        pe.wait_ge(*emptied(f"st{n}{hh}"))
                        for a in range(4):
                            pr = 4 * hh + a
                            last = mm(bank(f"st{n}{hh}")[:, a * P:(a + 1) * P], kd[r0:r0 + CH, t, pr * P:(pr + 1) * P],
                                      v_tok[r0:r0 + CH, t, 2 * pr:2 * pr + 2, 0:DH], start=True, stop=True)
                        last.then_inc(*fills(f"st{n}{hh}"))
                pe.wait_ge(*emptied("gate1"))
                for t in range(NT):
                    last = mm(bank("gate1")[:, t * E:(t + 1) * E], x1T[:, t * P:(t + 1) * P], mg[:, :], start=True, stop=True)
                last.then_inc(*fills("gate1"))
                moe0(6)
                pe.wait_ge(*read_out("s11"))
                pe.wait_ge(*given("qd_ready"))
                pe.wait_ge(*read_out("st21"))
                for j in range(4):
                    pe.wait_ge(*emptied(f"o{j}"))
                    mm(bank(f"o{j}"), identb[:, :], zerob[:, :], start=True, stop=False)
                    for a in range(2):
                        for t in range(NT):
                            for c in range(2):
                                pr = 2 * j + a
                                mm(bank(f"o{j}")[c * DH:(c + 1) * DH, a * N + t * P:a * N + (t + 1) * P],
                                   v_tok[:, t, 2 * pr + c, 0:DH], pbd[:, t, c, pr, :], start=False, stop=False)
                    for a in range(2):
                        for n in range(1, NC):
                            pr = 2 * j + a
                            last = mm(bank(f"o{j}")[:, a * N + n * CH:a * N + (n + 1) * CH], st[:, n - 1, pr, :],
                                      el[:, pr, n * CH:(n + 1) * CH], start=False, stop=(a == 1 and n == NC - 1))
                    last.then_inc(*fills(f"o{j}"))
                pe.wait_ge(*read_out("o3"))
                pe.wait_ge(*emptied("wo1"))
                for t in range(NT):
                    for pr in range(NP):
                        last = mm(bank("wo1")[:, t * P:(t + 1) * P], oT1[:, pr, t * P:(t + 1) * P], lwo[:, pr, :], start=(pr == 0), stop=(pr == NP - 1))
                last.then_inc(*fills("wo1"))
                pe.wait_ge(*given("oh_ready"))
                pe.wait_ge(*emptied("ohT"))
                for t in range(NT):
                    last = tr(bank("ohT")[0:E, t * P:(t + 1) * P], small[:, 256 + t * E:256 + (t + 1) * E])
                last.then_inc(*fills("ohT"))
                moe0(7)
                pe.wait_ge(*given("z2_ready"))
                pe.wait_ge(*emptied("z2T"))
                for t in range(NT):
                    last = tr(bank("z2T")[:, t * P:(t + 1) * P], xr1[:, t, :])
                last.then_inc(*fills("z2T"))
                pe.wait_ge(*read_out("ohT"))
                pe.wait_ge(*emptied("b2y"))
                for t in range(NT):
                    last = mm(bank("b2y")[:, t * P:(t + 1) * P], ohT[:, t * P:(t + 1) * P], mb2[:, :], start=True, stop=True)
                last.then_inc(*fills("b2y"))
                pe.wait_ge(*read_out("z2T"))
                for j in range(2):
                    pe.wait_ge(*emptied(f"f{j}"))
                    for a in range(2):
                        last = mm(bank(f"f{j}")[:, a * N:(a + 1) * N], lw1[:, (2 * j + a) * P:(2 * j + a + 1) * P], xT[:, 1, :], start=True, stop=True)
                    last.then_inc(*fills(f"f{j}"))
                moe0(8)
                pe.wait_ge(*read_out("f1"))
                pe.wait_ge(*emptied("w2"))
                for t in range(NT):
                    for c in range(4):
                        last = mm(bank("w2")[:, t * P:(t + 1) * P], g1[:, c, t * P:(t + 1) * P], lw2[:, c, :], start=(c == 0), stop=(c == 3))
                last.then_inc(*fills("w2"))

            def body():
                if "A" in now["stages"]:
                    attention0()
                else:
                    for e in range(E + 1):
                        moe1(e)
                if now["n"] == 0:
                    pe.wait_ge(sem("weights"), 16 * NLOAD[0])
                    pe.wait_ge(sem("bg3_ready"), 48)
                if "C" in now["stages"]:
                    attention1()
                else:
                    for e in range(E + 1):
                        moe0(e)

            for n, (stages, times) in enumerate(SEGMENTS):
                if times == 1:
                    segment(n, 0)
                    body()
                else:
                    with pe.Fori(0, times) as i:
                        segment(n, i)
                        body()

        @blk.scalar
        def _(act):
            af = nc.scalar.activation

            def rstd(name, src, dst, scale, bias):
                act.wait_ge(*given(f"{name}_stat"))
                af(dst, src, ACT.Ln, scale=scale, bias=bias).then_inc(*signals("act_chain"))
                act.wait_ge(*chained("act_chain"))
                af(dst, dst, ACT.Exp, scale=-0.5).then_inc(*signals(f"{name}_rstd"))

            act.wait_ge(sem("first_weights"), 16 * NFIRST[0])
            act.preload_act_table_set("natural_log_exp_and_others")
            eps = cols[:, 42:43]

            def moe0(e):
                if "B" not in now["stages"]:
                    return
                if e < E:
                    act.wait_ge(*filled(f"a{e}"))
                    if e >= 2:
                        act.wait_ge(*filled(f"y{e - 2}"))
                    af(g0[:, e % 2, :, :], bank(f"a{e}").rearrange("p (c n) -> p c n", c=2), ACT.Silu).then_inc(*frees(f"a{e}"))
                else:
                    act.wait_ge(*read_out(f"y{E - 1}"))
                    af(sg[:, :, :], acc0[:, :, :], ACT.Silu).then_inc(*signals("sg_ready"))
                act.preload_act_table_set("natural_log_exp_and_others")

            def moe1(e):
                if "D" not in now["stages"]:
                    return
                if e < E:
                    if e:
                        act.wait_ge(*filled(f"yy{e - 1}"))
                    for j in range(2):
                        act.wait_ge(*filled(f"h{e}{j}"))
                        for a in range(2):
                            c = 2 * j + a
                            ins = af(r1[:, c, :], bank(f"h{e}{j}")[:, a * N:(a + 1) * N], ACT.Relu,
                                     bias=cols[:, 8 + 4 * e + c:9 + 4 * e + c])
                        ins.then_inc(*frees(f"h{e}{j}"))
                else:
                    act.wait_ge(*read_out(f"yy{E - 1}"))
                    af(sg[:, :, :], acc1[:, :, :], ACT.Silu).then_inc(*signals("sg1_ready"))
                    act.preload_act_table_set("natural_log_exp_and_others")

            def norms1():
                if "C" not in now["stages"]:
                    return
                rstd("ln1", small[:, 1:4:2], small[:, 4:6], 1.0, eps)
                rstd("ln1b", small[:, 1:4:2], small[:, 4:6], 1.0, eps)

            def z_products(t):
                if "C" not in now["stages"]:
                    return
                for c in range(2):
                    act.wait_ge(*filled(f"z{t}{c}"))
                    af(a_tok[:, t, c * 512:(c + 1) * 512], bank(f"z{t}{c}"), ACT.Exp, scale=-1.0).then_inc(*frees(f"z{t}{c}"))

            def attention0():
                moe1(0)
                rstd("ln0", small[:, 1:4:2], small[:, 4:6], 1.0, eps)
                rstd("rms0", small[:, 6:8], small[:, 8:10], 1.0 / D, eps)
                moe1(1)
                for j in range(4):
                    act.wait_ge(*filled(f"q{j}"))
                    af(e_q[:, 2 * j:2 * j + 2, :], bank(f"q{j}").rearrange("p (a n) -> p a n", a=2), ACT.Exp).then_inc(*signals("eq"))
                    af(qt[:, 2 * j:2 * j + 2, :], bank(f"q{j}").rearrange("p (a n) -> p a n", a=2), ACT.Relu).then_inc(*frees(f"q{j}"))
                for t in range(NT):
                    for c in range(2):
                        act.wait_ge(*filled(f"k{t}{c}"))
                        af(e_k[:, t, c * 512:(c + 1) * 512], bank(f"k{t}{c}"), ACT.Exp).then_inc(*signals("ek"))
                        af(k_tok[:, t, c * 512:(c + 1) * 512], bank(f"k{t}{c}"), ACT.Relu).then_inc(*frees(f"k{t}{c}"))
                moe1(2)
                moe1(3)
                moe1(4)
                for t in range(NT):
                    for c in range(2):
                        act.wait_ge(*filled(f"oT{t}{c}"))
                        src = bank(f"oT{t}{c}").rearrange("p (a n) -> p a n", a=4)
                        ins = af(oT[:, 4 * c:4 * c + 4, t * P:(t + 1) * P], src, ACT.Copy)
                        ins.then_inc(*frees(f"oT{t}{c}"))
                for n in range(12):
                    act.wait_ge(*read_out(f"sc{n}"))
                    af(pp[:, n, :], pp[:, n, :], ACT.Exp, scale=float(HD) ** -0.5).then_inc(*signals("p_ready"))
                    if n == 5:
                        moe1(5)
                norms1()
                for n in range(0, 12, 2):
                    act.wait_ge(*filled(f"pT{n}"))
                    af(pT[:, n, :], bank(f"pT{n}"), ACT.Copy).then_inc(*frees(f"pT{n}"))
                    if n == 4:
                        moe1(6)
                moe1(7)
                act.wait_ge(*filled("aT"))
                af(aT[:, :], bank("aT")[:, 0:N], ACT.Copy).then_inc(*frees("aT"))
                for t in range(NT):
                    act.wait_ge(*read_out("wo"))
                    af(sq[:, t, :], x2[:, t, :], ACT.Square, accum_out=small[:, 10 + t:11 + t]).then_inc(*signals("act_chain"))
                    act.wait_ge(*chained("act_chain"))
                af(small[:, 12:14], small[:, 10:12], ACT.Ln, scale=1.0 / D, bias=eps).then_inc(*signals("act_chain"))
                act.wait_ge(*chained("act_chain"))
                af(small[:, 12:14], small[:, 12:14], ACT.Exp, scale=-0.5).then_inc(*signals("rms2_rstd"))
                moe1(8)
                act.wait_ge(*filled("hT"))
                af(hT[:, :], bank("hT")[:, 0:N], ACT.Copy, scale=cols[:, 1:2]).then_inc(*frees("hT"))
                z_products(0)
                act.wait_ge(*given("lg_ready"))
                af(small[:, 32:48], small[:, 32:48], ACT.Exp).then_inc(*signals("eg_ready"))
                z_products(1)

            def attention1():
                if "A" not in now["stages"]:
                    norms1()
                if "A" not in now["stages"]:
                    z_products(0)
                    z_products(1)
                moe0(0)
                moe0(1)
                moe0(2)
                for j in range(4):
                    act.wait_ge(*filled(f"lq{j}"))
                    src = bank(f"lq{j}").rearrange("p (a n) -> p a n", a=2)
                    af(sqT[:, 2 * j:2 * j + 2, :], src, ACT.Square).then_inc(*signals("sq_done"))
                    af(qt[:, 2 * j:2 * j + 2, :], src, ACT.Copy).then_inc(*frees(f"lq{j}"))
                for j in range(4):
                    act.wait_ge(*filled(f"lk{j}"))
                    af(kT[:, 2 * j:2 * j + 2, :], bank(f"lk{j}").rearrange("p (a n) -> p a n", a=2), ACT.Copy).then_inc(*frees(f"lk{j}"))
                for t in range(NT):
                    act.wait_ge(*given("ez_clamped", t + 1))
                    af(a_tok[:, t, :], a_tok[:, t, :], ACT.Ln, bias=1.0).then_inc(*signals("a_ready"))
                for j in range(4):
                    sj = sqT[:, 2 * j:2 * j + 2, :]
                    act.wait_ge(*read_out(f"nq{j}"))
                    af(sj, sj, ACT.Ln, scale=1e6).then_inc(*signals("act_chain"))
                    act.wait_ge(*chained("act_chain"))
                    af(sj, sj, ACT.Exp, scale=-0.5).then_inc(*signals("rq_ready"))
                for t in range(NT):
                    for c in range(2):
                        act.wait_ge(*filled(f"tk{t}{c}"))
                        af(ks[:, t, c * 512:(c + 1) * 512], bank(f"tk{t}{c}"), ACT.Square).then_inc(*signals("ks"))
                moe0(3)
                act.wait_ge(*given("ssk_ready"))
                af(small[:, 96:128], small[:, 96:128], ACT.Ln, scale=1e6).then_inc(*signals("act_chain"))
                act.wait_ge(*chained("act_chain"))
                af(small[:, 96:128], small[:, 96:128], ACT.Exp, scale=-0.5).then_inc(*signals("rk_ready"))
                for t in range(NT):
                    for c in range(2):
                        act.wait_ge(*filled(f"d{t}{c}"))
                        for ch in range(2):
                            rows = slice(ch * CH, (ch + 1) * CH)
                            src = bank(f"d{t}{c}")[rows, :].rearrange("p (a n) -> p a n", a=NP)
                            ins = af(pbd[rows, t, c, :, ch * CH:(ch + 1) * CH], src, ACT.Exp, scale=-1.0 / DH)
                            if ch == 0:
                                ins.then_inc(*signals("dec_half"))
                        ins.then_inc(*frees(f"d{t}{c}"))
                for t in range(NT):
                    for c in range(2):
                        act.wait_ge(*filled(f"te{t}{c}"))
                        af(kd[:, t, c * 512:(c + 1) * 512], bank(f"te{t}{c}"), ACT.Exp, scale=-1.0).then_inc(*frees(f"te{t}{c}"))
                moe0(4)
                for j in range(4):
                    act.wait_ge(*filled(f"la{j}"))
                    af(el[:, 2 * j:2 * j + 2, :], bank(f"la{j}").rearrange("p (a n) -> p a n", a=2), ACT.Exp, scale=-1.0).then_inc(*frees(f"la{j}"))
                moe0(5)
                moe0(6)
                for j in range(4):
                    act.wait_ge(*filled(f"o{j}"))
                    af(oT1[:, 2 * j:2 * j + 2, :], bank(f"o{j}").rearrange("p (a n) -> p a n", a=2), ACT.Copy).then_inc(*frees(f"o{j}"))
                moe0(7)
                rstd("ln2", small[:, 1:4:2], small[:, 4:6], 1.0, eps)
                for j in range(2):
                    act.wait_ge(*filled(f"f{j}"))
                    for a in range(2):
                        c = 2 * j + a
                        ins = af(g1[:, c, :], bank(f"f{j}")[:, a * N:(a + 1) * N], ACT.Gelu, bias=cols[:, 4 + c:5 + c])
                        if a == 0:
                            ins.then_inc(*signals("gelu_half"))
                    ins.then_inc(*frees(f"f{j}"))
                act.preload_act_table_set("natural_log_exp_and_others")
                moe0(8)

            def body():
                if "A" in now["stages"]:
                    attention0()
                else:
                    for e in range(E + 1):
                        moe1(e)
                if now["n"] == 0:
                    act.wait_ge(sem("weights"), 16 * NLOAD[0])
                if "C" in now["stages"]:
                    attention1()
                else:
                    for e in range(E + 1):
                        moe0(e)
                checked()

            for n, (stages, times) in enumerate(SEGMENTS):
                if times == 1:
                    segment(n, 0)
                    body()
                else:
                    with act.Fori(0, times) as i:
                        segment(n, i)
                        body()

        @blk.vector
        def _(dve):
            v = nc.vector

            def carry():
                v.memset(small[:, 511:512], 0.0)

            def stats(src, name):
                for t in range(NT):
                    v.bn_stats(small[:, 16 + 6 * t:22 + 6 * t], src[:, t, :]).then_inc(*signals("dve_chain"))
                    dve.wait_ge(*chained("dve_chain"))
                    if t == NT - 1:
                        carry()
                for t in range(NT):
                    ins = v.bn_aggr(small[:, 2 * t:2 * t + 2], small[:, 16 + 6 * t:22 + 6 * t])
                ins.then_inc(*signals(f"{name}_stat"))
                dve.wait_ge(*given(f"{name}_stat"))

            def normed(dst, src, name, ready=None):
                stats(src, name)
                dve.wait_ge(*given(f"{name}_rstd"))
                for t in range(NT):
                    ins = v.tensor_scalar(dst[:, t, :], src[:, t, :], small[:, 2 * t:2 * t + 1], small[:, 4 + t:5 + t], ALU.subtract, ALU.mult)
                    if t == NT - 1 and ready:
                        ins.then_inc(*signals(ready))
                    else:
                        ins.then_inc(*signals("dve_chain"))
                        dve.wait_ge(*chained("dve_chain"))

            def tok(ap):
                return ap.rearrange("p (t d) -> p t d", t=NT)

            dve.wait_ge(sem("bg_loaded"), 16)
            ch0 = [0]

            def step(ins):
                ch0[0] += 1
                ins.then_inc(sem("setup_chain"), 1)
                dve.wait_ge(sem("setup_chain"), ch0[0])

            bg_whole, rest = big[0:1, 0:INNER], big[0:1, INNER:2 * INNER]
            step(v.tensor_copy(kd_b16(0), bg_whole))
            step(v.tensor_tensor(rest, bg_whole, kd_b16(0), ALU.subtract))
            step(v.tensor_copy(kd_b16(1), rest))
            step(v.tensor_tensor(rest, rest, kd_b16(1), ALU.subtract))
            v.tensor_copy(kd_b16(2), rest).then_inc(sem("bg_split"), 1)
            
            dve.wait_ge(sem("bg3_ready"), 48)
            dve.wait_ge(sem("first_weights"), 16 * NFIRST[0])
            dve.wait_ge(sem("zeros"), 5)
            dve.sem_inc(sem("x_free"), 1)
            dve.sem_inc(sem("ew0_free"), 1)
            dve.sem_inc(sem("ew1_free"), 1)
            lg = small[:, 160:176].rearrange("p (t e) -> p t e", t=NT)
            m8 = small[:, 176:192].rearrange("p (t e) -> p t e", t=NT)
            idf = small[:, 192:208].rearrange("p (t e) -> p t e", t=NT)
            io = iota8[:, :].rearrange("p (o e) -> p o e", o=1).to_broadcast([P, NT, E])
            gw = small[:, 240:256].rearrange("p (t e) -> p t e", t=NT)
            oh1 = small[:, 256:272].rearrange("p (t e) -> p t e", t=NT)

            def moe0(e):
                if "B" not in now["stages"]:
                    return
                if e < E:
                    dve.wait_ge(*filled(f"b{e}"))
                    dve.wait_ge(*read_out(f"a{e}"))
                    gs = g0[:, e % 2, :, :]
                    v.tensor_tensor(gs, gs, bank(f"b{e}").rearrange("p (c n) -> p c n", c=2), ALU.mult).then_inc(*frees(f"b{e}"))
                if e:
                    dve.wait_ge(*filled(f"y{e - 1}"))
                    for t in range(NT):
                        ins = v.scalar_tensor_tensor(out=acc0[:, t, :], in0=bank(f"y{e - 1}")[:, t * P:(t + 1) * P], scalar=gw[:, t, e - 1:e],
                                                     in1=(x2 if e == 1 else acc0)[:, t, :], op0=ALU.mult, op1=ALU.add)
                        if t == 0:
                            ins.then_inc(*signals("dve_chain"))
                            dve.wait_ge(*chained("dve_chain"))
                    ins.then_inc(*frees(f"y{e - 1}"))
                    dve.wait_ge(*read_out(f"y{e - 1}"))
                if e == E:
                    dve.wait_ge(*given("sg_ready"))
                    v.tensor_tensor(x1[:, :, :], s0[:, :, :], sg[:, :, :], ALU.mult).then_inc(*signals("dve_chain"))
                    dve.wait_ge(*chained("dve_chain"))
                    v.tensor_tensor(x1[:, :, :], x1[:, :, :], x_keep[:, :, :], ALU.add).then_inc(*signals("dve_chain"))
                    dve.wait_ge(*chained("dve_chain"))

            def moe1(e):
                if "D" not in now["stages"]:
                    return
                if e:
                    dve.wait_ge(*filled(f"yy{e - 1}"))
                    for t in range(NT):
                        ins = v.scalar_tensor_tensor(out=acc1[:, t, :], in0=bank(f"yy{e - 1}")[:, t * P:(t + 1) * P], scalar=oh1[:, t, e - 1:e],
                                                     in1=acc1[:, t, :], op0=ALU.mult, op1=ALU.add)
                        if t == 0:
                            ins.then_inc(*signals(f"ew{(e - 1) % 2}_free"))
                    ins.then_inc(*frees(f"yy{e - 1}"))
                    dve.wait_ge(*read_out(f"yy{e - 1}"))
                if e == E:
                    dve.wait_ge(*given("sg1_ready"))
                    v.tensor_tensor(y2[:, :, :], y2[:, :, :], sg[:, :, :], ALU.mult).then_inc(*signals("dve_chain"))
                    dve.wait_ge(*chained("dve_chain"))
                    v.tensor_tensor(y2[:, :, :], y2[:, :, :], x1_keep[:, :, :], ALU.add).then_inc(*signals("out_ready"))

            def norms1():
                if "C" not in now["stages"]:
                    return
                normed(xn1, x1, "ln1")
                normed(xr1, xn1, "ln1b", "z1_ready")

            def z_inputs():
                if "C" not in now["stages"]:
                    return
                dve.wait_ge(*filled("zT"))
                v.tensor_copy(x1T[:, :], bank("zT")[:, 0:N]).then_inc(*signals("dve_chain"))
                dve.wait_ge(*chained("dve_chain"))
                v.tensor_scalar(xT[:, 1, :], bank("zT")[:, N:2 * N], cols[:, 2:3], cols[:, 40:41], ALU.mult, ALU.add).then_inc(*frees("zT"))

            def attention0():
                dve.wait_ge(*given("x_ready", 1, 16))
                normed(xn, x, "ln0", "xn_ready")
                dve.wait_ge(*given("xn_ready"))
                for t in range(NT):
                    v.scalar_tensor_tensor(out=xr[:, t, :], in0=xn[:, t, :], scalar=1.0, in1=xn[:, t, :], op0=ALU.mult, op1=ALU.mult).then_inc(*signals("dve_chain"))
                    dve.wait_ge(*chained("dve_chain"))
                v.tensor_reduce(small[:, 6:8], xr[:, :, :], AX.X, ALU.add).then_inc(*signals("rms0_stat"))
                dve.wait_ge(*filled("xT"))
                v.tensor_copy(xT[:, 0, :], bank("xT")[:, 0:N]).then_inc(*frees("xT"))
                dve.wait_ge(*given("rms0_rstd"))
                for t in range(NT):
                    ins = v.tensor_scalar(xr[:, t, :], xn[:, t, :], small[:, 8 + t:9 + t], None, ALU.mult)
                    if t == 0:
                        ins.then_inc(*signals("dve_chain"))
                        dve.wait_ge(*chained("dve_chain"))
                ins.then_inc(*signals("xr_ready"))
                moe1(0)
                moe1(1)
                v.tensor_copy(x_keep[:, :, :], x[:, :, :]).then_inc(*signals("x_free"))
                v.memset(v_tok[:, :, :, DH:V0], 1.0).then_inc(*signals("ones_ready"))
                for j in range(4):
                    dve.wait_ge(*read_out(f"q{j}"))
                    s = slice(2 * j, 2 * j + 2)
                    ins = v.scalar_tensor_tensor(out=qt[:, s, :], in0=e_q[:, s, :], scalar=1.0, in1=qt[:, s, :], op0=ALU.min, op1=ALU.add)
                    ins.then_inc(*signals("q0_ready" if j == 3 else "q0_part"))
                for t in range(NT):
                    for c in range(2):
                        dve.wait_ge(*read_out(f"k{t}{c}"))
                        s = slice(c * 512, (c + 1) * 512)
                        ins = v.scalar_tensor_tensor(out=k_tok[:, t, s], in0=e_k[:, t, s], scalar=1.0, in1=k_tok[:, t, s], op0=ALU.min, op1=ALU.add)
                        ins.then_inc(*signals("k0_ready" if 2 * t + c == 3 else "k0_part"))
                dve.wait_ge(*filled("rT"))
                v.tensor_scalar(xT[:, 1, :], bank("rT")[:, 0:N], cols[:, 0:1], None, ALU.mult).then_inc(*frees("rT"))
                for t in range(NT):
                    for c in range(2):
                        dve.wait_ge(*filled(f"v{t}{c}"))
                        v.tensor_copy(v_tok[:, t, 8 * c:8 * c + 8, 0:DH], bank(f"v{t}{c}").rearrange("p (h d) -> p h d", d=DH)).then_inc(*frees(f"v{t}{c}"))
                for j in range(2):
                    dve.wait_ge(*filled(f"rq{j}"))
                    cb = ropec[:, 0:1, :].to_broadcast([P, 2, N])
                    v.tensor_tensor(rp[:, 2 * j:2 * j + 2, :], bank(f"rq{j}").rearrange("p (a n) -> p a n", a=2), cb, ALU.mult).then_inc(*frees(f"rq{j}"))
                for j in range(2):
                    dve.wait_ge(*filled(f"rs{j}"))
                    sbc = ropec[:, 1:2, :].to_broadcast([P, 2, N])
                    v.tensor_tensor(rp[:, 4 + 2 * j:6 + 2 * j, :], bank(f"rs{j}").rearrange("p (a n) -> p a n", a=2), sbc, ALU.mult).then_inc(*frees(f"rs{j}"))
                dve.wait_ge(*filled("rk"))
                v.tensor_tensor(kr[:, :], bank("rk")[:, 0:N], ropec[:, 0, :], ALU.mult).then_inc(*signals("dve_chain"))
                dve.wait_ge(*chained("dve_chain"))
                v.tensor_tensor(krs, bank("rk")[:, N:2 * N], ropec[:, 1, :], ALU.mult).then_inc(*frees("rk"))
                dve.wait_ge(*filled("v9"))
                v.tensor_copy(v9[:, :, :, 0:HD], bank("v9")[:, 0:64].rearrange("p (t g d) -> p t g d", t=NT, g=NKV)).then_inc(*frees("v9"))
                dve.wait_ge(*read_out("rk"))
                v.tensor_tensor(kr[:, :], kr[:, :], krs, ALU.add).then_inc(*signals("dve_chain"))
                dve.wait_ge(*chained("dve_chain"))
                moe1(2)
                for j in range(4):
                    dve.wait_ge(*filled(f"kv{j}"))
                    for c in range(2):
                        rows, cs = slice(c * DH, (c + 1) * DH), slice(c * V0, (c + 1) * V0)
                        src = bank(f"kv{j}").rearrange("p (a n) -> p a n", a=2)[rows, :, cs]
                        ins = v.tensor_copy(kvb[rows, 2 * j:2 * j + 2, cs], src)
                        if c == 0:
                            ins.then_inc(*signals("dve_chain"))
                            dve.wait_ge(*chained("dve_chain"))
                    ins.then_inc(*frees(f"kv{j}"))
                moe1(3)
                for t in range(NT):
                    for j in range(4):
                        dve.wait_ge(*filled(f"num{t}{j}"))
                        nm = bank(f"num{t}{j}").rearrange("p (a n) -> p a n", a=2)[:, :, 0:2 * V0].rearrange("p a (h v) -> p a h v", v=V0)
                        dn = small[:, 304 + 4 * (j % 2):308 + 4 * (j % 2)]
                        den = dn.rearrange("p (a h) -> p a h", a=2)
                        v.tensor_scalar(den, nm[:, :, :, DH], 1e-6, None, ALU.add).then_inc(*signals("dve_chain"))
                        dve.wait_ge(*chained("dve_chain"))
                        v.reciprocal(dn, dn).then_inc(*signals("dve_chain"))
                        dve.wait_ge(*chained("dve_chain"))
                        ot = o_tok[:, t, 256 * j:256 * (j + 1)].rearrange("p (a h v) -> p a h v", a=2, v=DH)
                        rb = dn.rearrange("p (a h o) -> p a h o", a=2, o=1).to_broadcast([P, 2, 2, DH])
                        v.tensor_tensor(ot, nm[:, :, :, 0:DH], rb, ALU.mult).then_inc(*frees(f"num{t}{j}"))
                moe1(4)
                v.tensor_tensor(qt[:, 0:4, :], rp[:, 0:4, :], rp[:, 4:8, :], ALU.add).then_inc(*signals("rope_ready"))
                for n in range(12):
                    hs = 4 if n < 4 else 2
                    dve.wait_ge(*filled(f"sc{n}"))
                    sc = bank(f"sc{n}").rearrange("p (h k) -> p h k", h=hs)
                    nm = small[:, 320 + 4 * (n % 2):320 + 4 * (n % 2) + hs]
                    v.tensor_reduce(nm, sc, AX.X, ALU.max, negate=True).then_inc(*signals("dve_chain"))
                    dve.wait_ge(*chained("dve_chain"))
                    nb = nm.rearrange("p (h o) -> p h o", o=1).to_broadcast([P, hs, 512 // hs])
                    if n == 0:
                        dve.wait_ge(*given("rope_ready"))
                    v.tensor_tensor(pp[:, n, :].rearrange("p (h k) -> p h k", h=hs), sc, nb, ALU.add).then_inc(*frees(f"sc{n}"))
                    if n == 1:
                        dve.wait_ge(*filled("s0"))
                        v.tensor_tensor(s0[:, :, :], tok(bank("s0")[:, 0:N]), boutb[:, :].rearrange("p (o d) -> p o d", o=1).to_broadcast([P, NT, D]), ALU.add).then_inc(*frees("s0"))
                    if n == 5:
                        moe1(5)
                norms1()
                for n in range(1, 12, 2):
                    dve.wait_ge(*filled(f"pT{n}"))
                    v.tensor_copy(pT[:, n, :], bank(f"pT{n}")).then_inc(*frees(f"pT{n}"))
                    if n == 5:
                        moe1(6)
                dve.wait_ge(*filled("pv"))
                pv = bank("pv")[:, 0:2 * NHF * V1].rearrange("p (h v) -> p h v", v=V1)
                v.reciprocal(small[:, 128:160].rearrange("p (h o) -> p h o", o=1), pv[:, :, HD:V1]).then_inc(*signals("dve_chain"))
                dve.wait_ge(*chained("dve_chain"))
                v.tensor_tensor(ao[:, :, :].rearrange("p t (h d) -> p (t h) d", d=HD), pv[:, :, 0:HD],
                                     small[:, 128:160].rearrange("p (h o) -> p h o", o=1).to_broadcast([P, 2 * NHF, HD]), ALU.mult).then_inc(*frees("pv"))
                moe1(7)
                dve.wait_ge(*filled("wo"))
                v.tensor_tensor(x2[:, :, :], xn[:, :, :], tok(bank("wo")[:, 0:N]), ALU.add).then_inc(*frees("wo"))
                z_inputs()
                dve.wait_ge(*given("rms2_rstd"))
                for t in range(NT):
                    ins = v.tensor_scalar(sq[:, t, :], x2[:, t, :], small[:, 12 + t:13 + t], None, ALU.mult)
                    if t == 0:
                        ins.then_inc(*signals("dve_chain"))
                        dve.wait_ge(*chained("dve_chain"))
                ins.then_inc(*signals("h2_ready"))
                moe1(8)
                dve.wait_ge(*filled("gate"))
                v.tensor_copy(small[:, 160:176], bank("gate")[:, 0:NT * E]).then_inc(*frees("gate"))
                dve.wait_ge(*read_out("gate"))
                carry()
                for t in range(NT):
                    ins = v.max(m8[:, t, :], lg[:, t, :])
                ins.then_inc(*signals("dve_chain"))
                dve.wait_ge(*chained("dve_chain"))
                carry()
                for t in range(NT):
                    ins = v.max_index(idx8[:, t, :], m8[:, t, :], lg[:, t, :])
                ins.then_inc(*signals("dve_chain"))
                dve.wait_ge(*chained("dve_chain"))
                v.tensor_tensor(small[:, 32:48].rearrange("p (t e) -> p t e", t=NT), lg, m8[:, :, 0:1].to_broadcast([P, NT, E]), ALU.subtract).then_inc(*signals("lg_ready"))
                v.tensor_copy(idf, idx8[:, :, :]).then_inc(*signals("dve_chain"))
                dve.wait_ge(*chained("dve_chain"))
                oh = small[:, 208:240].rearrange("p (k t e) -> p k t e", k=2, t=NT)
                for k in range(2):
                    v.tensor_tensor(oh[:, k, :, :], io, idf[:, :, k:k + 1].to_broadcast([P, NT, E]), ALU.is_equal).then_inc(*signals("dve_chain"))
                    dve.wait_ge(*chained("dve_chain"))
                v.tensor_tensor(oh[:, 0, :, :], oh[:, 0, :, :], oh[:, 1, :, :], ALU.add).then_inc(*signals("dve_chain"))
                dve.wait_ge(*chained("dve_chain"))
                dve.wait_ge(*given("eg_ready"))
                v.tensor_tensor(gw, small[:, 32:48].rearrange("p (t e) -> p t e", t=NT), oh[:, 0, :, :], ALU.mult).then_inc(*signals("dve_chain"))
                dve.wait_ge(*chained("dve_chain"))
                v.tensor_reduce(small[:, 56:58], gw, AX.X, ALU.add).then_inc(*signals("dve_chain"))
                dve.wait_ge(*chained("dve_chain"))
                v.reciprocal(small[:, 56:58], small[:, 56:58]).then_inc(*signals("dve_chain"))
                dve.wait_ge(*chained("dve_chain"))
                v.tensor_tensor(gw, gw, small[:, 56:58].rearrange("p (t o) -> p t o", o=1).to_broadcast([P, NT, E]), ALU.mult).then_inc(*signals("dve_chain"))
                dve.wait_ge(*chained("dve_chain"))

            def attention1():
                moe0(0)
                moe0(1)
                if "D" in now["stages"]:
                    dve.wait_ge(*given("out_ready"))
                v.tensor_copy(x1_keep[:, :, :], x1[:, :, :]).then_inc(*signals("dve_chain"))
                dve.wait_ge(*chained("dve_chain"))
                if "A" not in now["stages"]:
                    norms1()
                    z_inputs()
                moe0(2)
                for t in range(NT):
                    dve.wait_ge(*read_out(f"z{t}1"))
                    v.tensor_scalar(a_tok[:, t, :], a_tok[:, t, :], 999999.0, None, ALU.min).then_inc(*signals("ez_clamped"))
                for j in range(4):
                    dve.wait_ge(*filled(f"nq{j}"))
                    v.tensor_scalar(sqT[:, 2 * j:2 * j + 2, :], bank(f"nq{j}").rearrange("p (a n) -> p a n", a=2), 1e-24, None, ALU.max).then_inc(*frees(f"nq{j}"))
                for t in range(NT):
                    dve.wait_ge(*given("a_ready", t + 1))
                    am = small[:, 272 + t * H:272 + (t + 1) * H]
                    v.tensor_reduce(am, a_tok[:, t, :].rearrange("p (h d) -> p h d", d=DH), AX.X, ALU.add).then_inc(*signals("dve_chain"))
                    dve.wait_ge(*chained("dve_chain"))
                    v.tensor_tensor(at3[:, t, :, :], am.rearrange("p (h o) -> p h o", o=1).to_broadcast([P, H, CH]),
                                         tri64[:, :].rearrange("p (o c) -> p o c", o=1).to_broadcast([P, H, CH]), ALU.mult).then_inc(*signals("at3_ready"))
                for t in range(NT):
                    for c in range(2):
                        dve.wait_ge(*filled(f"tk{t}{c}"))
                        dve.wait_ge(*given("ks", 2 * t + c + 1))
                        v.tensor_copy(k_tok[:, t, c * 512:(c + 1) * 512], bank(f"tk{t}{c}")).then_inc(*frees(f"tk{t}{c}"))
                v.tensor_reduce(small[:, 96:128], ks_row.rearrange("p (h d) -> p h d", d=DH), AX.X, ALU.add).then_inc(*signals("dve_chain"))
                dve.wait_ge(*chained("dve_chain"))
                v.tensor_scalar(small[:, 96:128], small[:, 96:128], 1e-24, None, ALU.max).then_inc(*signals("ssk_ready"))
                moe0(3)
                for j in range(4):
                    dve.wait_ge(*given("rq_ready", j + 1))
                    s = slice(2 * j, 2 * j + 2)
                    ins = v.scalar_tensor_tensor(out=qt[:, s, :], in0=sqT[:, s, :], scalar=1e3, in1=qt[:, s, :], op0=ALU.mult, op1=ALU.mult)
                    ins.then_inc(*signals("qn_ready" if j == 3 else "qn_part"))
                dve.wait_ge(*given("rk_ready"))
                for t in range(NT):
                    for c in range(2):
                        dve.wait_ge(*filled(f"tv{t}{c}"))
                        rb = small[:, 96 + t * H + 8 * c:96 + t * H + 8 * c + 8].rearrange("p (h o) -> p h o", o=1).to_broadcast([P, 8, DH])
                        v.scalar_tensor_tensor(out=v_tok[:, t, 8 * c:8 * c + 8, 0:DH], in0=bank(f"tv{t}{c}").rearrange("p (h d) -> p h d", d=DH),
                                                    scalar=1e3, in1=rb, op0=ALU.mult, op1=ALU.mult).then_inc(*frees(f"tv{t}{c}"))
                for t in range(NT):
                    for c in range(2):
                        dve.wait_ge(*read_out(f"te{t}{c}"))
                        s = slice(c * 512, (c + 1) * 512)
                        ins = v.tensor_tensor(kd[:, t, s], kd[:, t, s], k_tok[:, t, s], ALU.mult)
                        ins.then_inc(*signals("kd_ready" if 2 * t + c == 3 else "kd_part"))
                moe0(4)
                for t in range(NT):
                    for c in range(2):
                        dve.wait_ge(*filled(f"s{t}{c}"))
                        dve.wait_ge(*read_out(f"d{t}{c}"))
                        for ch in range(2):
                            rows = slice(ch * CH, (ch + 1) * CH)
                            w = pbd[rows, t, c, :, ch * CH:(ch + 1) * CH]
                            ins = v.tensor_tensor(w, bank(f"s{t}{c}")[rows, :].rearrange("p (a n) -> p a n", a=NP), w, ALU.mult)
                            if ch == 0:
                                ins.then_inc(*signals("dve_chain"))
                                dve.wait_ge(*chained("dve_chain"))
                        ins.then_inc(*frees(f"s{t}{c}"))
                dve.wait_ge(*read_out("la3"))
                v.tensor_copy(cd[:, :, :], el[:, :, CH - 1::CH]).then_inc(*signals("cd_ready"))
                dve.wait_ge(*given("cd_ready"))
                moe0(5)
                for n in range(NC - 1):
                    for hh in range(2):
                        dve.wait_ge(*filled(f"st{n}{hh}"))
                        ps = slice(4 * hh, 4 * hh + 4)
                        for c in range(2):
                            rows = slice(c * DH, (c + 1) * DH)
                            src = bank(f"st{n}{hh}").rearrange("p (a n) -> p a n", a=4)[rows, :, rows]
                            dst = st[rows, n, ps, rows]
                            if n == 0:
                                ins = v.tensor_copy(dst, src)
                            else:
                                v.tensor_tensor(dst, st[rows, n - 1, ps, rows], cd[rows, ps, n:n + 1].to_broadcast([DH, 4, DH]), ALU.mult).then_inc(*signals("dve_chain"))
                                dve.wait_ge(*chained("dve_chain"))
                                ins = v.tensor_tensor(dst, dst, src, ALU.add)
                            if c == 0:
                                ins.then_inc(*signals("dve_chain"))
                                dve.wait_ge(*chained("dve_chain"))
                        ins.then_inc(*frees(f"st{n}{hh}"))
                        dve.wait_ge(*read_out(f"st{n}{hh}"))
                dve.wait_ge(*filled("gate1"))
                v.tensor_tensor(lg, bank("gate1")[:, 0:NT * E].rearrange("p (t e) -> p t e", t=NT),
                                     bgb[:, :].rearrange("p (o e) -> p o e", o=1).to_broadcast([P, NT, E]), ALU.add).then_inc(*frees("gate1"))
                dve.wait_ge(*read_out("gate1"))
                carry()
                for t in range(NT):
                    ins = v.max(m8[:, t, :], lg[:, t, :])
                ins.then_inc(*signals("dve_chain"))
                dve.wait_ge(*chained("dve_chain"))
                carry()
                for t in range(NT):
                    ins = v.max_index(idx8[:, t, :], m8[:, t, :], lg[:, t, :])
                ins.then_inc(*signals("dve_chain"))
                dve.wait_ge(*chained("dve_chain"))
                v.tensor_copy(idf, idx8[:, :, :]).then_inc(*signals("dve_chain"))
                dve.wait_ge(*chained("dve_chain"))
                v.tensor_tensor(oh1, io, idf[:, :, 0:1].to_broadcast([P, NT, E]), ALU.is_equal).then_inc(*signals("oh_ready"))
                moe0(6)
                dve.wait_ge(sem("stored"), 16 * row("C") + 16)
                dve.wait_ge(*filled("wo1"))
                v.tensor_tensor(y2[:, :, :], xn1[:, :, :], tok(bank("wo1")[:, 0:N]), ALU.add).then_inc(*frees("wo1"))
                dve.wait_ge(*read_out("wo1"))
                dve.wait_ge(*filled("ohT"))
                v.tensor_copy(ohT[:, :], bank("ohT")[0:E, 0:N]).then_inc(*frees("ohT"))
                normed(xr1, y2, "ln2", "z2_ready")
                moe0(7)
                dve.wait_ge(*filled("z2T"))
                v.tensor_scalar(xT[:, 1, :], bank("z2T")[:, 0:N], cols[:, 3:4], cols[:, 41:42], ALU.mult, ALU.add).then_inc(*frees("z2T"))
                dve.wait_ge(*filled("b2y"))
                v.tensor_copy(acc1[:, :, :], tok(bank("b2y")[:, 0:N])).then_inc(*frees("b2y"))
                dve.wait_ge(*read_out("b2y"))
                b2bb = b2b[:, :].rearrange("p (o d) -> p o d", o=1).to_broadcast([P, NT, D])
                v.tensor_tensor(y2[:, :, :], y2[:, :, :], b2bb, ALU.add).then_inc(*signals("dve_chain"))
                dve.wait_ge(*chained("dve_chain"))
                moe0(8)
                dve.wait_ge(*filled("w2"))
                v.tensor_tensor(y2[:, :, :], y2[:, :, :], tok(bank("w2")[:, 0:N]), ALU.add).then_inc(*frees("w2"))

            def body():
                if "A" in now["stages"]:
                    attention0()
                else:
                    for e in range(E + 1):
                        moe1(e)
                if now["n"] == 0:
                    dve.wait_ge(sem("weights"), 16 * NLOAD[0])
                if "C" in now["stages"]:
                    attention1()
                else:
                    for e in range(E + 1):
                        moe0(e)
                checked()

            for n, (stages, times) in enumerate(SEGMENTS):
                if times == 1:
                    segment(n, 0)
                    body()
                else:
                    with dve.Fori(0, times) as i:
                        segment(n, i)
                        body()

SHAPES = {}

def kernel(**inputs):
    import concourse.bacc as bacc
    from concourse.bass_utils import run_bass_kernel_spmd

    I = {k: np.asarray(v) for k, v in inputs.items()}
    ca = np.ascontiguousarray
    bf = mybir.dt.np(mybir.dt.bfloat16)

    def split_k(w):
        return ca(w.reshape(-1, P, w.shape[-1]).transpose(1, 0, 2))

    wq = I["L0_ffn_wqkv"]
    q = wq[:NHF * HD].reshape(NKV, GR, HD, D)
    k = wq[NHF * HD:(NHF + NKV) * HD].reshape(NKV, 1, HD, D)
    turn = np.r_[HD // 2:HD, 0:HD // 2]
    wrope = np.zeros((D, 10, P), np.float32)
    for g in range(NKV):
        for a in range(GR):
            wrope[:, a, 32 * g:32 * g + HD] = q[g, a].T
            wrope[:, 4 + a, 32 * g:32 * g + HD] = q[g, a][turn].T
        wrope[:, 8, 32 * g:32 * g + HD] = k[g, 0].T
        wrope[:, 9, 32 * g:32 * g + HD] = k[g, 0][turn].T
    inv = (1.0 / np.float32(10000.0) ** (np.arange(0, HD, 2, dtype=np.float32) / np.float32(HD))).astype(np.float32)
    ang = np.arange(N, dtype=np.float32)[:, None] * inv[None, :]
    ang = np.concatenate([ang, ang], -1).T
    ropec = np.zeros((P, 2, N), np.float32)
    for g in range(NKV):
        ropec[32 * g:32 * g + HD, 0] = np.cos(ang)
        ropec[32 * g:32 * g + HD, 1] = np.sin(ang) * np.r_[-np.ones(HD // 2), np.ones(HD // 2)].astype(np.float32)[:, None]
    ew = np.concatenate([I["L1_ffn_W1"], I["L1_ffn_W2"].reshape(E, 4, P, D).transpose(0, 2, 1, 3).reshape(E, P, 4 * D)], -1)
    cols = np.concatenate([
        I["L0_ffn_ln1_w"][:, None], I["L0_ffn_ln2_w"][:, None], I["L1_attn_ln1_w"][:, None], I["L1_attn_ln2_w"][:, None],
        I["L1_attn_b1"].reshape(4, P).T, I["L1_ffn_b1"].reshape(E * 4, P).T,
        I["L1_attn_ln1_b"][:, None], I["L1_attn_ln2_b"][:, None], np.full((P, 1), 1e-5, np.float32)], 1)
    r = np.arange(P)
    same = (r[:, None] // CH) == (r[None, :] // CH)
    keep = r[None, :] <= r[:, None]
    cmask = np.zeros((P, 2, 512), np.float32)
    cmask[:, 0] = np.tile(np.where(keep, 0, NEG), (1, 4))
    cmask[:, 1] = np.tile(np.concatenate([np.zeros((P, P)), np.where(keep, 0, NEG)], 1), (1, 2))
    dmask = np.tile(np.where(np.arange(CH)[None, :] < (r % CH)[:, None], -NEG, 0)[:, None, :], (1, 8, 1))
    arrays = {
        "x": I["L0_attn_x"],
        "wqkv0": I["L0_attn_Wqkv"], "wout0": split_k(I["L0_attn_Wout"]), "bout": I["L0_attn_bout"],
        "wrope": wrope, "ropec": ropec, "wv9": ca(wq[(NHF + NKV) * HD:].T), "woT": ca(I["L0_ffn_wo"].T), "gateT": ca(I["L0_ffn_gate_w"].T),
        "w13T": ca(I["L0_ffn_w13"].transpose(2, 0, 1)),
        "w2T": ca(I["L0_ffn_w2"].reshape(E, D, 2, P).transpose(3, 0, 2, 1)),
        "lqkvg": ca(np.concatenate([I["L1_attn_Wq"], I["L1_attn_Wk"], I["L1_attn_Wv"], I["L1_attn_Wg"]], 1)),
        "bg": I["L1_attn_bg"].reshape(1, -1), "lwo": split_k(I["L1_attn_Wo"]), "lw1": I["L1_attn_W1"], "lw2": split_k(I["L1_attn_W2"]),
        "mg": I["L1_ffn_Wg"], "mb2": I["L1_ffn_b2"], "cols": ca(cols), "bgm": I["L1_ffn_bg"], "b2": I["L1_attn_b2"], "ew": ca(ew),
        "identb": np.eye(P, dtype=np.float32).astype(bf), "cmask": cmask.astype(bf), "dmask": dmask.astype(bf), "ones3": np.ones((3, P), bf),
        "tri": (same & (r[:, None] <= r[None, :])).astype(np.float32), "strict": (same & (r[:, None] > r[None, :])).astype(np.float32),
        "tri64": ((r % CH)[:, None] <= np.arange(CH)[None, :]).astype(np.float32), "ident": np.eye(P, dtype=np.float32),
        "samehead": same.astype(np.float32),
        "iota8": np.tile(np.arange(E, dtype=np.float32), (P, 1)),
    }
    nc = bacc.Bacc("TRN2", target_bir_lowering=False, num_devices=1)
    feeds = {f"in_{n}": ca(a) for n, a in arrays.items()}
    A = {n: nc.dram_tensor(f"in_{n}", a.shape, mybir.dt.from_np(a.dtype), kind="ExternalInput").ap() for n, a in arrays.items()}
    out = nc.dram_tensor("out", (B, N, D), mybir.dt.float32, kind="ExternalOutput").ap()
    build(nc, A, out)
    r = run_bass_kernel_spmd(nc, [feeds], core_ids=[0])
    return r.results[0]["out"]
```
